# Optimizing a Trainium2 kernel written in Bass

```python
import numpy as np
import jax
import jax.numpy as jnp

def _softmax(x, axis=-1):
    return jax.nn.softmax(x, axis=axis)

def _gelu(x):
    return jax.nn.gelu(x, approximate=True)

def _silu(x):
    return jax.nn.silu(x)

def _sigmoid(x):
    return jax.nn.sigmoid(x)

def _layernorm(x, axis=-1, eps=1e-05):
    m = jnp.mean(x, axis=axis, keepdims=True)
    v = jnp.var(x, axis=axis, keepdims=True)
    return (x - m) / jnp.sqrt(v + eps)

def _scatter_add(tgt, idx, src, axis=0):
    return tgt.at[idx].add(src)

def _segment_sum(src, seg, n):
    return jax.ops.segment_sum(src, seg, n)
kernel_name = 'mk_decoder_preln_d1_seqx_r4_f9e012'

def setup_inputs(seed: int=0):
    np.random.seed(seed)
    _w = jnp.asarray

    def _rec_inputs():
        import jax
        import jax.numpy as jnp
        _rk = jax.random.key(seed)
        x = -0.0002928 + 1 * jax.random.normal(jax.random.fold_in(_rk, 1), (1, 2048, 256), jnp.float32)
        _lenS = 2048 - jax.random.randint(jax.random.fold_in(_rk, 7), (1,), 0, max(1, 2048 // 4) + 1, jnp.int32)
        _lenS2 = 1601 - jax.random.randint(jax.random.fold_in(_rk, 8), (1,), 0, max(1, 1601 // 4) + 1, jnp.int32)
        _ctx_1024P = jax.random.normal(jax.random.fold_in(_rk, 11), (1, 16, 256), jnp.float32)
        _ctx_1024c = jax.random.dirichlet(jax.random.fold_in(_rk, 511), 0.3 * jnp.ones((16,), jnp.float32), (1, 1601))
        _ctx_1024t = jnp.einsum('bsk,bkd->bsd', _ctx_1024c, _ctx_1024P)
        _ctx_1024t = _ctx_1024t * jax.lax.rsqrt(jnp.mean(jnp.square(_ctx_1024t)) + 1e-12) * 0.953939
        ctx_1024 = -1.39393e-06 + 0.999914 * (_ctx_1024t + 0.3 * jax.random.normal(jax.random.fold_in(_rk, 611), (1, 1601, 256), jnp.float32))
        _validS = jnp.arange(2048)[None, :] < _lenS[:, None]
        _validS2 = jnp.arange(1601)[None, :] < _lenS2[:, None]
        _causal = jnp.tril(jnp.ones((2048, 2048), dtype=bool))
        mask_BxSxS2_bf1 = jnp.ones((1, 2048, 1601), dtype=bool)
        return (x, ctx_1024, mask_BxSxS2_bf1)
    x, ctx_1024, mask_BxSxS2_bf1 = _rec_inputs()

    def _L0_attn_setup():
        import jax, jax.numpy as jnp
        import numpy as np
        HIDDEN = 256
        B, S = (8, 512)
        key = jax.random.key(seed)
        k1, k2, k3, k4 = jax.random.split(key, 4)
        gain = 1.2
        bound = gain * np.sqrt(6.0 / (HIDDEN + HIDDEN))
        return {'hidden_states': jax.random.normal(k1, (B, S, HIDDEN), dtype=jnp.float32), 'Wq': jax.random.uniform(k2, (HIDDEN, HIDDEN), jnp.float32, -bound, bound), 'bq': jnp.zeros((HIDDEN,), jnp.float32), 'Wv': jax.random.uniform(k3, (HIDDEN, HIDDEN), jnp.float32, -bound, bound), 'bv': jnp.zeros((HIDDEN,), jnp.float32), 'anomaly_matrix': jax.random.uniform(k4, (HIDDEN, HIDDEN), jnp.float32, -2.0, 2.0)}
    _L0_attn_all = _L0_attn_setup()
    _L0_attn_in = {k: v for k, v in _L0_attn_all.items() if k in ('Wq', 'bq', 'Wv', 'bv', 'anomaly_matrix')}
    del _L0_attn_all

    def _L0_xattn_setup():
        import jax, jax.numpy as jnp
        import numpy as np
        DIM = 256
        HEAD_DIM = 64
        NUM_HEADS = DIM // HEAD_DIM
        SCALE = HEAD_DIM ** (-0.5)
        key = jax.random.key(seed)
        k_x, k_ctx, k_wq, k_wkv, k_wo = jax.random.split(key, 5)
        B, N, M = (2, 512, 512)
        x = jax.random.normal(k_x, (B, N, DIM), dtype=jnp.float32)
        context = jax.random.normal(k_ctx, (B, M, DIM), dtype=jnp.float32)
        mask = jnp.ones((B, N, M), dtype=bool)
        s = DIM ** (-0.5)
        Wq = jax.random.normal(k_wq, (DIM, DIM), dtype=jnp.float32) * s
        Wkv = jax.random.normal(k_wkv, (DIM, 2 * DIM), dtype=jnp.float32) * s
        Wo = jax.random.normal(k_wo, (DIM, DIM), dtype=jnp.float32) * s
        return {'x': x, 'context': context, 'mask': mask, 'Wq': Wq, 'Wkv': Wkv, 'Wo': Wo}
    _L0_xattn_all = _L0_xattn_setup()
    _L0_xattn_in = {k: v for k, v in _L0_xattn_all.items() if k in ('Wq', 'Wkv', 'Wo')}
    del _L0_xattn_all

    def _L0_ffn_setup():
        import jax, jax.numpy as jnp
        import numpy as np
        D_MODEL = 256
        D_FF = 1024
        N_EXPERTS = 4
        key = jax.random.key(seed)
        ks = jax.random.split(key, 8)
        s_in = 1.0 / np.sqrt(D_MODEL)
        s_ff = 1.0 / np.sqrt(D_FF)
        x = jax.random.normal(ks[0], (4, 512, D_MODEL), dtype=jnp.float32)
        W1 = jax.random.uniform(ks[1], (N_EXPERTS, D_MODEL, D_FF), jnp.float32, -s_in, s_in)
        b1 = jax.random.uniform(ks[2], (N_EXPERTS, D_FF), jnp.float32, -s_in, s_in)
        W2 = jax.random.uniform(ks[3], (N_EXPERTS, D_FF, D_MODEL), jnp.float32, -s_ff, s_ff)
        b2 = jax.random.uniform(ks[4], (N_EXPERTS, D_MODEL), jnp.float32, -s_ff, s_ff)
        Wg = jax.random.uniform(ks[5], (D_MODEL, N_EXPERTS), jnp.float32, -s_in, s_in)
        bg = jax.random.uniform(ks[6], (N_EXPERTS,), jnp.float32, -s_in, s_in)
        return {'x': x, 'W1': W1, 'b1': b1, 'W2': W2, 'b2': b2, 'Wg': Wg, 'bg': bg}
    _L0_ffn_all = _L0_ffn_setup()
    _L0_ffn_in = {k: v for k, v in _L0_ffn_all.items() if k in ('W1', 'b1', 'W2', 'b2', 'Wg', 'bg')}
    del _L0_ffn_all
    return {'x': x, 'ctx_1024': ctx_1024, 'mask_BxSxS2_bf1': mask_BxSxS2_bf1, 'L0_attn_Wq': _L0_attn_in['Wq'], 'L0_attn_bq': _L0_attn_in['bq'], 'L0_attn_Wv': _L0_attn_in['Wv'], 'L0_attn_bv': _L0_attn_in['bv'], 'L0_attn_anomaly_matrix': _L0_attn_in['anomaly_matrix'], 'L0_xattn_Wq': _L0_xattn_in['Wq'], 'L0_xattn_Wkv': _L0_xattn_in['Wkv'], 'L0_xattn_Wo': _L0_xattn_in['Wo'], 'L0_ffn_W1': _L0_ffn_in['W1'], 'L0_ffn_b1': _L0_ffn_in['b1'], 'L0_ffn_W2': _L0_ffn_in['W2'], 'L0_ffn_b2': _L0_ffn_in['b2'], 'L0_ffn_Wg': _L0_ffn_in['Wg'], 'L0_ffn_bg': _L0_ffn_in['bg']}

def reference(x, ctx_1024, mask_BxSxS2_bf1, L0_attn_Wq, L0_attn_bq, L0_attn_Wv, L0_attn_bv, L0_attn_anomaly_matrix, L0_xattn_Wq, L0_xattn_Wkv, L0_xattn_Wo, L0_ffn_W1, L0_ffn_b1, L0_ffn_W2, L0_ffn_b2, L0_ffn_Wg, L0_ffn_bg):
    import jax
    import jax.numpy as jnp

    def _L0_attn_ref(hidden_states, Wq, bq, Wv, bv, anomaly_matrix):
        import jax, jax.numpy as jnp
        import numpy as np
        HIDDEN = 256
        B, S = (8, 512)
        input_norm = jnp.linalg.norm(hidden_states, axis=-1, keepdims=True)
        scaled = hidden_states / (input_norm + 1e-09)
        q = jnp.einsum('bsh,oh->bso', scaled, Wq) + bq
        v = jnp.einsum('bsh,oh->bso', scaled, Wv) + bv
        tq = jnp.einsum('bsh,hk->bsk', q, anomaly_matrix)
        scores = jnp.einsum('bsh,bth->bst', q, tq) / jnp.sqrt(jnp.float32(HIDDEN))
        probs = jax.nn.softmax(scores, axis=-1)
        ctx = jnp.einsum('bst,bth->bsh', probs, v)
        return ctx * input_norm

    def _L0_xattn_ref(x, context, mask, Wq, Wkv, Wo):
        import jax, jax.numpy as jnp
        import numpy as np
        DIM = 256
        HEAD_DIM = 64
        NUM_HEADS = DIM // HEAD_DIM
        SCALE = HEAD_DIM ** (-0.5)
        B, N, C = x.shape
        M = context.shape[1]
        H, D = (NUM_HEADS, HEAD_DIM)
        q = (x @ Wq).reshape(B, N, H, D).transpose(0, 2, 1, 3)
        kv = (context @ Wkv).reshape(B, M, 2, H, D).transpose(2, 0, 3, 1, 4)
        k, v = (kv[0], kv[1])
        attn = jnp.einsum('bhnd,bhmd->bhnm', q, k) * SCALE
        attn = jnp.where(mask[:, None, :, :], attn, -jnp.inf)
        attn = jax.nn.softmax(attn, axis=-1)
        out = jnp.einsum('bhnm,bhmd->bhnd', attn, v)
        out = out.transpose(0, 2, 1, 3).reshape(B, N, C)
        return out @ Wo

    def _L0_ffn_ref(x, W1, b1, W2, b2, Wg, bg):
        import jax, jax.numpy as jnp
        import numpy as np
        D_MODEL = 256
        D_FF = 1024
        N_EXPERTS = 4
        gate_logits = jnp.einsum('bld,de->ble', x, Wg) + bg
        idx = jnp.argmax(jax.nn.softmax(gate_logits, axis=-1), axis=-1)
        h = jnp.einsum('bld,edf->belf', x, W1) + b1[None, :, None, :]
        h = jax.nn.gelu(h, approximate=False)
        y = jnp.einsum('belf,efd->beld', h, W2) + b2[None, :, None, :]
        onehot = jax.nn.one_hot(idx, N_EXPERTS, dtype=x.dtype)
        out = jnp.einsum('beld,ble->bld', y, onehot)
        return out
    x = x + _L0_attn_ref(_layernorm(x, axis=-1), L0_attn_Wq, L0_attn_bq, L0_attn_Wv, L0_attn_bv, L0_attn_anomaly_matrix)
    x = x + _L0_xattn_ref(_layernorm(x, axis=-1), ctx_1024, mask_BxSxS2_bf1, L0_xattn_Wq, L0_xattn_Wkv, L0_xattn_Wo)
    x = x + _L0_ffn_ref(_layernorm(x, axis=-1), L0_ffn_W1, L0_ffn_b1, L0_ffn_W2, L0_ffn_b2, L0_ffn_Wg, L0_ffn_bg)
    return x

_drawn_inputs = setup_inputs


def setup_inputs(seed=0):
    import zlib

    import numpy as np

    out = dict(_drawn_inputs(seed))
    spreads = {'L0_attn_bq': (0.0, 0.727), 'L0_attn_bv': (0.0, 0.1)}
    factors = {'L0_attn_Wq': 5.042,
     'L0_attn_Wv': 2.858,
     'L0_attn_anomaly_matrix': 4.824,
     'L0_ffn_b1': 8.0,
     'L0_ffn_b2': 6.19,
     'L0_ffn_bg': 3.29}
    for name, (base, spread) in spreads.items():
        noise = np.random.default_rng([zlib.crc32(name.encode()), seed]).standard_normal(out[name].shape)
        drawn = base * np.exp(spread * noise) if base else spread * noise
        out[name] = jnp.asarray(drawn.astype(out[name].dtype))
    for name, factor in factors.items():
        out[name] = (out[name] * factor).astype(out[name].dtype)
    return out
```

```python
from contextlib import ExitStack

import numpy as np

import concourse.bass as bass
from concourse import mybir

ALU = mybir.AluOpType
ACT = mybir.ActivationFunctionType
AX = mybir.AxisListType
F32 = mybir.dt.float32
F32R = mybir.dt.float32r
F16 = mybir.dt.float16
BF16 = mybir.dt.bfloat16
U8 = mybir.dt.uint8
I32 = mybir.dt.int32
U32 = mybir.dt.uint32

P = 128
N = 2048
D = 256
C = D // P
T = N // P
M = 1601
H = 4
HD = D // H
KB = 402
MP = 4 * KB
MC = -(-M // P)
MLAST = M - (MC - 1) * P
NB = N // 512
E = 4
DF = 1024
FC = DF // P
EPS = 1e-5
PAD_BIAS = -3.38e38
MAX_CAP = 3.0e38
MASKED = 3.4e38
REGION = N + P
SPARE = E * REGION
REC = D + 4
BLOCKS = T + E - 1
XROWS = SPARE + E * P
V_TOP = 4096.0
RING = 4
NOBODY = 65536.0


LOOP = False
DBG = False


def split_groups(h):
    return [range(g, min(g + 4, MC)) for g in range(0, MC, 4)]


XG = split_groups(0)
NG = len(XG)

USES = ([("x", 3, 0), ("x", 3, 1), ("xn",), ("x", 3, 2), ("x", 3, 3), ("xq",), ("qs",), ("o",), ("wo",)]
        + [("s", 0), ("x3",), ("s", 1), ("x", 0, 0), ("x", 0, 1), ("x", 0, 2), ("x", 0, 3), ("gate",)]
        + [("s", 2), ("x", 1, 0), ("x", 1, 1), ("x", 1, 2), ("x", 1, 3), ("rank",)]
        + [("s", 3), ("x", 2, 0), ("x", 2, 1), ("x", 2, 2), ("x", 2, 3)])
assert len(USES) % 2 == 0


def stage_of(use):
    if use[0] == "s":
        return 0
    if use[0] in ("xn", "xq", "qs") or (use[0] == "x" and use[1] < 3):
        return 1
    return 2


def active(use, j):
    return 0 <= j - stage_of(use) < T


def previous_use(use, j):
    k = USES.index(use)
    bank = k % 2
    for back in range(3):
        order = USES[:k] if back == 0 else USES
        for at in range(len(order) - 1, -1, -1):
            if at % 2 == bank and active(USES[at], j - back):
                return USES[at], back
    return None, 0


def build(nc, io):
    with ExitStack() as ctx:
        emit(nc, io, ctx)


def emit(nc, io, ctx):
    def sb(name, shape, dt, on=None):
        return (on or ctx).enter_context(nc.sbuf_tensor(name, shape, dt))

    def sem(name):
        return ctx.enter_context(nc.semaphore(name))

    u_dram = nc.dram_tensor("u_dram", [T, P, 2 * C, P], F32, kind="Internal").ap()
    rows_dram = nc.dram_tensor("rows_dram", [XROWS, REC], F32, kind="Internal").ap()

    scores = ctx.enter_context(nc.psum_tensor("scores", [P, 4, 512], F32))
    flip = ctx.enter_context(nc.psum_tensor("flip", [P, 2, 512], F32))
    self_out = ctx.enter_context(nc.psum_tensor("self_out", [P, 512], F32))
    cross_out = ctx.enter_context(nc.psum_tensor("cross_out", [P, 512], F32))

    ident = sb("ident", [P, P], F32)
    barrier = sb("barrier", [P, 4], F32)
    below = sb("below", [P, P], BF16)
    ones = sb("ones", [P, P], BF16)
    minus_half = sb("minus_half", [P, T], F32)
    plus_half = sb("plus_half", [P, T], F32)
    token = sb("token", [P, 1], F32)
    expert_w = sb("expert_w", [P, E], F32)
    seen = sb("seen", [P, E], F32)
    norms = sb("norms", [P, T], F32)
    v_scale = sb("v_scale", [P, 2], F32)
    bg_row = sb("bg_row", [P, E], F32)
    wg = sb("wg", [P, C, E], F32)
    wq_cross = sb("wq_cross", [P, 2, C, D], F32R)
    wo_cross = sb("wo_cross", [P, 2, C, D], F32R)
    region_base = sb("region_base", [P, E], F32)
    lane = sb("lane", [P, 1], F32)
    sixteenth = sb("sixteenth", [P, E, T], F32)
    block_no = sb("block_no", [P, 2, BLOCKS], F32)

    ffn = ExitStack()
    w1s = sb("w1s", [P, 2, C, E * DF], F32R, ffn)
    w2s = sb("w2s", [P, 2, FC, E * D], F32R, ffn)
    w_stage = sb("w_stage", [P, 2, C * DF], F32, ffn)
    b1_row = sb("b1_row", [P, E * DF], F32, ffn)
    b2_row = sb("b2_row", [P, E * D], F32, ffn)
    rows = sb("rows", [P, RING, REC], F32, ffn)
    xn_f = sb("xn_f", [P, D], F32, ffn)
    xt_f = sb("xt_f", [P, 2, C, P], F32R, ffn)
    hidden = sb("hidden", [P, DF], F32, ffn)
    ht = sb("ht", [P, 2, FC, P], F32R, ffn)
    base_f = sb("base_f", [P, D], F32, ffn)
    out_f = sb("out_f", [P, 2, D], F32, ffn)
    who = sb("who", [P, RING, 1], U32, ffn)
    bs_f = sb("bs_f", [P, 6], F32, ffn)
    mv_f = sb("mv_f", [P, 2], F32, ffn)
    rs_f = sb("rs_f", [P, 2], F32, ffn)
    count = sb("count", [P, E], F32, ffn)
    over = sb("over", [P, E, T], F32, ffn)
    need = sb("need", [P, E], F32, ffn)
    ends = sb("ends", [P, E], F32, ffn)
    past = sb("past", [P, BLOCKS, E], F32, ffn)
    past_n = sb("past_n", [P, BLOCKS, E], F32, ffn)
    tab = sb("tab", [P, 5, BLOCKS], F32, ffn)
    table = sb("table", [P, 3, BLOCKS], I32, ffn)
    ffn.close()

    keep = ctx.enter_context(ExitStack())
    keys_self = sb("keys_self", [P, 2, C, N], F32R, keep)
    vals_self = sb("vals_self", [P, T, 2, D], F32R, keep)
    keys_cross = sb("keys_cross", [P, 2, H, MP], F32R, keep)
    vals_cross = sb("vals_cross", [P, MC, H, 2, HD], F16, keep)

    s_const = sem("s_const")
    s_wload = [sem(f"s_wload{i}") for i in range(8)]
    s_x_in = sem("s_x_in")

    pro = ExitStack()
    w_raw = sb("w_raw", [P, 3, C, D], F32, pro)
    w_self = sb("w_self", [P, 3, 2, C, D], F32R, pro)
    x_all = sb("x_all", [P, T, D], F32, pro)
    xt_pro = sb("xt_pro", [P, 2, C, 512], F32R, pro)
    u_out = sb("u_out", [P, 4, 2 * C, P], F32R, pro)
    v_tmp = sb("v_tmp", [P, 2, D], F32, pro)
    stats_pro = sb("stats_pro", [P, T, 6], F32, pro)
    mv_pro = sb("mv_pro", [P, T, 2], F32, pro)
    lnw = sb("lnw", [P, 6, T], F32, pro)
    bq_col = sb("bq_col", [P, C], F32, pro)
    bv_row = sb("bv_row", [P, D], F32, pro)
    pro_names = (w_raw, w_self, x_all, xt_pro, u_out, v_tmp)
    pro.close()

    pro2 = ExitStack()
    w2_raw = sb("w2_raw", [P, 4, C, D], F32, pro2)
    wk_dup = sb("wk_dup", [P, 2, C, H, 2, HD], F32R, pro2)
    wv_cross = sb("wv_cross", [P, 2, C, D], F32R, pro2)
    ctx_raw = sb("ctx_raw", [P, C, KB], F32, pro2)
    ctx_t = sb("ctx_t", [P, 2, C, MP], F32R, pro2)
    v_f32 = sb("v_f32", [P, MC, D], F32, pro2)
    v_max = sb("v_max", [P, 4], F32, pro2)
    pro2.close()

    loop = ExitStack()
    u_tile = sb("u_tile", [P, 2 * C, P], F32R, loop)
    x_tile = sb("x_tile", [P, D], F32, loop)
    mask_tile = sb("mask_tile", [P, M], U8, loop)
    mask_bias = sb("mask_bias", [P, MP], BF16, loop)
    exp_self = sb("exp_self", [P, N], F32, loop)
    exp_cross = sb("exp_cross", [P, 2, MP], F32, loop)
    ps_self = sb("ps_self", [P, 2, 2, 512], F32R, loop)
    ps_cross = sb("ps_cross", [P, 2, 2, 512], F16, loop)
    x1 = sb("x1", [P, D], F32, loop)
    x1_old = sb("x1_old", [P, D], F32, loop)
    xn = sb("xn", [P, D], F32, loop)
    xt = sb("xt", [P, 2, C, P], F32R, loop)
    qs = sb("qs", [P, H, 2, HD], F32R, loop)
    qt = sb("qt", [P, H, P], F32R, loop)
    o_sum = sb("o_sum", [P, H, HD], F32, loop)
    o_tile = sb("o_tile", [P, D], F32, loop)
    ot = sb("ot", [P, 2, C, P], F32R, loop)
    record = sb("record", [P, REC], F32, loop)
    xn3 = sb("xn3", [P, D], F32, loop)
    x3t = sb("x3t", [P, C, P], F32, loop)
    pads = sb("pads", [P, REC], F32, loop)
    bs1 = sb("bs1", [P, 6], F32, loop)
    mv1 = sb("mv1", [P, 2], F32, loop)
    rs1 = sb("rs1", [P, 2], F32, loop)
    bs3 = sb("bs3", [P, 6], F32, loop)
    mv3 = sb("mv3", [P, 2], F32, loop)
    rs3 = sb("rs3", [P, 2], F32, loop)
    norm_col = sb("norm_col", [P, 1], F32, loop)
    smax = sb("smax", [P, NB], F32, loop)
    sneg = sb("sneg", [P, 1], F32, loop)
    sden = sb("sden", [P, 1], F32, loop)
    scoef = sb("scoef", [P, 2], F32, loop)
    xneg = sb("xneg", [P, 2, 2], F32, loop)
    xden = sb("xden", [P, H], F32, loop)
    xcoef = sb("xcoef", [P, 2, H], F32, loop)
    logits = sb("logits", [P, E], F32, loop)
    gsc = sb("gsc", [P, 6, E], F32, loop)
    onehot = sb("onehot", [P, E], F32, loop)
    onehot16 = sb("onehot16", [P, E], BF16, loop)
    dest = sb("dest", [P, 1], F32, loop)
    dest_i = sb("dest_i", [P, 1], U32, loop)
    rank_e = sb("rank_e", [P, E], F32, loop)
    pad_i = sb("pad_i", [P, 2 * E], U32, loop)
    pad_f = sb("pad_f", [P, 2 * E], F32, loop)
    loop.close()

    s_w0 = sem("s_w0")
    s_xstat = sem("s_xstat")
    s_ln = sem("s_ln")
    s_lnd = sem("s_lnd")
    s_xs = sem("s_xs")
    s_wsplit_hi = sem("s_wsplit_hi")
    s_wsplit_lo = sem("s_wsplit_lo")
    s_ptf = sem("s_ptf")
    s_pthi = sem("s_pthi")
    s_ptlo = sem("s_ptlo")
    s_q = sem("s_q")
    s_qhi = sem("s_qhi")
    s_qlo = sem("s_qlo")
    s_u = sem("s_u")
    s_uhi = sem("s_uhi")
    s_ulo = sem("s_ulo")
    s_u_st = sem("s_u_st")
    s_v = sem("s_v")
    s_vt = sem("s_vt")
    s_vhi = sem("s_vhi")
    s_vlo = sem("s_vlo")
    s_pro1 = sem("s_pro1")
    s_w2 = sem("s_w2")
    s_w2hi = sem("s_w2hi")
    s_w2lo = sem("s_w2lo")
    s_ctx = sem("s_ctx")
    s_ctxhi = sem("s_ctxhi")
    s_ctxlo = sem("s_ctxlo")
    s_k = sem("s_k")
    s_khi = sem("s_khi")
    s_klo = sem("s_klo")
    s_vx = sem("s_vx")
    s_vxf = sem("s_vxf")
    s_vmax = sem("s_vmax")
    s_vall = sem("s_vall")
    s_vsc = sem("s_vsc")
    s_vxhi = sem("s_vxhi")
    s_vxlo = sem("s_vxlo")

    u_loaded = sem("u_loaded")
    x_loaded = sem("x_loaded")
    mask_loaded = sem("mask_loaded")
    scores_ready = sem("scores_ready")
    max_part = sem("max_part")
    self_max = sem("self_max")
    self_exp = sem("self_exp")
    s_flipped = sem("s_flipped")
    s_hi = sem("s_hi")
    s_lo = sem("s_lo")
    s_used = sem("s_used")
    norm_ready = sem("norm_ready")
    coef_step = sem("coef_step")
    x1_ready = sem("x1_ready")
    stats1 = sem("stats1")
    rstd1 = sem("rstd1")
    xn_ready = sem("xn_ready")
    xn_flipped = sem("xn_flipped")
    xt_hi = sem("xt_hi")
    xt_lo = sem("xt_lo")
    q_ready = sem("q_ready")
    qs_hi = sem("qs_hi")
    qs_lo = sem("qs_lo")
    q_flipped = sem("q_flipped")
    qt_ready = sem("qt_ready")
    bias_ready = sem("bias_ready")
    xs_ready = sem("xs_ready")
    xmax_a = sem("xmax_a")
    xmax = sem("xmax")
    xexp = sem("xexp")
    x_flipped = sem("x_flipped")
    x_hi = sem("x_hi")
    x_lo = sem("x_lo")
    x_used = sem("x_used")
    o_summed = sem("o_summed")
    o_step = sem("o_step")
    o_ready = sem("o_ready")
    o_flipped = sem("o_flipped")
    ot_hi = sem("ot_hi")
    ot_lo = sem("ot_lo")
    wo_ready = sem("wo_ready")
    x2_ready = sem("x2_ready")
    x1_copied = sem("x1_copied")
    stats3 = sem("stats3")
    mean1 = sem("mean1")
    mean3 = sem("mean3")
    rstd3 = sem("rstd3")
    xn3_ready = sem("xn3_ready")
    x3_flipped = sem("x3_flipped")
    x3t_ready = sem("x3t_ready")
    gate_ready = sem("gate_ready")
    logits_ready = sem("logits_ready")
    gate_step = sem("gate_step")
    onehot_ready = sem("onehot_ready")
    rank_ready = sem("rank_ready")
    rank_added = sem("rank_added")
    rank_used = sem("rank_used")
    dest_step = sem("dest_step")
    dest_ready = sem("dest_ready")
    token_set = sem("token_set")
    token_next = sem("token_next")
    routed = sem("routed")
    s_pads = sem("s_pads")
    s_pad_ok = sem("s_pad_ok")
    s_dbg = sem("s_dbg")

    attention_done = sem("attention_done")
    pad_dest = sem("pad_dest")
    pad_dest_i = sem("pad_dest_i")
    pads_out = sem("pads_out")
    table_step = sem("table_step")
    table_ready = sem("table_ready")
    w_loaded = [sem("w_loaded_even"), sem("w_loaded_odd")]
    b_loaded = sem("b_loaded")
    w_hi = sem("w_hi")
    w_lo = sem("w_lo")
    rows_loaded = sem("rows_loaded")
    f_stats = sem("f_stats")
    f_mean = sem("f_mean")
    f_eps = sem("f_eps")
    f_rstd = sem("f_rstd")
    f_xn = sem("f_xn")
    f_who = sem("f_who")
    f_x_flipped = sem("f_x_flipped")
    f_xt_hi = sem("f_xt_hi")
    f_xt_lo = sem("f_xt_lo")
    f_h = sem("f_h")
    f_bias = sem("f_bias")
    f_gelu = sem("f_gelu")
    f_h_flipped = sem("f_h_flipped")
    f_ht_hi = sem("f_ht_hi")
    f_ht_lo = sem("f_ht_lo")
    f_y = sem("f_y")
    f_base = sem("f_base")
    f_out = sem("f_out")
    f_stored = sem("f_stored")

    done = {
        "s": lambda u, t: (s_lo, 4 * t + u[1] + 1),
        "x": lambda u, t: (x_lo, 16 * t + 4 * u[1] + u[2] + 1),
        "xn": lambda u, t: (xt_lo, t + 1),
        "xq": lambda u, t: (qs_lo, t + 1),
        "qs": lambda u, t: (qt_ready, t + 1),
        "o": lambda u, t: (ot_lo, t + 1),
        "wo": lambda u, t: (x2_ready, t + 1),
        "x3": lambda u, t: (x3t_ready, t + 1),
        "gate": lambda u, t: (logits_ready, t + 1),
        "rank": lambda u, t: (rank_used, t + 1),
    }

    def bank(use):
        return USES.index(use) % 2

    GROUPS = N // 512
    block = ctx.enter_context(nc.Block())

    def run_pipeline(eng, body):
        for j in (0, 1):
            body(j, j)
        if LOOP:
            with eng.Fori(2, T - 1) as j:
                body(j, 5)
        else:
            for j in range(2, T - 1):
                body(j, j)
        for j in (T - 1, T, T + 1):
            body(j, j)

    def run_blocks(eng, body):
        body(0, 0)
        if LOOP:
            with eng.Fori(1, BLOCKS - 2, RING) as b:
                for n in range(RING):
                    body(b + n, 1 + n + RING)
        else:
            for b in range(1, BLOCKS - 2):
                body(b, b)
        for b in (BLOCKS - 2, BLOCKS - 1, BLOCKS):
            body(b, b)

    @block.sync
    def _(sp):
        sp.dma_start(x_all[:, :, :], io["x"].rearrange("(t p) d -> p t d", p=P)).then_inc(s_x_in, 16)
        for n, w in enumerate(("WqT", "AT", "WvT")):
            sp.dma_start(w_raw[:, n, :, :], io[w].rearrange("(c p) n -> p c n", p=P)).then_inc(s_w0, 16)
        sp.dma_start(bq_col[:, :], io["bq"].rearrange("(c p) -> p c", p=P), allow_slow_non_contiguous=True).then_inc(s_w0, 16)
        sp.dma_start(bv_row[:, :], bass.AP(io["bv"].tensor, 0, [[0, P], [1, D]])).then_inc(s_w0, 16)
        sp.dma_start(bg_row[:, :], bass.AP(io["bg"].tensor, 0, [[0, P], [1, E]])).then_inc(s_w0, 16)
        sp.dma_start(wg[:, :, :], io["Wg"].rearrange("(c p) e -> p c e", p=P)).then_inc(s_w0, 16)
        for g in range(GROUPS):
            sp.wait_ge(s_ulo, C * (g + 1))
            sp.wait_ge(s_uhi, C * (g + 1))
            sp.dma_start(u_dram[4 * g:4 * g + 4].rearrange("t p c s -> p t c s"), u_out[:, :, :, :].bitcast(F32)).then_inc(s_u_st, 16)
        sp.wait_ge(s_u_st, 16 * GROUPS)
        sp.wait_ge(s_pro1, 3)
        wkv = io["Wkv"].rearrange("(c p) n -> p c n", p=P)
        sp.dma_start(w2_raw[:, 0, :, :], wkv[:, :, 0:D]).then_inc(s_w2, 16)
        sp.dma_start(w2_raw[:, 1, :, :], wkv[:, :, D:2 * D]).then_inc(s_w2, 16)
        sp.dma_start(w2_raw[:, 2, :, :], io["xWq"].rearrange("(c p) n -> p c n", p=P)).then_inc(s_w2, 16)
        sp.dma_start(w2_raw[:, 3, :, :], io["Wo"].rearrange("(c p) n -> p c n", p=P)).then_inc(s_w2, 16)
        ctx_v = io["ctxT"].rearrange("(c p) m -> p c m", p=P)
        for g in range(4):
            lo, hi = g * KB, min((g + 1) * KB, M)
            if g:
                sp.wait_ge(s_ctxlo, g)
            sp.dma_start(ctx_raw[:, :, 0:hi - lo], ctx_v[:, :, lo:hi]).then_inc(s_ctx, 16)

        sp.wait_ge(s_pro1, 6)
        def loads_a(t):
            sp.dma_start(u_tile[:, :, :].bitcast(F32), u_dram[bass.ds(t, 1), :, :, :].rearrange("a p c s -> p (a c) s")).then_inc(u_loaded, 16)

        def loads_x(t):
            sp.dma_start(x_tile[:, :], io["x"][bass.ds(t * P, P), :]).then_inc(x_loaded, 16)

        def loads_m(t):
            sp.dma_start(mask_tile[:, :], io["mask"][bass.ds(t * P, P), :]).then_inc(mask_loaded, 16)

        loads_a(0)
        loads_x(0)
        loads_m(0)

        def body(j, k):
            if k < T - 1:
                sp.wait_ge(scores_ready, 4 * j + 4)
                loads_a(j + 1)
            if 1 <= k <= T - 1:
                sp.wait_ge(x1_ready, j)
                loads_x(j)
            if 1 <= k <= T - 1:
                sp.wait_ge(bias_ready, j)
                loads_m(j)
            if DBG and k >= 2:
                sp.wait_ge(dest_ready, j - 1)
                sp.wait_ge(token_set, j - 1)
                sp.dma_start(io["dbg"][bass.ds((j - 2) * P, P), :], record[:, :]).then_inc(s_dbg, 16)
        run_pipeline(sp, body)

        sp.wait_ge(attention_done, 3)
        sp.wait_ge(routed, 16 * T)
        for n in range(2 * E):
            e = n % E
            if n >= 2:
                sp.wait_ge(w_hi, n - 1)
                sp.wait_ge(w_lo, n - 1)
            if n < E:
                sp.dma_start(w_stage[:, n % 2, :].rearrange("p (c n) -> p c n", c=C),
                             io["W1"][e].rearrange("(c p) n -> p c n", p=P)).then_inc(w_loaded[n % 2], 16)
            else:
                sp.dma_start(w_stage[:, n % 2, :].rearrange("p (c n) -> p c n", c=FC),
                             io["W2"][e].rearrange("(c p) n -> p c n", p=P)).then_inc(w_loaded[n % 2], 16)
            if n == 1:
                sp.dma_start(b1_row[:, :], bass.AP(io["b1"].tensor, 0, [[0, P], [1, E * DF]])).then_inc(b_loaded, 16)
                sp.dma_start(b2_row[:, :], bass.AP(io["b2"].tensor, 0, [[0, P], [1, E * D]])).then_inc(b_loaded, 16)

        sp.wait_ge(s_pad_ok, 16 * E)
        sp.wait_ge(pads_out, 16 * E)
        sp.wait_ge(table_ready, 3)

        def load_rows(b, k):
            if k >= 1:
                sp.wait_ge(rows_loaded, 16 * b)
            row = sp.value_load(table[0:1, 0, bass.ds(b, 1)], min_val=0, max_val=XROWS - P)
            sp.dma_start(rows[:, k % RING, :], rows_dram[bass.ds(row, P), :]).then_inc(rows_loaded, 16)

        for b in range(2):
            load_rows(b, b)

        def blocks(b, k):
            if k < BLOCKS - 2:
                if k >= 2:
                    sp.wait_ge(f_base, b - 1)
                    sp.wait_ge(f_who, b - 1)
                load_rows(b + 2, k + 2)
        run_blocks(sp, blocks)
        sp.wait_ge(f_stored, 16 * BLOCKS)

    @block.gpsimd
    def _(pool):
        pool.memset(ident[:, :], 0.0).then_inc(s_const, 1)
        pool.memset(below[:, :], 1.0).then_inc(s_const, 1)
        pool.memset(ones[:, :], 1.0).then_inc(s_const, 1)
        pool.memset(minus_half[:, :], -0.5).then_inc(s_const, 1)
        pool.memset(plus_half[:, :], 0.5).then_inc(s_const, 1)
        pool.iota(token[:, :], pattern=[[0, 1]], base=0, channel_multiplier=1,
                  allow_small_or_imprecise_dtypes=True).then_inc(s_const, 1)
        pool.iota(expert_w[:, :], pattern=[[-1, E]], base=E, channel_multiplier=0,
                  allow_small_or_imprecise_dtypes=True).then_inc(s_const, 1)
        pool.iota(seen[:, :], pattern=[[REGION, E]], base=0, channel_multiplier=0,
                  allow_small_or_imprecise_dtypes=True).then_inc(s_const, 1)
        pool.iota(region_base[:, :], pattern=[[REGION, E]], base=0, channel_multiplier=0,
                  allow_small_or_imprecise_dtypes=True).then_inc(s_const, 1)
        pool.iota(lane[:, :], pattern=[[0, 1]], base=0, channel_multiplier=1,
                  allow_small_or_imprecise_dtypes=True).then_inc(s_const, 1)
        pool.iota(sixteenth[:, :, :], pattern=[[0, E], [P, T]], base=0, channel_multiplier=0,
                  allow_small_or_imprecise_dtypes=True).then_inc(s_const, 1)
        pool.iota(block_no[:, 0, :], pattern=[[1, BLOCKS]], base=0, channel_multiplier=0,
                  allow_small_or_imprecise_dtypes=True).then_inc(s_const, 1)
        pool.iota(block_no[:, 1, :], pattern=[[P, BLOCKS]], base=0, channel_multiplier=0,
                  allow_small_or_imprecise_dtypes=True).then_inc(s_const, 1)
        pool.wait_ge(s_const, 2)
        pool.affine_select(out=ident[:, :], in_=ident[:, :], compare_op=ALU.not_equal, fill=1.0, base=0,
                           pattern=[[-1, P]], channel_multiplier=1).then_inc(s_const, 1)
        pool.affine_select(out=below[:, :], in_=below[:, :], compare_op=ALU.is_gt, fill=0.0, base=0,
                           pattern=[[1, P]], channel_multiplier=-1).then_inc(s_const, 1)
        pool.wait_ge(s_const, 5)
        pool.wait_ge(s_lnd, 1)
        pool.tensor_tensor(lnw[:, 1, :], lnw[:, 0, :], minus_half[:, :], ALU.pow).then_inc(s_ln, 1)
        pool.tensor_tensor(lnw[:, 2, :], mv_pro[:, :, 1], plus_half[:, :], ALU.pow).then_inc(s_ln, 1)
        pool.wait_ge(s_pro1, 3)
        pool.wait_ge(s_u_st, 16 * GROUPS)
        pool.memset(v_f32[:, MC - 1, :], 0.0).then_inc(s_vall, 1)
        pool.wait_ge(s_vmax, 1)
        pool.partition_all_reduce(v_max[:, 1:2], v_max[:, 0:1], P, bass.bass_isa.ReduceOp.max).then_inc(s_vall, 1)

        pool.wait_ge(s_pro1, 6)
        pool.memset(mask_bias[:, M:MP], PAD_BIAS).then_inc(s_pads, 1)
        pool.memset(pads[:, :], 0.0).then_inc(s_pads, 1)
        pool.wait_ge(s_pads, 2)
        pool.memset(pads[:, D:REC], NOBODY).then_inc(s_pads, 1)
        pool.memset(record[:, D + 1:REC], 0.0).then_inc(s_pads, 1)
        pool.wait_ge(s_pads, 4)
        for n in range(E):
            pool.dma_start(rows_dram[SPARE + n * P:SPARE + (n + 1) * P, :], pads[:, :]).then_inc(s_pad_ok, 16)

        def body(j, k):
            a, b, c = k < T, 1 <= k <= T, k >= 2
            if b:
                pool.wait_ge(stats1, 2 * j)
                pool.tensor_tensor(rs1[:, 1:2], rs1[:, 0:1], minus_half[:, 0:1], ALU.pow).then_inc(rstd1, 1)
                if c:
                    pool.wait_ge(xmax, 4 * (j - 1))
                pool.wait_ge(mask_loaded, 16 * j)
                pool.wait_ge(s_pads, 1)
                pool.tensor_scalar(mask_bias[:, 0:M], mask_tile[:, :], -1.0, MASKED, ALU.add, ALU.mult).then_inc(bias_ready, 1)
            if a:
                if b:
                    pool.wait_ge(coef_step, 2 * j)
                pool.wait_ge(s_pads, 1)
                pool.tensor_copy(norm_col[:, :], norms[:, bass.ds(j, 1)]).then_inc(norm_ready, 1)
            if c:
                pool.wait_ge(stats3, 2 * (j - 1))
                pool.tensor_tensor(rs3[:, 1:2], rs3[:, 0:1], minus_half[:, 0:1], ALU.pow).then_inc(rstd3, 1)
            if b:
                if c:
                    pool.wait_ge(x2_ready, j - 1)
                pool.wait_ge(x1_ready, j)
                pool.wait_ge(s_pads, 1)
                pool.tensor_copy(x1_old[:, :], x1[:, :]).then_inc(x1_copied, 1)
            if c:
                if k > 2:
                    pool.wait_ge(token_next, j - 2)
                    pool.wait_ge(routed, 16 * (j - 2))
                pool.wait_ge(s_pads, 1)
                pool.tensor_copy(record[:, D:D + 1], token[:, :]).then_inc(token_set, 1)
                pool.wait_ge(token_set, j - 1)
                pool.wait_ge(s_pads, 1)
                pool.tensor_scalar(token[:, :], token[:, :], float(P), 1.0, ALU.add, ALU.mult).then_inc(token_next, 1)
                pool.wait_ge(x2_ready, j - 1)
                pool.wait_ge(dest_ready, j - 1)
                if DBG:
                    pool.wait_ge(s_dbg, 16 * (j - 1))
                pool.wait_ge(s_pads, 1)
                pool.indirect_dma_start(out=rows_dram[:, :], out_offset=bass.IndirectOffsetOnAxis(ap=dest_i[:, 0:1], axis=0),
                                        in_=record[:, :], in_offset=None).then_inc(routed, 16)
        run_pipeline(pool, body)

        for e in range(E):
            pool.wait_ge(pad_dest_i, 1)
            pool.indirect_dma_start(out=rows_dram[:, :], out_offset=bass.IndirectOffsetOnAxis(ap=pad_i[:, e:e + 1], axis=0),
                                    in_=pads[:, :], in_offset=None).then_inc(pads_out, 16)

        def blocks(b, k):
            def norm(b, k):
                pool.wait_ge(f_eps, b + 1)
                pool.tensor_tensor(rs_f[:, 1:2], rs_f[:, 0:1], minus_half[:, 0:1], ALU.pow).then_inc(f_rstd, 1)
                if k >= RING:
                    pool.wait_ge(f_stored, 16 * (b - RING + 1))
                pool.wait_ge(rows_loaded, 16 * (b + 1))
                pool.wait_ge(s_pads, 4)
                pool.tensor_copy(who[:, k % RING, :], rows[:, k % RING, D:D + 1]).then_inc(f_who, 1)

            if k == 0:
                norm(0, 0)
                norm(1, 1)
            if k < BLOCKS - 2:
                norm(b + 2, k + 2)
            if k >= 1:
                if k >= 2:
                    pool.wait_ge(f_stored, 16 * (b - 1))
                pool.wait_ge(f_who, b)
                pool.wait_ge(f_out, b)
                pool.wait_ge(s_pads, 4)
                pool.indirect_dma_start(out=io["out"][:, :],
                                        out_offset=bass.IndirectOffsetOnAxis(ap=who[:, (k - 1) % RING, 0:1], axis=0),
                                        in_=out_f[:, (k - 1) % 2, :], in_offset=None, bounds_check=N - 1,
                                        oob_is_err=False).then_inc(f_stored, 16)
        run_blocks(pool, blocks)

    @block.tensor
    def _(pe):
        def three(out, lhs, rhs, first=True, last=True):
            n = 0
            for c in range(C):
                for a, b in ((0, 0), (0, 1), (1, 0)):
                    mm = pe.matmul(out, lhs(a, c), rhs(b, c), start=(n == 0 and first), stop=(n == 3 * C - 1 and last))
                    n += 1
            return mm

        pe.wait_ge(s_const, 15)
        NS = 3
        for g in range(GROUPS):
            for c in range(C):
                pe.wait_ge(s_xs, 4 * (g + 1))
                if g:
                    pe.wait_ge(s_ptlo, C * (g - 1) + c + 1)
                for n in range(4):
                    tr = pe.transpose(flip[:, c, n * P:(n + 1) * P], x_all[:, 4 * g + n, c * P:(c + 1) * P], ident[:, :])
                tr.then_inc(s_ptf, 1)
            if g == 0:
                pe.wait_ge(s_wsplit_lo, NS)
            pe.wait_ge(s_ptlo, C * (g + 1))
            for o in range(C):
                if g:
                    pe.wait_ge(s_qlo, C * (g - 1) + o + 1)
                three(scores[:, o, :], lambda a, c: w_self[:, 0, a, c, o * P:(o + 1) * P],
                      lambda b, c: xt_pro[:, b, c, :]).then_inc(s_q, 1)
            for n in range(4):
                if g and n % 2 == 0:
                    pe.wait_ge(s_vt, 4 * (g - 1) + n + 2)
                three(scores[:, 2 + n // 2, (n % 2) * D:(n % 2 + 1) * D] , lambda a, c: xt_pro[:, a, c, n * P:(n + 1) * P],
                      lambda b, c: w_self[:, 2, b, c, :]).then_inc(s_v, 1)
            for o in range(C):
                pe.wait_ge(s_qlo, C * (g + 1))
                if g:
                    pe.wait_ge(s_ulo, C * (g - 1) + o + 1)
                out = self_out if o == 0 else cross_out
                three(out[:, :], lambda a, c: w_self[:, 1, a, c, o * P:(o + 1) * P],
                      lambda b, c: keys_self[:, b, c, g * 512:(g + 1) * 512]).then_inc(s_u, 1)
        pe.wait_ge(s_vt, 4 * GROUPS)

        n_k = 0
        for g in range(4):
            pe.wait_ge(s_w2lo, 4)
            pe.wait_ge(s_ctxlo, g + 1)
            for h in range(H):
                if g:
                    pe.wait_ge(s_klo, H * (g - 1) + h + 1)
                three(scores[:, h, 0:KB], lambda a, c: wk_dup[:, a, c, h, :, :],
                      lambda b, c: ctx_t[:, b, c, g * KB:(g + 1) * KB]).then_inc(s_k, 1)
        for m in range(MC):
            rows = P if m < MC - 1 else MLAST
            if m >= 2:
                pe.wait_ge(s_vxf, m - 1)
            three(flip[0:rows, m % 2, 0:D], lambda a, c: ctx_t[:, a, c, m * P:m * P + rows],
                  lambda b, c: wv_cross[:, b, c, :]).then_inc(s_vx, 1)

        pe.wait_ge(s_pro1, 6)

        def wait_bank(use, j, k):
            before, back = previous_use(use, k)
            if before is not None:
                s, v = done[before[0]](before, j - back - stage_of(before))
                pe.wait_ge(s, v)

        def self_scores(j, k, n):
            if n == 0:
                pe.wait_ge(u_loaded, 16 * (j + 1))
            if k >= 2:
                pe.wait_ge(xmax_a if n < 2 else xmax, 4 * (j - 1))
            elif k == 1:
                pe.wait_ge(self_exp, 1)
            three(scores[:, n, :], lambda a, c: u_tile[:, a * C + c, :],
                  lambda b, c: keys_self[:, b, c, n * 512:(n + 1) * 512]).then_inc(scores_ready, 1)

        def self_flip(j, k, g):
            use = ("s", g)
            if g == 0:
                pe.wait_ge(self_exp, j + 1)
            wait_bank(use, j, k)
            for n in range(4):
                m = 4 * g + n
                tr = pe.transpose(flip[:, bank(use), n * P:(n + 1) * P], exp_self[:, m * P:(m + 1) * P], ident[:, :])
            tr.then_inc(s_flipped, 1)

        def self_values(j, k, g):
            pe.wait_ge(s_lo, 4 * j + g + 1)
            if g == 0 and k >= 1:
                pe.wait_ge(x1_ready, j)
            for n in range(4):
                m = 4 * g + n
                for a, b in ((0, 0), (0, 1), (1, 0)):
                    mm = pe.matmul(self_out[:, 0:D], ps_self[:, g % 2, a, n * P:(n + 1) * P], vals_self[:, m, b, :],
                                   start=(m == 0 and a == 0 and b == 0), stop=(m == T - 1 and a == 1))
            mm.then_inc(s_used, 1)

        def cross_scores(j, k, h):
            if h == 0:
                pe.wait_ge(qt_ready, j)
                if k < T:
                    pe.wait_ge(self_exp, j + 1)
            for n in range(4):
                if h > 0 or k >= T:
                    pe.wait_ge(xmax_a if n < 2 else xmax, 4 * (j - 1) + h)
                for part in range(2):
                    mm = pe.matmul(scores[:, n, 0:KB], qt[:, h, :], keys_cross[:, part, h, n * KB:(n + 1) * KB],
                                   start=(part == 0), stop=(part == 1))
                if n % 2:
                    mm.then_inc(xs_ready, 1)

        def cross_flip(j, k, h, g):
            use = ("x", h, g)
            t = j - stage_of(use)
            if g == 0:
                pe.wait_ge(xexp, 4 * t + h + 1)
            wait_bank(use, j, k)
            for n, m in enumerate(XG[g]):
                rows = P if m < MC - 1 else MLAST
                tr = pe.transpose(flip[0:rows, bank(use), n * P:(n + 1) * P], exp_cross[:, h % 2, m * P:m * P + rows], ident[:, :])
            tr.then_inc(x_flipped, 1)

        def cross_values(j, k, h, g):
            t = j - stage_of(("x", h, g))
            pe.wait_ge(x_lo, 16 * t + 4 * h + g + 1)
            if h == 0 and g == 0 and k >= 2:
                pe.wait_ge(o_summed, t)
            for n, m in enumerate(XG[g]):
                rows = P if m < MC - 1 else MLAST
                pe.matmul(cross_out[:, h * P:(h + 1) * P], ps_cross[0:rows, g % 2, 0, n * P:(n + 1) * P],
                          vals_cross[0:rows, m, h, :, :], start=(m == 0), stop=False, skip_group_check=True)
                mm = pe.matmul(cross_out[:, h * P:h * P + HD], ps_cross[0:rows, g % 2, 1, n * P:(n + 1) * P],
                               vals_cross[0:rows, m, h, 0, :], start=False, stop=(m == MC - 1), skip_group_check=True)
            mm.then_inc(x_used, 1)

        def small(use, j, k, ready, value, filled, work):
            pe.wait_ge(ready, value)
            wait_bank(use, j, k)
            work(flip[:, bank(use), :]).then_inc(filled, 1)

        def flip_row(src):
            def work(out):
                for c in range(C):
                    tr = pe.transpose(out[:, c * P:(c + 1) * P], src[:, c * P:(c + 1) * P], ident[:, :])
                return tr
            return work

        def flip_queries(out):
            for h in range(H):
                tr = pe.transpose(out[:, h * P:(h + 1) * P], qs[:, h, :, :].bitcast(F32), ident[:, :])
            return tr

        def gate(out):
            for c in range(C):
                mm = pe.matmul(out[:, 0:E], x3t[:, c, :], wg[:, c, :], start=(c == 0), stop=(c == C - 1))
            return mm

        def rank(out):
            pe.matmul(out[:, 0:E], below[:, :], onehot16[:, :], start=True, stop=True)
            return pe.matmul(out[:, E:2 * E], ones[:, :], onehot16[:, :], start=True, stop=True)

        def body(j, k):
            a, b, c = k < T, 1 <= k <= T, k >= 2
            if a:
                self_scores(j, k, 0)
            if c:
                cross_flip(j, k, 3, 0)
                cross_flip(j, k, 3, 1)
            if a:
                self_scores(j, k, 1)
            if b:
                small(("xn",), j, k, xn_ready, j, xn_flipped, flip_row(xn))
            if c:
                cross_values(j, k, 3, 0)
                cross_flip(j, k, 3, 2)
                cross_values(j, k, 3, 1)
                cross_flip(j, k, 3, 3)
            if b:
                small(("xq",), j, k, xt_lo, j, q_ready,
                      lambda out: three(out[:, 0:D], lambda a, c: xt[:, a, c, :], lambda b, c: wq_cross[:, b, c, :]))
            if a:
                self_scores(j, k, 2)
            if c:
                cross_values(j, k, 3, 2)
                cross_values(j, k, 3, 3)
            if b:
                small(("qs",), j, k, qs_lo, j, q_flipped, flip_queries)
            if a:
                self_scores(j, k, 3)
            if c:
                small(("o",), j, k, o_ready, j - 1, o_flipped, flip_row(o_tile))
                small(("wo",), j, k, ot_lo, j - 1, wo_ready,
                      lambda out: three(out[:, 0:D], lambda a, c: ot[:, a, c, :], lambda b, c: wo_cross[:, b, c, :]))
            for h in range(H):
                if a:
                    self_flip(j, k, h)
                if b:
                    cross_scores(j, k, h)
                if h == 0 and c:
                    small(("x3",), j, k, xn3_ready, j - 1, x3_flipped, flip_row(xn3))
                if h and b:
                    cross_flip(j, k, h - 1, 0)
                if a:
                    self_values(j, k, h)
                if h and b:
                    cross_flip(j, k, h - 1, 1)
                    cross_values(j, k, h - 1, 0)
                    cross_flip(j, k, h - 1, 2)
                    cross_values(j, k, h - 1, 1)
                    cross_flip(j, k, h - 1, 3)
                if h == 1 and c:
                    small(("gate",), j, k, x3t_ready, j - 1, gate_ready, gate)
                if h == 2 and c:
                    small(("rank",), j, k, onehot_ready, j - 1, rank_ready, rank)
                if h and b:
                    cross_values(j, k, h - 1, 2)
                    cross_values(j, k, h - 1, 3)
        run_pipeline(pe, body)
        pe.wait_ge(x2_ready, T)
        pe.wait_ge(table_ready, 3)

        def flip_x(b, k):
            pe.wait_ge(f_xn, b + 1)
            for c in range(C):
                tr = pe.transpose(self_out[:, c * P:(c + 1) * P], xn_f[:, c * P:(c + 1) * P], ident[:, :])
            tr.then_inc(f_x_flipped, 1)

        def blocks(b, k):
            if k == 0:
                flip_x(0, 0)
            if k >= 1:
                for n in range(2):
                    pe.wait_ge(f_gelu, 2 * (b - 1) + n + 1)
                    for c in range(4):
                        f = 4 * n + c
                        tr = pe.transpose(flip[:, n, c * P:(c + 1) * P], hidden[:, f * P:(f + 1) * P], ident[:, :])
                    tr.then_inc(f_h_flipped, 1)
            if k < BLOCKS:
                if k == 0:
                    pe.wait_ge(w_lo, E)
                pe.wait_ge(f_xt_lo, b + 1)
                off = pe.value_load(table[0:1, 1, bass.ds(b, 1)], min_val=0, max_val=(E - 1) * DF)
                for n in range(2):
                    three(scores[:, n, :], lambda a, c: xt_f[:, a, c, :],
                          lambda p, c: w1s[:, p, c, bass.ds(off + n * 512, 512)]).then_inc(f_h, 1)
            if k < BLOCKS - 1:
                flip_x(b + 1, k + 1)
            if k >= 1:
                if k == 1:
                    pe.wait_ge(w_lo, 2 * E)
                off2 = pe.value_load(table[0:1, 2, bass.ds(b - 1, 1)], min_val=0, max_val=(E - 1) * D)
                if k >= 2:
                    pe.wait_ge(f_out, b - 1)
                for f in range(FC):
                    if f % 4 == 0:
                        pe.wait_ge(f_ht_lo, 2 * (b - 1) + f // 4 + 1)
                    for a, p in ((0, 0), (0, 1), (1, 0)):
                        mm = pe.matmul(cross_out[:, 0:D], ht[:, a, f, :], w2s[:, p, f, bass.ds(off2, D)],
                                       start=(f == 0 and a == 0 and p == 0), stop=(f == FC - 1 and a == 1))
                mm.then_inc(f_y, 1)
        run_blocks(pe, blocks)

    @block.scalar
    def _(act):
        def copy(out, in_, **kw):
            return act.activation(out, in_, ACT.Copy, **kw)

        act.wait_ge(s_w0, 16 * 7)
        for n in range(3):
            copy(w_self[:, n, 0, :, :], w_raw[:, n, :, :]).then_inc(s_wsplit_hi, 1)
        for g in range(GROUPS):
            for c in range(C):
                act.wait_ge(s_ptf, C * g + c + 1)
                if g:
                    act.wait_ge(s_v, 4 * g)
                    act.wait_ge(s_q, C * g)
                copy(xt_pro[:, 0, c, :], flip[:, c, :]).then_inc(s_pthi, 1)
            for o in range(C):
                act.wait_ge(s_q, C * g + o + 1)
                act.activation(keys_self[:, 0, o, g * 512:(g + 1) * 512], scores[:, o, :], ACT.Identity,
                               bias=bq_col[:, o:o + 1]).then_inc(s_qhi, 1)
            for n in range(4):
                act.wait_ge(s_vt, 4 * g + n + 1)
                copy(vals_self[:, 4 * g + n, 0, :], v_tmp[:, n % 2, :]).then_inc(s_vhi, 1)
            for o in range(C):
                act.wait_ge(s_u, C * g + o + 1)
                if g:
                    act.wait_ge(s_u_st, 16 * g)
                out = self_out if o == 0 else cross_out
                act.activation(u_out[:, :, o, :], out[:, :].rearrange("p (t s) -> p t s", t=4), ACT.Copy,
                               scale=1.0 / 16.0).then_inc(s_uhi, 1)
        act.wait_ge(s_ulo, C * GROUPS)
        copy(barrier[:, 0:1], ident[:, 0:1]).then_inc(s_pro1, 1)

        act.wait_ge(s_pro1, 3)
        act.wait_ge(s_u_st, 16 * GROUPS)
        act.wait_ge(s_w2, 64)
        for dup in range(2):
            copy(wk_dup[:, 0, :, :, dup, :], w2_raw[:, 0, :, :].rearrange("p c (h d) -> p c h d", h=H)).then_inc(s_w2hi, 1)
        for n, w in ((1, wv_cross), (2, wq_cross), (3, wo_cross)):
            copy(w[:, 0, :, :], w2_raw[:, n, :, :]).then_inc(s_w2hi, 1)
        for g in range(4):
            act.wait_ge(s_ctx, 16 * (g + 1))
            act.wait_ge(s_vsc, 1)
            copy(ctx_t[:, 0, :, g * KB:min((g + 1) * KB, M)], ctx_raw[:, :, 0:min(KB, M - g * KB)]).then_inc(s_ctxhi, 1)
        for g in range(4):
            for h in range(H):
                act.wait_ge(s_k, H * g + h + 1)
                copy(keys_cross[:, 0, h, g * KB:(g + 1) * KB], scores[:, h, 0:KB]).then_inc(s_khi, 1)
        for m in range(MC):
            rows = P if m < MC - 1 else MLAST
            act.wait_ge(s_vx, m + 1)
            if m == MC - 1:
                act.wait_ge(s_vall, 1)
            copy(v_f32[0:rows, m, :], flip[0:rows, m % 2, 0:D]).then_inc(s_vxf, 1)
        act.wait_ge(s_vsc, 4)
        for m in range(MC):
            act.activation(vals_cross[:, m, :, 0, :], v_f32[:, m, :].rearrange("p (h d) -> p h d", h=H), ACT.Copy,
                           scale=v_scale[:, 0:1]).then_inc(s_vxhi, 1)
        act.wait_ge(s_vxlo, MC)
        act.wait_ge(s_klo, 4 * H)
        copy(barrier[:, 2:3], ident[:, 0:1]).then_inc(s_pro1, 1)
        act.wait_ge(s_pro1, 6)

        def cross_hi(j, k, h, g):
            use = ("x", h, g)
            t = j - stage_of(use)
            act.wait_ge(x_flipped, 16 * t + 4 * h + g + 1)
            if h + g + k > 3 + 0:
                pass
            w = len(XG[g]) * P
            rows = P if g < NG - 1 else MLAST
            if not (k == 1 and h == 0 and g < 2):
                act.wait_ge(x_used, 16 * t + 4 * h + g - 1)
            copy(ps_cross[0:rows, g % 2, 0, 0:w], flip[0:rows, bank(use), 0:w]).then_inc(x_hi, 1)

        def self_hi(j, k, g):
            act.wait_ge(s_flipped, 4 * j + g + 1)
            if not (k == 0 and g < 2):
                act.wait_ge(s_used, 4 * j + g - 1)
            copy(ps_self[:, g % 2, 0, :], flip[:, bank(("s", g)), :]).then_inc(s_hi, 1)

        def body(j, k):
            a, b, c = k < T, 1 <= k <= T, k >= 2
            if c:
                cross_hi(j, k, 3, 0)
                cross_hi(j, k, 3, 1)
            if b:
                act.wait_ge(xn_flipped, j)
                copy(xt[:, 0, :, :], flip[:, bank(("xn",)), 0:D].rearrange("p (c s) -> p c s", c=C)).then_inc(xt_hi, 1)
            if c:
                cross_hi(j, k, 3, 2)
                cross_hi(j, k, 3, 3)
            if b:
                act.wait_ge(q_ready, j)
                if k >= 2:
                    act.wait_ge(q_flipped, j - 1)
                copy(qs[:, :, 0, :], flip[:, bank(("xq",)), 0:D].rearrange("p (h d) -> p h d", h=H)).then_inc(qs_hi, 1)
                act.wait_ge(q_flipped, j)
                if k >= 2:
                    act.wait_ge(xs_ready, 8 * (j - 1))
                act.activation(qt[:, :, :], flip[:, bank(("qs",)), :].rearrange("p (h s) -> p h s", h=H), ACT.Copy,
                               scale=HD ** -0.5).then_inc(qt_ready, 1)
            if a:
                act.wait_ge(self_max, j + 1)
                if k >= 1:
                    act.wait_ge(s_used, 4 * j)
                    act.wait_ge(x1_ready, j)
                act.activation(exp_self[:, :].rearrange("p (n s) -> p n s", n=NB), scores[:, :, :], ACT.Exp,
                               bias=sneg[:, 0:1], accum_out=sden[:, 0:1]).then_inc(self_exp, 1)
            if c:
                act.wait_ge(o_flipped, j - 1)
                copy(ot[:, 0, :, :], flip[:, bank(("o",)), 0:D].rearrange("p (c s) -> p c s", c=C)).then_inc(ot_hi, 1)
            for h in range(H):
                if a:
                    self_hi(j, k, h)
                if h == 0 and c:
                    act.wait_ge(x3_flipped, j - 1)
                    if k > 2:
                        act.wait_ge(gate_ready, j - 2)
                    copy(x3t[:, :, :], flip[:, bank(("x3",)), 0:D].rearrange("p (c s) -> p c s", c=C)).then_inc(x3t_ready, 1)
                if h and b:
                    cross_hi(j, k, h - 1, 0)
                    cross_hi(j, k, h - 1, 1)
                    cross_hi(j, k, h - 1, 2)
                if h and b:
                    cross_hi(j, k, h - 1, 3)
                if b:
                    act.wait_ge(xmax, 4 * (j - 1) + h + 1)
                    if h == 0 and c:
                        act.wait_ge(o_step, 2 * (j - 1))
                    act.activation(exp_cross[:, h % 2, :], exp_cross[:, h % 2, :], ACT.Exp, bias=xneg[:, h % 2, 1:2],
                                   scale=-1.0, accum_out=xden[:, h:h + 1]).then_inc(xexp, 1)
        run_pipeline(act, body)
        act.wait_ge(s_used, 4 * T)
        act.wait_ge(x_used, 16 * T)
        copy(barrier[:, 0:1], ident[:, 0:1]).then_inc(attention_done, 1)

        act.wait_ge(attention_done, 3)
        for n in range(2 * E):
            e = n % E
            act.wait_ge(w_loaded[n % 2], 16 * (n // 2 + 1))
            if n < E:
                copy(w1s[:, 0, :, e * DF:(e + 1) * DF], w_stage[:, n % 2, :].rearrange("p (c n) -> p c n", c=C)).then_inc(w_hi, 1)
            else:
                copy(w2s[:, 0, :, e * D:(e + 1) * D], w_stage[:, n % 2, :].rearrange("p (c n) -> p c n", c=FC)).then_inc(w_hi, 1)

        def blocks(b, k):
            def x_hi_f(b):
                act.wait_ge(f_x_flipped, b + 1)
                copy(xt_f[:, 0, :, :], self_out[:, 0:D].rearrange("p (c s) -> p c s", c=C)).then_inc(f_xt_hi, 1)

            def gelu(b, n):
                act.wait_ge(f_bias, 2 * b + n + 1)
                cols = slice(n * 512, (n + 1) * 512)
                act.activation(hidden[:, cols], hidden[:, cols], ACT.Gelu).then_inc(f_gelu, 1)

            if k == 0:
                x_hi_f(0)
            if k >= 1:
                for n in range(2):
                    act.wait_ge(f_h_flipped, 2 * (b - 1) + n + 1)
                    if k >= 2:
                        act.wait_ge(f_y, b - 1)
                    copy(ht[:, 0, 4 * n:4 * n + 4, :], flip[:, n, :].rearrange("p (c s) -> p c s", c=4)).then_inc(f_ht_hi, 1)
            if k < BLOCKS:
                gelu(b, 0)
            if k < BLOCKS - 1:
                x_hi_f(b + 1)
            if k < BLOCKS:
                gelu(b, 1)
        run_blocks(act, blocks)

    @block.vector
    def _(dve):
        def low(out, full, hi):
            return dve.tensor_tensor(out, full, hi, ALU.subtract)

        dve.wait_ge(s_x_in, 16)
        for t in range(T):
            dve.bn_stats(stats_pro[:, t, :], x_all[:, t, :]).then_inc(s_xstat, 1)
        dve.wait_ge(s_xstat, T)
        for t in range(T):
            dve.bn_aggr(mv_pro[:, t, :], stats_pro[:, t, :]).then_inc(s_xstat, 1)
        dve.wait_ge(s_xstat, 2 * T)
        dve.tensor_scalar(lnw[:, 0, :], mv_pro[:, :, 1], EPS, None, ALU.add).then_inc(s_lnd, 1)
        for n in range(3):
            dve.wait_ge(s_wsplit_hi, n + 1)
            low(w_self[:, n, 1, :, :], w_raw[:, n, :, :], w_self[:, n, 0, :, :].bitcast(F32)).then_inc(s_wsplit_lo, 1)
        dve.wait_ge(s_ln, 2)
        dve.scalar_tensor_tensor(out=norms[:, :], in0=lnw[:, 1, :], scalar=float(D) ** 0.5, in1=lnw[:, 2, :],
                                 op0=ALU.mult, op1=ALU.mult).then_inc(s_lnd, 1)
        dve.wait_ge(s_lnd, 2)
        dve.tensor_scalar(lnw[:, 3, :], norms[:, :], 1e-9, None, ALU.add).then_inc(s_lnd, 1)
        dve.wait_ge(s_lnd, 3)
        dve.reciprocal(lnw[:, 4, :], lnw[:, 3, :]).then_inc(s_lnd, 1)
        dve.wait_ge(s_lnd, 4)
        dve.tensor_tensor(lnw[:, 5, :], lnw[:, 4, :], lnw[:, 1, :], ALU.mult).then_inc(s_lnd, 1)
        dve.wait_ge(s_lnd, 5)
        for t in range(T):
            dve.tensor_scalar(x_all[:, t, :], x_all[:, t, :], mv_pro[:, t, 0:1], lnw[:, 5, t:t + 1],
                              ALU.subtract, ALU.mult).then_inc(s_xs, 1)
        for g in range(GROUPS):
            for c in range(C):
                dve.wait_ge(s_pthi, C * g + c + 1)
                low(xt_pro[:, 1, c, :], flip[:, c, :], xt_pro[:, 0, c, :].bitcast(F32)).then_inc(s_ptlo, 1)
            for o in range(C):
                dve.wait_ge(s_qhi, C * g + o + 1)
                cols = slice(g * 512, (g + 1) * 512)
                dve.scalar_tensor_tensor(out=keys_self[:, 1, o, cols], in0=scores[:, o, :], scalar=bq_col[:, o:o + 1],
                                         in1=keys_self[:, 0, o, cols].bitcast(F32), op0=ALU.add,
                                         op1=ALU.subtract).then_inc(s_qlo, 1)
            for n in range(4):
                dve.wait_ge(s_v, 4 * g + n - n % 2 + 2)
                if 4 * g + n >= 2:
                    dve.wait_ge(s_vhi, 4 * g + n - 1)
                    dve.wait_ge(s_vlo, 4 * g + n - 1)
                dve.tensor_tensor(v_tmp[:, n % 2, :], scores[:, 2 + n // 2, (n % 2) * D:(n % 2 + 1) * D], bv_row[:, :],
                                  ALU.add).then_inc(s_vt, 1)
                if n % 2:
                    for m in (n - 1, n):
                        dve.wait_ge(s_vhi, 4 * g + m + 1)
                        dve.wait_ge(s_vt, 4 * g + m + 1)
                        low(vals_self[:, 4 * g + m, 1, :], v_tmp[:, m % 2, :],
                            vals_self[:, 4 * g + m, 0, :].bitcast(F32)).then_inc(s_vlo, 1)
            for o in range(C):
                dve.wait_ge(s_uhi, C * g + o + 1)
                out = self_out if o == 0 else cross_out
                dve.scalar_tensor_tensor(out=u_out[:, :, C + o, :], in0=out[:, :].rearrange("p (t s) -> p t s", t=4),
                                         scalar=1.0 / 16.0, in1=u_out[:, :, o, :].bitcast(F32), op0=ALU.mult,
                                         op1=ALU.subtract).then_inc(s_ulo, 1)
        dve.wait_ge(s_vlo, 4 * GROUPS)
        dve.wait_ge(s_vhi, 4 * GROUPS)
        dve.wait_ge(s_u_st, 16 * GROUPS)
        dve.tensor_copy(barrier[:, 1:2], ident[:, 0:1]).then_inc(s_pro1, 2)

        dve.wait_ge(s_pro1, 3)
        dve.memset(ctx_t[:, :, :, M:MP].bitcast(F32), 0.0).then_inc(s_vsc, 1)
        for dup in range(2):
            dve.wait_ge(s_w2hi, dup + 1)
            for c in range(C):
                op = low(wk_dup[:, 1, c, :, dup, :], w2_raw[:, 0, c, :].rearrange("p (h d) -> p h d", h=H),
                         wk_dup[:, 0, c, :, dup, :].bitcast(F32))
            if dup:
                op.then_inc(s_w2lo, 1)
        for n, w in ((1, wv_cross), (2, wq_cross), (3, wo_cross)):
            dve.wait_ge(s_w2hi, 2 + n)
            low(w[:, 1, :, :], w2_raw[:, n, :, :], w[:, 0, :, :].bitcast(F32)).then_inc(s_w2lo, 1)
        for g in range(4):
            dve.wait_ge(s_ctxhi, g + 1)
            cols = slice(g * KB, min((g + 1) * KB, M))
            low(ctx_t[:, 1, :, cols], ctx_raw[:, :, 0:min(KB, M - g * KB)], ctx_t[:, 0, :, cols].bitcast(F32)).then_inc(s_ctxlo, 1)
        for g in range(4):
            for h in range(H):
                dve.wait_ge(s_khi, H * g + h + 1)
                cols = slice(g * KB, (g + 1) * KB)
                low(keys_cross[:, 1, h, cols], scores[:, h, 0:KB], keys_cross[:, 0, h, cols].bitcast(F32)).then_inc(s_klo, 1)
        dve.wait_ge(s_vxf, MC)
        dve.tensor_reduce(v_max[:, 0:1], v_f32[:, :, :], AX.XY, ALU.max, apply_absolute_value=True).then_inc(s_vmax, 1)
        dve.wait_ge(s_vall, 2)
        dve.tensor_scalar(v_max[:, 2:3], v_max[:, 1:2], 1e-30, 1.0 / V_TOP, ALU.max, ALU.mult).then_inc(s_vsc, 1)
        dve.wait_ge(s_vsc, 2)
        dve.tensor_copy(v_scale[:, 1:2], v_max[:, 2:3]).then_inc(s_vsc, 1)
        dve.reciprocal(v_scale[:, 0:1], v_max[:, 2:3]).then_inc(s_vsc, 1)
        for m in range(MC):
            dve.wait_ge(s_vxhi, m + 1)
            dve.wait_ge(s_vsc, 4)
            dve.scalar_tensor_tensor(out=vals_cross[:, m, :, 1, :], in0=v_f32[:, m, :].rearrange("p (h d) -> p h d", h=H),
                                     scalar=v_scale[:, 0:1], in1=vals_cross[:, m, :, 0, :], op0=ALU.mult,
                                     op1=ALU.subtract).then_inc(s_vxlo, 1)
        dve.wait_ge(s_vxlo, MC)
        dve.tensor_copy(barrier[:, 3:4], ident[:, 0:1]).then_inc(s_pro1, 2)
        dve.wait_ge(s_pro1, 6)

        def cross_lo(j, k, h, g):
            use = ("x", h, g)
            t = j - stage_of(use)
            w = len(XG[g]) * P
            rows = P if g < NG - 1 else MLAST
            dve.wait_ge(x_hi, 16 * t + 4 * h + g + 1)
            low(ps_cross[0:rows, g % 2, 1, 0:w], flip[0:rows, bank(use), 0:w], ps_cross[0:rows, g % 2, 0, 0:w]).then_inc(x_lo, 1)

        def self_lo(j, k, g):
            dve.wait_ge(s_hi, 4 * j + g + 1)
            low(ps_self[:, g % 2, 1, :], flip[:, bank(("s", g)), :], ps_self[:, g % 2, 0, :].bitcast(F32)).then_inc(s_lo, 1)

        def part_max(j, k, n):
            dve.wait_ge(scores_ready, 4 * j + n + 1)
            dve.tensor_reduce(smax[:, n:n + 1], scores[:, n, :], AX.X, ALU.max).then_inc(max_part, 1)

        def cross_max(j, k, h, half):
            dve.wait_ge(xs_ready, 8 * (j - 1) + 2 * h + half + 1)
            if half == 0:
                if h == 0:
                    dve.wait_ge(bias_ready, j)
                if h >= 2 or k >= 2:
                    dve.wait_ge(x_flipped, 16 * (j - 1) + 4 * (h - 1))
            else:
                dve.wait_ge(xmax_a, 4 * (j - 1) + h + 1)
            cols = slice(2 * half * KB, 2 * (half + 1) * KB)
            dve.tensor_tensor_reduce(exp_cross[:, h % 2, cols].rearrange("p (n s) -> p n s", n=2),
                                     scores[:, 2 * half:2 * half + 2, 0:KB],
                                     mask_bias[:, cols].rearrange("p (n s) -> p n s", n=2), -1.0,
                                     xneg[:, h % 2, 0:1] if half else MAX_CAP, ALU.add, ALU.min,
                                     xneg[:, h % 2, half:half + 1]).then_inc(xmax if half else xmax_a, 1)

        def body(j, k):
            a, b, c = k < T, 1 <= k <= T, k >= 2
            if b:
                dve.wait_ge(self_exp, j)
                dve.reciprocal(scoef[:, 0:1], sden[:, 0:1]).then_inc(coef_step, 1)
                dve.wait_ge(coef_step, 2 * j - 1)
                dve.wait_ge(norm_ready, j)
                dve.tensor_tensor(scoef[:, 1:2], scoef[:, 0:1], norm_col[:, :], ALU.mult).then_inc(coef_step, 1)
                dve.wait_ge(coef_step, 2 * j)
                dve.wait_ge(s_used, 4 * j)
                dve.wait_ge(x_loaded, 16 * j)
                if k >= 2:
                    dve.wait_ge(x1_copied, j - 1)
                dve.scalar_tensor_tensor(out=x1[:, :], in0=self_out[:, 0:D], scalar=scoef[:, 1:2], in1=x_tile[:, :],
                                         op0=ALU.mult, op1=ALU.add).then_inc(x1_ready, 1)
                dve.wait_ge(x1_ready, j)
                dve.bn_stats(bs1[:, :], x1[:, :]).then_inc(stats1, 1)
            if c:
                cross_lo(j, k, 3, 0)
            if b:
                dve.wait_ge(stats1, 2 * j - 1)
                dve.bn_aggr(mv1[:, :], bs1[:, :]).then_inc(mean1, 1)
                dve.wait_ge(mean1, j)
                dve.tensor_scalar(rs1[:, 0:1], mv1[:, 1:2], EPS, None, ALU.add).then_inc(stats1, 1)
            if a:
                part_max(j, k, 0)
            if c:
                cross_lo(j, k, 3, 1)
            if b:
                dve.wait_ge(rstd1, j)
                dve.tensor_scalar(xn[:, :], x1[:, :], mv1[:, 0:1], rs1[:, 1:2], ALU.subtract, ALU.mult).then_inc(xn_ready, 1)
            if a:
                part_max(j, k, 1)
            if b:
                dve.wait_ge(xt_hi, j)
                low(xt[:, 1, :, :], flip[:, bank(("xn",)), 0:D].rearrange("p (c s) -> p c s", c=C),
                    xt[:, 0, :, :].bitcast(F32)).then_inc(xt_lo, 1)
            if c:
                cross_lo(j, k, 3, 2)
                cross_lo(j, k, 3, 3)
            if b:
                dve.wait_ge(qs_hi, j)
                low(qs[:, :, 1, :], flip[:, bank(("xq",)), 0:D].rearrange("p (h d) -> p h d", h=H),
                    qs[:, :, 0, :].bitcast(F32)).then_inc(qs_lo, 1)
            if a:
                part_max(j, k, 2)
            if c:
                dve.wait_ge(x_used, 16 * (j - 1))
                dve.tensor_reduce(o_sum[:, :, :], cross_out[:, :].rearrange("p (h two d) -> p h d two", h=H, two=2),
                                  AX.X, ALU.add).then_inc(o_summed, 1)
                dve.wait_ge(xexp, 4 * (j - 1))
                dve.reciprocal(xcoef[:, 0, :], xden[:, :]).then_inc(o_step, 1)
                dve.wait_ge(o_step, 2 * (j - 1) - 1)
                dve.tensor_scalar(xcoef[:, 1, :], xcoef[:, 0, :], v_scale[:, 1:2], None, ALU.mult).then_inc(o_step, 1)
                dve.wait_ge(o_step, 2 * (j - 1))
                dve.wait_ge(o_summed, j - 1)
                dve.tensor_tensor(o_tile[:, :].rearrange("p (h d) -> p h d", h=H), o_sum[:, :, :],
                                  xcoef[:, 1, :].unsqueeze(2).broadcast_to([P, H, HD]), ALU.mult).then_inc(o_ready, 1)
            if a:
                part_max(j, k, 3)
                dve.wait_ge(max_part, 4 * j + 4)
                dve.tensor_reduce(sneg[:, 0:1], smax[:, :], AX.X, ALU.max, negate=True).then_inc(self_max, 1)
            if c:
                dve.wait_ge(ot_hi, j - 1)
                low(ot[:, 1, :, :], flip[:, bank(("o",)), 0:D].rearrange("p (c s) -> p c s", c=C),
                    ot[:, 0, :, :].bitcast(F32)).then_inc(ot_lo, 1)
                dve.wait_ge(wo_ready, j - 1)
                dve.wait_ge(x1_copied, j - 1)
                if k > 2:
                    dve.wait_ge(routed, 16 * (j - 2))
                dve.tensor_tensor(record[:, 0:D], flip[:, bank(("wo",)), 0:D], x1_old[:, :], ALU.add).then_inc(x2_ready, 1)
                dve.wait_ge(x2_ready, j - 1)
                dve.bn_stats(bs3[:, :], record[:, 0:D]).then_inc(stats3, 1)
                dve.wait_ge(stats3, 2 * (j - 1) - 1)
                dve.bn_aggr(mv3[:, :], bs3[:, :]).then_inc(mean3, 1)
                dve.wait_ge(mean3, j - 1)
                dve.tensor_scalar(rs3[:, 0:1], mv3[:, 1:2], EPS, None, ALU.add).then_inc(stats3, 1)
            for h in range(H):
                if a:
                    self_lo(j, k, h)
                if b:
                    cross_max(j, k, h, 0)
                if h == 0 and c:
                    dve.wait_ge(rstd3, j - 1)
                    dve.tensor_scalar(xn3[:, :], record[:, 0:D], mv3[:, 0:1], rs3[:, 1:2], ALU.subtract,
                                      ALU.mult).then_inc(xn3_ready, 1)
                if b:
                    cross_max(j, k, h, 1)
                if h and b:
                    cross_lo(j, k, h - 1, 0)
                    cross_lo(j, k, h - 1, 1)
                    cross_lo(j, k, h - 1, 2)
                    cross_lo(j, k, h - 1, 3)
                if h == 1 and c:
                    gates(j, k)
                if h == 2 and c:
                    ranks(j, k)

        def gates(j, k):
            g = [0]

            def step(op):
                g[0] += 1
                op.then_inc(gate_step, 1)
                dve.wait_ge(gate_step, 6 * (j - 2) + g[0])

            dve.wait_ge(gate_ready, j - 1)
            dve.tensor_tensor(logits[:, :], flip[:, bank(("gate",)), 0:E], bg_row[:, :], ALU.add).then_inc(logits_ready, 1)
            dve.wait_ge(logits_ready, j - 1)
            step(dve.tensor_reduce(gsc[:, 0, 0:1], logits[:, :], AX.X, ALU.max))
            step(dve.scalar_tensor_tensor(out=gsc[:, 1, :], in0=logits[:, :], scalar=gsc[:, 0, 0:1], in1=expert_w[:, :],
                                          op0=ALU.is_equal, op1=ALU.mult))
            step(dve.tensor_reduce(gsc[:, 2, 0:1], gsc[:, 1, :], AX.X, ALU.max))
            step(dve.tensor_scalar(gsc[:, 3, 0:1], gsc[:, 2, 0:1], 0.0, float(E), ALU.is_equal, ALU.mult))
            step(dve.tensor_tensor(gsc[:, 4, 0:1], gsc[:, 3, 0:1], gsc[:, 2, 0:1], ALU.add))
            step(dve.tensor_scalar(onehot[:, :], expert_w[:, :], gsc[:, 4, 0:1], None, ALU.is_equal))
            if k > 2:
                dve.wait_ge(rank_ready, j - 2)
            dve.tensor_copy(onehot16[:, :], onehot[:, :]).then_inc(onehot_ready, 1)

        def ranks(j, k):
            dve.wait_ge(rank_ready, j - 1)
            dve.tensor_tensor(rank_e[:, :], flip[:, bank(("rank",)), 0:E], seen[:, :], ALU.add).then_inc(rank_added, 1)
            dve.wait_ge(rank_added, j - 1)
            dve.tensor_tensor(seen[:, :], flip[:, bank(("rank",)), E:2 * E], seen[:, :], ALU.add).then_inc(rank_used, 1)
            dve.tensor_tensor_reduce(gsc[:, 5, :], rank_e[:, :], onehot[:, :], 1.0, 0.0, ALU.mult, ALU.add,
                                     dest[:, 0:1]).then_inc(dest_step, 1)
            dve.wait_ge(dest_step, j - 1)
            if k > 2:
                dve.wait_ge(routed, 16 * (j - 2))
            dve.tensor_copy(dest_i[:, :], dest[:, :]).then_inc(dest_ready, 1)

        run_pipeline(dve, body)

        dve.wait_ge(s_pads, 4)
        dve.wait_ge(rank_used, T)
        dve.tensor_scalar(pad_f[:, 0:E], seen[:, :], lane[:, 0:1], None, ALU.add).then_inc(pad_dest, 1)
        dve.wait_ge(pad_dest, 1)
        dve.tensor_copy(pad_i[:, 0:E], pad_f[:, 0:E]).then_inc(pad_dest_i, 1)
        dve.wait_ge(pad_dest_i, 1)
        dve.wait_ge(pads_out, 16 * E)
        dve.tensor_copy(barrier[:, 1:2], ident[:, 0:1]).then_inc(attention_done, 2)
        dve.wait_ge(attention_done, 3)
        steps = [0]

        def step(op):
            steps[0] += 1
            op.then_inc(table_step, 1)
            dve.wait_ge(table_step, steps[0])

        step(dve.tensor_tensor(count[:, :], seen[:, :], region_base[:, :], ALU.subtract))
        step(dve.tensor_tensor(over[:, :, :], count[:, :].unsqueeze(2).broadcast_to([P, E, T]), sixteenth[:, :, :], ALU.is_gt))
        step(dve.tensor_reduce(need[:, :], over[:, :, :], AX.X, ALU.add))
        step(dve.tensor_copy(ends[:, 0:1], need[:, 0:1]))
        for e in range(1, E):
            step(dve.tensor_tensor(ends[:, e:e + 1], ends[:, e - 1:e], need[:, e:e + 1], ALU.add))
        step(dve.tensor_tensor(past[:, :, :], block_no[:, 0, :].unsqueeze(2).broadcast_to([P, BLOCKS, E]),
                               ends[:, :].unsqueeze(1).broadcast_to([P, BLOCKS, E]), ALU.is_ge))
        step(dve.tensor_reduce(tab[:, 0, :], past[:, :, :], AX.X, ALU.add))
        step(dve.tensor_tensor(past_n[:, :, :], past[:, :, :], need[:, :].unsqueeze(1).broadcast_to([P, BLOCKS, E]), ALU.mult))
        step(dve.tensor_reduce(tab[:, 1, :], past_n[:, :, :], AX.X, ALU.add))
        step(dve.scalar_tensor_tensor(out=tab[:, 2, :], in0=tab[:, 0, :], scalar=float(REGION), in1=block_no[:, 1, :],
                                      op0=ALU.mult, op1=ALU.add))
        step(dve.scalar_tensor_tensor(out=tab[:, 3, :], in0=tab[:, 1, :], scalar=-float(P), in1=tab[:, 2, :],
                                      op0=ALU.mult, op1=ALU.add))
        dve.tensor_copy(table[:, 0, :], tab[:, 3, :]).then_inc(table_ready, 1)
        step(dve.tensor_scalar(tab[:, 4, :], tab[:, 0, :], float(E - 1), float(DF), ALU.min, ALU.mult))
        dve.tensor_copy(table[:, 1, :], tab[:, 4, :]).then_inc(table_ready, 1)
        dve.wait_ge(table_ready, 2)
        step(dve.tensor_scalar(tab[:, 4, :], tab[:, 0, :], float(E - 1), float(D), ALU.min, ALU.mult))
        dve.tensor_copy(table[:, 2, :], tab[:, 4, :]).then_inc(table_ready, 1)
        dve.wait_ge(table_ready, 3)

        def split_lo(n):
            e = n % E
            dve.wait_ge(w_hi, n + 1)
            if n < E:
                w, cols, ch = w1s, slice(e * DF, (e + 1) * DF), C
            else:
                w, cols, ch = w2s, slice(e * D, (e + 1) * D), FC
            low(w[:, 1, :, cols], w_stage[:, n % 2, :].rearrange("p (c n) -> p c n", c=ch),
                w[:, 0, :, cols].bitcast(F32)).then_inc(w_lo, 1)
        for n in range(2 * E):
            split_lo(n)
        dve.wait_ge(b_loaded, 32)

        def statistics(b, k):
            dve.wait_ge(rows_loaded, 16 * (b + 1))
            if k >= 1:
                dve.wait_ge(f_mean, b)
            dve.bn_stats(bs_f[:, :], rows[:, k % RING, 0:D]).then_inc(f_stats, 1)
            dve.wait_ge(f_stats, b + 1)
            if k >= 1:
                dve.wait_ge(f_xn, b)
            dve.bn_aggr(mv_f[:, :], bs_f[:, :]).then_inc(f_mean, 1)
            dve.wait_ge(f_mean, b + 1)
            if k >= 1:
                dve.wait_ge(f_rstd, b)
            dve.tensor_scalar(rs_f[:, 0:1], mv_f[:, 1:2], EPS, None, ALU.add).then_inc(f_eps, 1)

        def normalise(b, k):
            dve.wait_ge(f_rstd, b + 1)
            if k >= 1:
                dve.wait_ge(f_x_flipped, b)
            dve.tensor_scalar(xn_f[:, :], rows[:, k % RING, 0:D], mv_f[:, 0:1], rs_f[:, 1:2], ALU.subtract,
                              ALU.mult).then_inc(f_xn, 1)

        def blocks(b, k):
            def x_lo_f(b):
                dve.wait_ge(f_xt_hi, b + 1)
                low(xt_f[:, 1, :, :], self_out[:, 0:D].rearrange("p (c s) -> p c s", c=C),
                    xt_f[:, 0, :, :].bitcast(F32)).then_inc(f_xt_lo, 1)

            if k == 0:
                statistics(0, 0)
                normalise(0, 0)
                x_lo_f(0)
                statistics(b + 1, 1)
                normalise(b + 1, 1)
            if k >= 1:
                for n in range(2):
                    dve.wait_ge(f_ht_hi, 2 * (b - 1) + n + 1)
                    low(ht[:, 1, 4 * n:4 * n + 4, :], flip[:, n, :].rearrange("p (c s) -> p c s", c=4),
                        ht[:, 0, 4 * n:4 * n + 4, :].bitcast(F32)).then_inc(f_ht_lo, 1)
            if k < BLOCKS - 2:
                statistics(b + 2, k + 2)
            if k < BLOCKS:
                off = dve.value_load(table[0:1, 1, bass.ds(b, 1)], min_val=0, max_val=(E - 1) * DF)
                for n in range(2):
                    if k >= 1:
                        dve.wait_ge(f_h_flipped, 2 * (b - 1) + n + 1)
                    dve.wait_ge(f_h, 2 * b + n + 1)
                    dve.tensor_tensor(hidden[:, n * 512:(n + 1) * 512], scores[:, n, :],
                                      b1_row[:, bass.ds(off + n * 512, 512)], ALU.add).then_inc(f_bias, 1)
            if k < BLOCKS - 1:
                x_lo_f(b + 1)
            if k < BLOCKS - 2:
                normalise(b + 2, k + 2)
            if k >= 1:
                off2 = dve.value_load(table[0:1, 2, bass.ds(b - 1, 1)], min_val=0, max_val=(E - 1) * D)
                if k >= 2:
                    dve.wait_ge(f_out, b - 1)
                dve.tensor_tensor(base_f[:, :], rows[:, (k - 1) % RING, 0:D], b2_row[:, bass.ds(off2, D)],
                                  ALU.add).then_inc(f_base, 1)
                dve.wait_ge(f_base, b)
                dve.wait_ge(f_y, b)
                if k >= 3:
                    dve.wait_ge(f_stored, 16 * (b - 2))
                dve.tensor_tensor(out_f[:, (k - 1) % 2, :], cross_out[:, 0:D], base_f[:, :], ALU.add).then_inc(f_out, 1)
        run_blocks(dve, blocks)


def kernel(**inputs):
    import numpy as _np
    import concourse.bacc as _bacc
    from concourse import mybir as _mybir
    from concourse.bass_utils import run_bass_kernel_spmd as _run

    def array(name):
        return _np.asarray(inputs[name])

    laid_out = {
        "x": array("x")[0],
        "ctxT": array("ctx_1024")[0].T,
        "mask": array("mask_BxSxS2_bf1")[0].view(_np.uint8),
        "WqT": array("L0_attn_Wq").T,
        "AT": array("L0_attn_anomaly_matrix").T,
        "WvT": array("L0_attn_Wv").T,
        "bq": array("L0_attn_bq"),
        "bv": array("L0_attn_bv"),
        "xWq": array("L0_xattn_Wq"),
        "Wkv": array("L0_xattn_Wkv"),
        "Wo": array("L0_xattn_Wo"),
        "Wg": array("L0_ffn_Wg"),
        "bg": array("L0_ffn_bg"),
        "W1": array("L0_ffn_W1"),
        "b1": array("L0_ffn_b1"),
        "W2": array("L0_ffn_W2"),
        "b2": array("L0_ffn_b2"),
    }
    nc = _bacc.Bacc("TRN2", target_bir_lowering=False, num_devices=1)
    arrays, io = {}, {}
    for name, a in laid_out.items():
        arrays[name] = _np.ascontiguousarray(a)
        io[name] = nc.dram_tensor(name, arrays[name].shape, _mybir.dt.from_np(arrays[name].dtype), kind="ExternalInput").ap()
    io["out"] = nc.dram_tensor("out", (N, D), F32, kind="ExternalOutput").ap()
    build(nc, io)
    r = _run(nc, [arrays], core_ids=[0])
    return r.results[0]["out"].reshape(1, N, D)
```

```python
from contextlib import ExitStack

import numpy as np

import concourse.bass as bass
from concourse import mybir

ALU = mybir.AluOpType
ACT = mybir.ActivationFunctionType
AX = mybir.AxisListType
F32 = mybir.dt.float32
F32R = mybir.dt.float32r
F16 = mybir.dt.float16
BF16 = mybir.dt.bfloat16
U8 = mybir.dt.uint8
I32 = mybir.dt.int32
U32 = mybir.dt.uint32

P = 128
N = 2048
D = 256
C = D // P
T = N // P
M = 1601
H = 4
HD = D // H
KB = 402
MP = 4 * KB
MC = -(-M // P)
MLAST = M - (MC - 1) * P
NB = N // 512
E = 4
DF = 1024
FC = DF // P
EPS = 1e-5
PAD_BIAS = -3.38e38
MAX_CAP = 3.0e38
MASKED = 3.4e38
REGION = N + P
SPARE = E * REGION
REC = D + 4
BLOCKS = T + E - 1
XROWS = SPARE + E * P
V_TOP = 4096.0
XHALF = 2 * 512
RING = 4
NOBODY = 65536.0


LOOP = False
DBG = False


def split_groups(h):
    return [range(g, min(g + 4, MC)) for g in range(0, MC, 4)]


XG = split_groups(0)
NG = len(XG)

BANKS = {("x", 2, 2): 0, ("x", 2, 3): 1, ("xn",): 2, ("x", 3, 0): 0, ("xq",): 2, ("qs",): 2,
         ("x", 3, 1): 1, ("x", 3, 2): 2, ("s", 0): 0, ("x", 3, 3): 1, ("s", 1): 2, ("s", 2): 0,
         ("sum",): 2, ("s", 3): 0, ("o",): 1, ("x", 0, 0): 0, ("wo",): 1, ("x", 0, 1): 1,
         ("x", 0, 2): 0, ("x", 0, 3): 2, ("x", 1, 0): 1, ("x", 1, 1): 0, ("x3",): 2, ("x", 1, 2): 1,
         ("gate",): 2, ("x", 1, 3): 0, ("x", 2, 0): 1, ("x", 2, 1): 2, ("rank",): 0}
USES = list(BANKS)


def stage_of(use):
    if use[0] in ("s", "sum"):
        return 0
    if use[0] in ("xn", "xq", "qs") or (use[0] == "x" and (use[1] < 2 or use[1:] in ((2, 0), (2, 1)))):
        return 1
    return 2


def active(use, j):
    return 0 <= j - stage_of(use) < T


def previous_use(use, j):
    k = USES.index(use)
    for back in range(3):
        order = USES[:k] if back == 0 else USES
        for at in range(len(order) - 1, -1, -1):
            if BANKS[USES[at]] == BANKS[use] and active(USES[at], j - back):
                return USES[at], back
    return None, 0


def build(nc, io):
    with ExitStack() as ctx:
        emit(nc, io, ctx)


def emit(nc, io, ctx):
    def sb(name, shape, dt, on=None):
        return (on or ctx).enter_context(nc.sbuf_tensor(name, shape, dt))

    def sem(name):
        return ctx.enter_context(nc.semaphore(name))

    u_dram = nc.dram_tensor("u_dram", [T, P, 2 * C, P], F32, kind="Internal").ap()
    rows_dram = nc.dram_tensor("rows_dram", [XROWS, REC], F32, kind="Internal").ap()

    scores = ctx.enter_context(nc.psum_tensor("scores", [P, 4, 512], F32))
    flip = ctx.enter_context(nc.psum_tensor("flip", [P, 3, 512], F32))
    self_out = flip[:, 2, :]
    cross_out = ctx.enter_context(nc.psum_tensor("cross_out", [P, 512], F32))

    ident = sb("ident", [P, P], F32)
    barrier = sb("barrier", [P, 4], F32)
    below = sb("below", [P, P], BF16)
    ones = sb("ones", [P, P], BF16)
    minus_half = sb("minus_half", [P, T], F32)
    plus_half = sb("plus_half", [P, T], F32)
    token = sb("token", [P, 1], F32)
    expert_w = sb("expert_w", [P, E], F32)
    seen = sb("seen", [P, E], F32)
    norms = sb("norms", [P, T], F32)
    v_scale = sb("v_scale", [P, 2], F32)
    bg_row = sb("bg_row", [P, E], F32)
    wg = sb("wg", [P, C, E], F32)
    wq_cross = sb("wq_cross", [P, 2, C, D], F32R)
    wo_cross = sb("wo_cross", [P, 2, C, D], F32R)
    region_base = sb("region_base", [P, E], F32)
    lane = sb("lane", [P, 1], F32)
    sixteenth = sb("sixteenth", [P, T], F32)
    block_no = sb("block_no", [P, 2, BLOCKS], F32)

    count = sb("count", [P, E], F32)
    over = sb("over", [P, E, T], F32)
    pad_f = sb("pad_f", [P, 2, E], F32)
    pad_i = sb("pad_i", [P, 2, E], U32)
    need = sb("need", [P, E], F32)
    ends = sb("ends", [P, E], F32)
    past = sb("past", [P, BLOCKS, E], F32)
    tab = sb("tab", [P, 5, BLOCKS], F32)
    table = sb("table", [P, 3, BLOCKS], I32)

    ffn = ExitStack()
    w1s = sb("w1s", [P, 2, C, E * DF], F32R, ffn)
    w2s = sb("w2s", [P, 2, FC, E * D], F32R, ffn)
    w_stage = sb("w_stage", [P, 2, C * DF], F32, ffn)
    b1_row = sb("b1_row", [P, E * DF], F32, ffn)
    b2_row = sb("b2_row", [P, E * D], F32, ffn)
    rows = sb("rows", [P, RING, REC], F32, ffn)
    xn_f = sb("xn_f", [P, D], F32, ffn)
    xt_f = sb("xt_f", [P, 2, C, P], F32R, ffn)
    hidden = sb("hidden", [P, DF], F32, ffn)
    ht = sb("ht", [P, 2, FC, P], F32R, ffn)
    base_f = sb("base_f", [P, D], F32, ffn)
    out_f = sb("out_f", [P, 2, D], F32, ffn)
    who = sb("who", [P, RING, 1], U32, ffn)
    bs_f = sb("bs_f", [P, 6], F32, ffn)
    mv_f = sb("mv_f", [P, 2], F32, ffn)
    rs_f = sb("rs_f", [P, 2], F32, ffn)
    ffn.close()

    keep = ctx.enter_context(ExitStack())
    keys_self = sb("keys_self", [P, 2, C, N], F32R, keep)
    vals_self = sb("vals_self", [P, T, 2, D], F32R, keep)

    s_const = sem("s_const")
    s_wload = [sem(f"s_wload{i}") for i in range(8)]
    s_x_in = [sem(f"s_x_in{g}") for g in range(4)]
    s_bias_in = sem("s_bias_in")

    pro = ExitStack()
    w_raw = sb("w_raw", [P, 3, C, D], F32, pro)
    w_self = sb("w_self", [P, 3, 2, C, D], F32R, pro)
    x_all = sb("x_all", [P, T, D], F32, pro)
    xt_pro = sb("xt_pro", [P, 2, C, 512], F32R, pro)
    u_out = sb("u_out", [P, 4, 2 * C, P], F32R, pro)
    v_tmp = sb("v_tmp", [P, 2, D], F32, pro)
    stats_pro = sb("stats_pro", [P, T, 6], F32, pro)
    mv_pro = sb("mv_pro", [P, T, 2], F32, pro)
    var_eps = sb("var_eps", [P, T], F32, pro)
    rstd_pro = sb("rstd_pro", [P, T], F32, pro)
    std_pro = sb("std_pro", [P, T], F32, pro)
    norm_eps = sb("norm_eps", [P, T], F32, pro)
    norm_inv = sb("norm_inv", [P, T], F32, pro)
    row_scale = sb("row_scale", [P, T], F32, pro)
    bq_col = sb("bq_col", [P, C], F32, pro)
    bv_row = sb("bv_row", [P, D], F32, pro)
    pro.close()
    keys_cross = sb("keys_cross", [P, 2, H, MP], F32R, keep)
    vals_cross = sb("vals_cross", [P, MC, H, 2, HD], F16, keep)

    pro2 = ExitStack()
    w2_raw = sb("w2_raw", [P, 4, C, D], F32, pro2)
    wk_dup = sb("wk_dup", [P, 2, C, H, 2, HD], F32R, pro2)
    wv_cross = sb("wv_cross", [P, 2, C, D], F32R, pro2)
    ctx_raw = sb("ctx_raw", [P, C, KB], F32, pro2)
    ctx_t = sb("ctx_t", [P, 2, C, MP], F32R, pro2)
    v_f32 = sb("v_f32", [P, MC, D], F32, pro2)
    v_max = sb("v_max", [P, 2, 4], F32, pro2)
    v_top = sb("v_top", [P, 2], F32, pro2)
    pro2.close()

    loop = ExitStack()
    u_tile = sb("u_tile", [P, 2 * C, P], F32R, loop)
    x_tile = sb("x_tile", [P, D], F32, loop)
    exp_self = sb("exp_self", [P, N], F32, loop)
    ps_self = sb("ps_self", [P, 4, 2, 512], F32R, loop)
    mask_tile = sb("mask_tile", [P, M], U8, loop)
    mask_bias = sb("mask_bias", [P, MP], BF16, loop)
    exp_cross = sb("exp_cross", [P, 2, MP], F32, loop)
    ps_cross = sb("ps_cross", [P, 4, 2, 512], F16, loop)
    x1 = sb("x1", [P, D], F32, loop)
    x1_old = sb("x1_old", [P, D], F32, loop)
    xn = sb("xn", [P, D], F32, loop)
    xt = sb("xt", [P, 2, C, P], F32R, loop)
    qs = sb("qs", [P, H, 2, HD], F32R, loop)
    qt = sb("qt", [P, H, P], F32R, loop)
    o_tile = sb("o_tile", [P, H, HD], F32, loop)
    ot = sb("ot", [P, 2, C, P], F32R, loop)
    xn3 = sb("xn3", [P, D], F32, loop)
    x3t = sb("x3t", [P, C, P], F32, loop)
    bs1 = sb("bs1", [P, 6], F32, loop)
    mv1 = sb("mv1", [P, 2], F32, loop)
    rs1 = sb("rs1", [P, 2], F32, loop)
    bs3 = sb("bs3", [P, 6], F32, loop)
    mv3 = sb("mv3", [P, 2], F32, loop)
    rs3 = sb("rs3", [P, 2], F32, loop)
    norm_col = sb("norm_col", [P, 1], F32, loop)
    smax = sb("smax", [P, NB], F32, loop)
    sneg = sb("sneg", [P, 1], F32, loop)
    sden = sb("sden", [P, 2], F32, loop)
    ssum = sb("ssum", [P, 1], F32, loop)
    scoef = sb("scoef", [P, 2], F32, loop)
    xneg = sb("xneg", [P, 2, 2], F32, loop)
    xden = sb("xden", [P, 2, H], F32, loop)
    xcoef = sb("xcoef", [P, 3, H], F32, loop)
    logits = sb("logits", [P, E], F32, loop)
    gsc = sb("gsc", [P, 6, E], F32, loop)
    onehot = sb("onehot", [P, E], F32, loop)
    onehot16 = sb("onehot16", [P, E], BF16, loop)
    rank_e = sb("rank_e", [P, E], F32, loop)
    record = sb("record", [P, REC], F32, loop)
    pads = sb("pads", [P, REC], F32, loop)
    dest = sb("dest", [P, 1], F32, loop)
    dest_i = sb("dest_i", [P, 1], U32, loop)
    loop.close()

    s_w0 = sem("s_w0")
    s_xstat = sem("s_xstat")
    s_ln = sem("s_ln")
    s_lnd = sem("s_lnd")
    s_xs = sem("s_xs")
    s_wsplit_hi = sem("s_wsplit_hi")
    s_wsplit_lo = sem("s_wsplit_lo")
    s_ptf = sem("s_ptf")
    s_pthi = sem("s_pthi")
    s_ptlo = sem("s_ptlo")
    s_q = sem("s_q")
    s_qhi = sem("s_qhi")
    s_qlo = sem("s_qlo")
    s_u = sem("s_u")
    s_uhi = sem("s_uhi")
    s_ulo = sem("s_ulo")
    s_u_st = sem("s_u_st")
    s_v = sem("s_v")
    s_vt = sem("s_vt")
    s_vhi = sem("s_vhi")
    s_vlo = sem("s_vlo")
    s_pro1 = sem("s_pro1")
    s_w2 = sem("s_w2")
    s_w2hi = sem("s_w2hi")
    s_w2lo = sem("s_w2lo")
    s_ctx = sem("s_ctx")
    s_ctxhi = sem("s_ctxhi")
    s_ctxlo = sem("s_ctxlo")
    s_k = sem("s_k")
    s_khi = sem("s_khi")
    s_klo = sem("s_klo")
    s_vx = sem("s_vx")
    s_vxf = sem("s_vxf")
    s_vmax = sem("s_vmax")
    s_vtop = sem("s_vtop")
    s_norm = sem("s_norm")
    s_vall = sem("s_vall")
    s_vsc = sem("s_vsc")
    s_vxhi = sem("s_vxhi")
    s_vxlo = sem("s_vxlo")

    u_loaded = sem("u_loaded")
    x_loaded = sem("x_loaded")
    mask_loaded = sem("mask_loaded")
    scores_ready = sem("scores_ready")
    max_part = sem("max_part")
    self_max = sem("self_max")
    self_exp = sem("self_exp")
    sum_ready = sem("sum_ready")
    s_flipped = sem("s_flipped")
    s_hi = sem("s_hi")
    s_lo = sem("s_lo")
    s_used = sem("s_used")
    norm_ready = sem("norm_ready")
    coef_step = sem("coef_step")
    x1_ready = sem("x1_ready")
    stats1 = sem("stats1")
    rstd1 = sem("rstd1")
    xn_ready = sem("xn_ready")
    xn_flipped = sem("xn_flipped")
    xt_hi = sem("xt_hi")
    xt_lo = sem("xt_lo")
    q_ready = sem("q_ready")
    qs_hi = sem("qs_hi")
    qs_lo = sem("qs_lo")
    q_flipped = sem("q_flipped")
    qt_ready = sem("qt_ready")
    bias_ready = sem("bias_ready")
    xs_ready = sem("xs_ready")
    xmax_a = sem("xmax_a")
    xmax = sem("xmax")
    xexp = sem("xexp")
    x_flipped = sem("x_flipped")
    x_hi = sem("x_hi")
    x_lo = sem("x_lo")
    x_used = sem("x_used")
    o_summed = sem("o_summed")
    o_step = sem("o_step")
    o_ready = sem("o_ready")
    o_flipped = sem("o_flipped")
    ot_hi = sem("ot_hi")
    ot_lo = sem("ot_lo")
    wo_ready = sem("wo_ready")
    x2_ready = sem("x2_ready")
    x1_copied = sem("x1_copied")
    record_filled = sem("record_filled")
    stats3 = sem("stats3")
    mean1 = sem("mean1")
    mean3 = sem("mean3")
    rstd3 = sem("rstd3")
    xn3_ready = sem("xn3_ready")
    x3_flipped = sem("x3_flipped")
    x3t_ready = sem("x3t_ready")
    gate_ready = sem("gate_ready")
    logits_ready = sem("logits_ready")
    gate_step = sem("gate_step")
    onehot_ready = sem("onehot_ready")
    rank_ready = sem("rank_ready")
    rank_added = sem("rank_added")
    rank_used = sem("rank_used")
    dest_step = sem("dest_step")
    dest_ready = sem("dest_ready")
    token_set = sem("token_set")
    token_next = sem("token_next")
    routed = sem("routed")
    s_pads = sem("s_pads")
    s_pad_ok = sem("s_pad_ok")
    s_dbg = sem("s_dbg")

    gelu_table = sem("gelu_table")
    attention_done = sem("attention_done")
    pad_dest = sem("pad_dest")
    pad_dest_i = sem("pad_dest_i")
    pads_out = sem("pads_out")
    table_step = sem("table_step")
    table_ready = sem("table_ready")
    w_loaded = [sem("w_loaded_even"), sem("w_loaded_odd")]
    b_loaded = sem("b_loaded")
    w_hi = sem("w_hi")
    w_lo = sem("w_lo")
    rows_loaded = sem("rows_loaded")
    f_stats = sem("f_stats")
    f_mean = sem("f_mean")
    f_eps = sem("f_eps")
    f_rstd = sem("f_rstd")
    f_xn = sem("f_xn")
    f_who = sem("f_who")
    f_x_flipped = sem("f_x_flipped")
    f_xt_hi = sem("f_xt_hi")
    f_xt_lo = sem("f_xt_lo")
    f_h = sem("f_h")
    f_bias = sem("f_bias")
    f_gelu = sem("f_gelu")
    f_h_flipped = sem("f_h_flipped")
    f_ht_hi = sem("f_ht_hi")
    f_ht_lo = sem("f_ht_lo")
    f_y = sem("f_y")
    f_base = sem("f_base")
    f_out = sem("f_out")
    f_stored = sem("f_stored")

    done = {
        "s": lambda u, t: (s_lo, 4 * t + u[1] + 1),
        "x": lambda u, t: (x_lo, 16 * t + 4 * u[1] + u[2] + 1),
        "sum": lambda u, t: (x1_ready, t + 1),
        "xn": lambda u, t: (xt_lo, t + 1),
        "xq": lambda u, t: (qs_lo, t + 1),
        "qs": lambda u, t: (qt_ready, t + 1),
        "o": lambda u, t: (ot_lo, t + 1),
        "wo": lambda u, t: (x2_ready, t + 1),
        "x3": lambda u, t: (x3t_ready, t + 1),
        "gate": lambda u, t: (logits_ready, t + 1),
        "rank": lambda u, t: (rank_used, t + 1),
    }

    def bank(use):
        return BANKS[use]

    GROUPS = N // 512

    def value_chunks(n):
        return range(MC * n // (2 * H), MC * (n + 1) // (2 * H))

    block = ctx.enter_context(nc.Block())

    def run_pipeline(eng, body):
        for j in (0, 1):
            body(j, j)
        if LOOP:
            with eng.Fori(2, T - 1) as j:
                body(j, 5)
        else:
            for j in range(2, T - 1):
                body(j, j)
        for j in (T - 1, T, T + 1):
            body(j, j)

    def run_blocks(eng, body):
        body(0, 0)
        if LOOP:
            with eng.Fori(1, BLOCKS - 1 - RING, RING) as b:
                for n in range(RING):
                    body(b + n, 1 + n + RING)
        else:
            for b in range(1, BLOCKS - 2):
                body(b, b)
        for b in (BLOCKS - 2, BLOCKS - 1, BLOCKS):
            body(b, b)

    @block.sync
    def _(sp):
        x_rows = io["x"].rearrange("(t p) d -> p t d", p=P)
        sp.dma_start(x_all[:, 0:4, :], x_rows[:, 0:4, :]).then_inc(s_x_in[0], 16)
        for n, w in enumerate(("WqT", "WvT", "AT")):
            sp.dma_start(w_raw[:, n, :, :], io[w].rearrange("(c p) n -> p c n", p=P)).then_inc(s_w0, 16)
        for g in range(1, 4):
            sp.dma_start(x_all[:, 4 * g:4 * g + 4, :], x_rows[:, 4 * g:4 * g + 4, :]).then_inc(s_x_in[g], 16)
        sp.dma_start(bq_col[:, :], io["bq"].rearrange("(c p) -> p c", p=P), allow_slow_non_contiguous=True).then_inc(s_bias_in, 16)
        sp.dma_start(bv_row[:, :], bass.AP(io["bv"].tensor, 0, [[0, P], [1, D]])).then_inc(s_bias_in, 16)
        sp.dma_start(bg_row[:, :], bass.AP(io["bg"].tensor, 0, [[0, P], [1, E]])).then_inc(s_bias_in, 16)
        sp.dma_start(wg[:, :, :], io["Wg"].rearrange("(c p) e -> p c e", p=P)).then_inc(s_bias_in, 16)
        wkv = io["Wkv"].rearrange("(c p) n -> p c n", p=P)
        sp.dma_start(w2_raw[:, 0, :, :], wkv[:, :, 0:D]).then_inc(s_w2, 16)
        sp.dma_start(w2_raw[:, 1, :, :], wkv[:, :, D:2 * D]).then_inc(s_w2, 16)
        sp.dma_start(w2_raw[:, 2, :, :], io["xWq"].rearrange("(c p) n -> p c n", p=P)).then_inc(s_w2, 16)
        sp.dma_start(w2_raw[:, 3, :, :], io["Wo"].rearrange("(c p) n -> p c n", p=P)).then_inc(s_w2, 16)
        def store_u(g):
            sp.wait_ge(s_ulo, C * (g + 1))
            sp.wait_ge(s_uhi, C * (g + 1))
            sp.dma_start(u_dram[4 * g:4 * g + 4].rearrange("t p c s -> p t c s"), u_out[:, :, :, :].bitcast(F32)).then_inc(s_u_st, 16)

        ctx_v = io["ctxT"].rearrange("(c p) m -> p c m", p=P)
        for g in range(GROUPS):
            lo, hi = g * KB, min((g + 1) * KB, M)
            if g:
                sp.wait_ge(s_ctxlo, g)
            sp.dma_start(ctx_raw[:, :, 0:hi - lo], ctx_v[:, :, lo:hi]).then_inc(s_ctx, 16)
            if g:
                store_u(g - 1)
        store_u(GROUPS - 1)
        sp.wait_ge(s_u_st, 16 * GROUPS)
        sp.wait_ge(s_w2lo, 4)
        def loads_a(t):
            sp.dma_start(u_tile[:, :, :].bitcast(F32), u_dram[bass.ds(t, 1), :, :, :].rearrange("a p c s -> p (a c) s")).then_inc(u_loaded, 16)

        def loads_x(t):
            sp.dma_start(x_tile[:, :], io["x"][bass.ds(t * P, P), :]).then_inc(x_loaded, 16)

        def loads_m(t):
            sp.dma_start(mask_tile[:, :], io["mask"][bass.ds(t * P, P), :]).then_inc(mask_loaded, 16)

        loads_a(0)
        loads_x(0)
        sp.wait_ge(s_pro1, 3)
        loads_m(0)

        def body(j, k):
            if 1 <= k <= T - 1:
                sp.wait_ge(bias_ready, j)
                loads_m(j)
            if k < T - 1:
                sp.wait_ge(scores_ready, 4 * j + 4)
                loads_a(j + 1)
                sp.wait_ge(x1_ready, j + 1)
                loads_x(j + 1)
        run_pipeline(sp, body)

        sp.wait_ge(x1_ready, T)
        for n in range(2 * E):
            e = n % E
            if n >= 2:
                sp.wait_ge(w_hi, n - 1)
                sp.wait_ge(w_lo, n - 1)
            if n < E:
                sp.dma_start(w_stage[:, n % 2, :].rearrange("p (c n) -> p c n", c=C),
                             io["W1"][e].rearrange("(c p) n -> p c n", p=P)).then_inc(w_loaded[n % 2], 16)
            else:
                sp.dma_start(w_stage[:, n % 2, :].rearrange("p (c n) -> p c n", c=FC),
                             io["W2"][e].rearrange("(c p) n -> p c n", p=P)).then_inc(w_loaded[n % 2], 16)
            if n == E + 1:
                sp.wait_ge(x_used, 16 * T)
                sp.dma_start(b2_row[:, :], bass.AP(io["b2"].tensor, 0, [[0, P], [1, E * D]])).then_inc(b_loaded, 16)
                sp.dma_start(b1_row[:, :], bass.AP(io["b1"].tensor, 0, [[0, P], [1, E * DF]])).then_inc(b_loaded, 16)

        sp.wait_ge(s_pad_ok, 16 * E)
        sp.wait_ge(routed, 16 * T)
        sp.wait_ge(table_ready, 3)

        def load_rows(b, k):
            if k >= 1:
                sp.wait_ge(rows_loaded, 16 * b)
            row = sp.value_load(table[0:1, 0, bass.ds(b, 1)], min_val=0, max_val=XROWS - P)
            sp.dma_start(rows[:, k % RING, :], rows_dram[bass.ds(row, P), :]).then_inc(rows_loaded, 16)

        for b in range(2):
            load_rows(b, b)

        def blocks(b, k):
            if k < BLOCKS - 2:
                if k >= 2:
                    sp.wait_ge(f_base, b - 1)
                    sp.wait_ge(f_who, b - 1)
                load_rows(b + 2, k + 2)
        run_blocks(sp, blocks)
        sp.wait_ge(f_stored, 16 * BLOCKS)

    @block.gpsimd
    def _(pool):
        pool.memset(ident[:, :], 0.0).then_inc(s_const, 1)
        pool.memset(below[:, :], 1.0).then_inc(s_const, 1)
        pool.memset(ones[:, :], 1.0).then_inc(s_const, 1)
        pool.memset(minus_half[:, :], -0.5).then_inc(s_const, 1)
        pool.memset(plus_half[:, :], 0.5).then_inc(s_const, 1)
        pool.iota(token[:, :], pattern=[[0, 1]], base=0, channel_multiplier=1,
                  allow_small_or_imprecise_dtypes=True).then_inc(s_const, 1)
        pool.iota(expert_w[:, :], pattern=[[-1, E]], base=E, channel_multiplier=0,
                  allow_small_or_imprecise_dtypes=True).then_inc(s_const, 1)
        pool.iota(seen[:, :], pattern=[[REGION, E]], base=0, channel_multiplier=0,
                  allow_small_or_imprecise_dtypes=True).then_inc(s_const, 1)
        pool.iota(region_base[:, :], pattern=[[REGION, E]], base=0, channel_multiplier=0,
                  allow_small_or_imprecise_dtypes=True).then_inc(s_const, 1)
        pool.iota(lane[:, :], pattern=[[0, 1]], base=0, channel_multiplier=1,
                  allow_small_or_imprecise_dtypes=True).then_inc(s_const, 1)
        pool.iota(sixteenth[:, :], pattern=[[P, T]], base=0, channel_multiplier=0,
                  allow_small_or_imprecise_dtypes=True).then_inc(s_const, 1)
        pool.iota(block_no[:, 0, :], pattern=[[1, BLOCKS]], base=0, channel_multiplier=0,
                  allow_small_or_imprecise_dtypes=True).then_inc(s_const, 1)
        pool.iota(block_no[:, 1, :], pattern=[[P, BLOCKS]], base=0, channel_multiplier=0,
                  allow_small_or_imprecise_dtypes=True).then_inc(s_const, 1)
        pool.wait_ge(s_const, 2)
        pool.affine_select(out=ident[:, :], in_=ident[:, :], compare_op=ALU.not_equal, fill=1.0, base=0,
                           pattern=[[-1, P]], channel_multiplier=1).then_inc(s_const, 1)
        pool.affine_select(out=below[:, :], in_=below[:, :], compare_op=ALU.is_gt, fill=0.0, base=0,
                           pattern=[[1, P]], channel_multiplier=-1).then_inc(s_const, 1)
        pool.memset(v_f32[:, MC - 1, :], 0.0).then_inc(s_vall, 1)
        pool.wait_ge(s_const, 15)
        for g in range(4):
            cols = slice(4 * g, 4 * g + 4)
            pool.wait_ge(s_lnd, g + 1)
            pool.tensor_tensor(rstd_pro[:, cols], var_eps[:, cols], minus_half[:, cols], ALU.pow).then_inc(s_ln, 1)
            pool.tensor_tensor(std_pro[:, cols], mv_pro[:, cols, 1], plus_half[:, cols], ALU.pow).then_inc(s_ln, 1)
        pool.wait_ge(s_vmax, 4)
        pool.partition_all_reduce(v_max[:, 1, :], v_max[:, 0, :], P, bass.bass_isa.ReduceOp.max).then_inc(s_vall, 1)

        pool.wait_ge(s_pro1, 3)
        pool.memset(mask_bias[:, M:MP], PAD_BIAS).then_inc(s_pads, 1)
        pool.memset(pads[:, :], 0.0).then_inc(s_pads, 1)
        pool.wait_ge(s_pads, 2)
        pool.memset(pads[:, D:REC], NOBODY).then_inc(s_pads, 1)
        pool.memset(record[:, D + 1:REC], 0.0).then_inc(s_pads, 1)
        pool.wait_ge(s_pads, 4)
        for n in range(E):
            pool.dma_start(rows_dram[SPARE + n * P:SPARE + (n + 1) * P, :], pads[:, :]).then_inc(s_pad_ok, 16)

        def body(j, k):
            a, b, c = k < T, 1 <= k <= T, k >= 2
            if c:
                if k > 2:
                    pool.wait_ge(routed, 16 * (j - 2))
                pool.wait_ge(x1_copied, j - 1)
                pool.wait_ge(s_pads, 4)
                pool.tensor_copy(record[:, 0:D], x1_old[:, :]).then_inc(record_filled, 1)
            if b:
                if c:
                    pool.wait_ge(record_filled, j - 1)
                pool.wait_ge(x1_ready, j)
                pool.wait_ge(s_pads, 4)
                pool.tensor_copy(x1_old[:, :], x1[:, :]).then_inc(x1_copied, 1)
                if c:
                    pool.wait_ge(xmax, 4 * (j - 1))
                pool.wait_ge(mask_loaded, 16 * j)
                pool.wait_ge(s_pads, 4)
                pool.tensor_scalar(mask_bias[:, 0:M], mask_tile[:, :], -1.0, MASKED, ALU.add, ALU.mult).then_inc(bias_ready, 1)
            if k == T + 1:
                for n in range(2):
                    for e in range(E):
                        pool.wait_ge(pad_dest_i, 1)
                        pool.indirect_dma_start(out=rows_dram[:, :],
                                                out_offset=bass.IndirectOffsetOnAxis(ap=pad_i[:, n, e:e + 1], axis=0),
                                                in_=pads[:, :], in_offset=None).then_inc(pads_out, 16)
            if a:
                if b:
                    pool.wait_ge(coef_step, 2 * j)
                pool.wait_ge(s_pads, 4)
                pool.tensor_copy(norm_col[:, :], norms[:, bass.ds(j, 1)]).then_inc(norm_ready, 1)
            if c:
                pool.wait_ge(stats3, 2 * (j - 1))
                pool.tensor_tensor(rs3[:, 1:2], rs3[:, 0:1], minus_half[:, 0:1], ALU.pow).then_inc(rstd3, 1)
            if a:
                pool.wait_ge(stats1, 2 * j + 2)
                pool.tensor_tensor(rs1[:, 1:2], rs1[:, 0:1], minus_half[:, 0:1], ALU.pow).then_inc(rstd1, 1)
            if c:
                if k > 2:
                    pool.wait_ge(token_next, j - 2)
                pool.wait_ge(s_pads, 4)
                pool.tensor_copy(record[:, D:D + 1], token[:, :]).then_inc(token_set, 1)
                pool.wait_ge(token_set, j - 1)
                pool.wait_ge(s_pads, 4)
                pool.tensor_scalar(token[:, :], token[:, :], float(P), 1.0, ALU.add, ALU.mult).then_inc(token_next, 1)
                pool.wait_ge(x2_ready, j - 1)
                pool.wait_ge(dest_ready, j - 1)
                if k == T + 1:
                    pool.wait_ge(pads_out, 16 * 2 * E)
                pool.wait_ge(s_pads, 4)
                pool.indirect_dma_start(out=rows_dram[:, :], out_offset=bass.IndirectOffsetOnAxis(ap=dest_i[:, 0:1], axis=0),
                                        in_=record[:, :], in_offset=None).then_inc(routed, 16)
        run_pipeline(pool, body)

        def blocks(b, k):
            def norm(b, k):
                pool.wait_ge(f_eps, b + 1)
                pool.tensor_tensor(rs_f[:, 1:2], rs_f[:, 0:1], minus_half[:, 0:1], ALU.pow).then_inc(f_rstd, 1)
                if k >= RING:
                    pool.wait_ge(f_stored, 16 * (b - RING + 1))
                pool.wait_ge(rows_loaded, 16 * (b + 1))
                pool.wait_ge(s_pads, 4)
                pool.tensor_copy(who[:, k % RING, :], rows[:, k % RING, D:D + 1]).then_inc(f_who, 1)

            if k == 0:
                norm(0, 0)
                norm(1, 1)
            if k < BLOCKS - 2:
                norm(b + 2, k + 2)
            if k >= 1:
                if k >= 2:
                    pool.wait_ge(f_stored, 16 * (b - 1))
                pool.wait_ge(f_who, b)
                pool.wait_ge(f_out, b)
                pool.wait_ge(s_pads, 4)
                pool.indirect_dma_start(out=io["out"][:, :],
                                        out_offset=bass.IndirectOffsetOnAxis(ap=who[:, (k - 1) % RING, 0:1], axis=0),
                                        in_=out_f[:, (k - 1) % 2, :], in_offset=None, bounds_check=N - 1,
                                        oob_is_err=False).then_inc(f_stored, 16)
        run_blocks(pool, blocks)

    @block.tensor
    def _(pe):
        def three(out, lhs, rhs, first=True, last=True):
            n = 0
            for c in range(C):
                for a, b in ((0, 0), (0, 1), (1, 0)):
                    mm = pe.matmul(out, lhs(a, c), rhs(b, c), start=(n == 0 and first), stop=(n == 3 * C - 1 and last))
                    n += 1
            return mm

        def self_u(g):
            for o in range(C):
                if g == 0:
                    pe.wait_ge(s_wsplit_lo, 3)
                pe.wait_ge(s_qlo, C * (g + 1))
                if g:
                    pe.wait_ge(s_ulo, C * (g - 1) + o + 1)
                out = self_out if o == 0 else cross_out
                three(out[:, :], lambda a, c: w_self[:, 2, a, c, o * P:(o + 1) * P],
                      lambda b, c: keys_self[:, b, c, g * 512:(g + 1) * 512]).then_inc(s_u, 1)

        pe.wait_ge(s_const, 15)
        for g in range(GROUPS):
            for c in range(C):
                pe.wait_ge(s_xs, 4 * (g + 1))
                if g:
                    pe.wait_ge(s_ptlo, C * (g - 1) + c + 1)
                for n in range(4):
                    tr = pe.transpose(flip[:, c, n * P:(n + 1) * P], x_all[:, 4 * g + n, c * P:(c + 1) * P], ident[:, :])
                tr.then_inc(s_ptf, 1)
            if g:
                self_u(g - 1)
            if g == 0:
                pe.wait_ge(s_wsplit_lo, 1)
            pe.wait_ge(s_ptlo, C * (g + 1))
            for o in range(C):
                if g:
                    pe.wait_ge(s_qlo, C * (g - 1) + o + 1)
                three(scores[:, o, :], lambda a, c: w_self[:, 0, a, c, o * P:(o + 1) * P],
                      lambda b, c: xt_pro[:, b, c, :]).then_inc(s_q, 1)
            if g == 0:
                pe.wait_ge(s_wsplit_lo, 2)
            for n in range(4):
                if g and n % 2 == 0:
                    pe.wait_ge(s_vt, 4 * (g - 1) + n + 2)
                three(scores[:, 2 + n // 2, (n % 2) * D:(n % 2 + 1) * D] , lambda a, c: xt_pro[:, a, c, n * P:(n + 1) * P],
                      lambda b, c: w_self[:, 1, b, c, :]).then_inc(s_v, 1)
        self_u(GROUPS - 1)

        for m in range(MC):
            rows = P if m < MC - 1 else MLAST
            if m == 0:
                pe.wait_ge(s_w2lo, 2)
            pe.wait_ge(s_ctxlo, (m * P + rows - 1) // KB + 1)
            if m >= 2:
                pe.wait_ge(s_vxf, m - 1)
            three(flip[0:rows, m % 2, 0:D], lambda a, c: ctx_t[:, a, c, m * P:m * P + rows],
                  lambda b, c: wv_cross[:, b, c, :]).then_inc(s_vx, 1)
        for g in range(4):
            for h in range(H):
                if g:
                    pe.wait_ge(s_klo, H * (g - 1) + h + 1)
                elif h < 2:
                    pe.wait_ge(s_qlo, C * GROUPS)
                else:
                    pe.wait_ge(s_vt, 4 * GROUPS)
                three(scores[:, h, 0:KB], lambda a, c: wk_dup[:, a, c, h, :, :],
                      lambda b, c: ctx_t[:, b, c, g * KB:(g + 1) * KB]).then_inc(s_k, 1)

        pe.wait_ge(s_pro1, 3)

        def wait_bank(use, j, k):
            before, back = previous_use(use, k)
            if before is not None:
                s, v = done[before[0]](before, j - back - stage_of(before))
                pe.wait_ge(s, v)

        def self_scores(j, k, n):
            if n == 0:
                pe.wait_ge(u_loaded, 16 * (j + 1))
            if k >= 2:
                pe.wait_ge(xmax_a if n < 2 else xmax, 4 * (j - 1))
            elif k == 1:
                pe.wait_ge(self_exp, 1 + n // 2)
            three(scores[:, n, :], lambda a, c: u_tile[:, a * C + c, :],
                  lambda b, c: keys_self[:, b, c, n * 512:(n + 1) * 512]).then_inc(scores_ready, 1)

        def self_flip(j, k, g):
            use = ("s", g)
            if g % 2 == 0:
                pe.wait_ge(self_exp, 2 * j + g // 2 + 1)
            wait_bank(use, j, k)
            for n in range(4):
                m = 4 * g + n
                tr = pe.transpose(flip[:, bank(use), n * P:(n + 1) * P], exp_self[:, m * P:(m + 1) * P], ident[:, :])
            tr.then_inc(s_flipped, 1)

        def self_values(j, k, g):
            pe.wait_ge(s_lo, 4 * j + g + 1)
            if g == 0:
                wait_bank(("sum",), j, k)
            for n in range(4):
                m = 4 * g + n
                for a, b in ((0, 0), (0, 1), (1, 0)):
                    mm = pe.matmul(self_out[:, 0:D], ps_self[:, g, a, n * P:(n + 1) * P], vals_self[:, m, b, :],
                                   start=(m == 0 and a == 0 and b == 0), stop=(m == T - 1 and a == 1))
            mm.then_inc(s_used, 1)

        def cross_scores(j, k, h, half):
            if h == 0 and half == 0:
                pe.wait_ge(qt_ready, j)
            if h == 0 and k < T:
                pe.wait_ge(self_exp, 2 * j + half + 1)
            if h > 0 or k >= T:
                pe.wait_ge(xmax if half else xmax_a, 4 * (j - 1) + h)
            for n in (2 * half, 2 * half + 1):
                for part in range(2):
                    mm = pe.matmul(scores[:, n, 0:KB], qt[:, h, :], keys_cross[:, part, h, n * KB:(n + 1) * KB],
                                   start=(part == 0), stop=(part == 1))
            mm.then_inc(xs_ready, 1)

        def cross_flip(j, k, h, g):
            use = ("x", h, g)
            t = j - stage_of(use)
            if g % 2 == 0:
                pe.wait_ge(xexp, 8 * t + 2 * h + g // 2 + 1)
            wait_bank(use, j, k)
            for n, m in enumerate(XG[g]):
                rows = P if m < MC - 1 else MLAST
                tr = pe.transpose(flip[0:rows, bank(use), n * P:(n + 1) * P], exp_cross[:, h % 2, m * P:m * P + rows], ident[:, :])
            tr.then_inc(x_flipped, 1)

        def cross_values(j, k, h, g):
            t = j - (2 if (h, g) in ((2, 0), (2, 1)) else stage_of(("x", h, g)))
            pe.wait_ge(x_lo, 16 * t + 4 * h + g + 1)
            if h == 0 and g == 0 and k >= 2:
                pe.wait_ge(o_summed, t)
            for n, m in enumerate(XG[g]):
                rows = P if m < MC - 1 else MLAST
                pe.matmul(cross_out[:, h * P:(h + 1) * P], ps_cross[0:rows, g, 0, n * P:(n + 1) * P],
                          vals_cross[0:rows, m, h, :, :], start=(m == 0), stop=False, skip_group_check=True)
                mm = pe.matmul(cross_out[:, h * P:h * P + HD], ps_cross[0:rows, g, 1, n * P:(n + 1) * P],
                               vals_cross[0:rows, m, h, 0, :], start=False, stop=(m == MC - 1), skip_group_check=True)
            mm.then_inc(x_used, 1)

        def small(use, j, k, ready, value, filled, work):
            pe.wait_ge(ready, value)
            wait_bank(use, j, k)
            work(flip[:, bank(use), :]).then_inc(filled, 1)

        def flip_row(src):
            def work(out):
                for c in range(C):
                    tr = pe.transpose(out[:, c * P:(c + 1) * P], src[:, c * P:(c + 1) * P], ident[:, :])
                return tr
            return work

        def flip_queries(out):
            for h in range(H):
                tr = pe.transpose(out[:, h * P:(h + 1) * P], qs[:, h, :, :].bitcast(F32), ident[:, :])
            return tr

        def gate(out):
            for c in range(C):
                mm = pe.matmul(out[:, 0:E], x3t[:, c, :], wg[:, c, :], start=(c == 0), stop=(c == C - 1))
            return mm

        def rank(out):
            pe.matmul(out[:, 0:E], below[:, :], onehot16[:, :], start=True, stop=True)
            return pe.matmul(out[:, E:2 * E], ones[:, :], onehot16[:, :], start=True, stop=True)

        def body(j, k):
            a, b, c = k < T, 1 <= k <= T, k >= 2
            if a:
                self_scores(j, k, 0)
            if c:
                cross_flip(j, k, 2, 2)
            if a:
                self_scores(j, k, 1)
            if c:
                cross_flip(j, k, 2, 3)
            if b:
                small(("xn",), j, k, xn_ready, j, xn_flipped, flip_row(xn))
            if a:
                self_scores(j, k, 2)
            if c:
                cross_flip(j, k, 3, 0)
            if b:
                small(("xq",), j, k, xt_lo, j, q_ready,
                      lambda out: three(out[:, 0:D], lambda a, c: xt[:, a, c, :], lambda b, c: wq_cross[:, b, c, :]))
            if a:
                self_scores(j, k, 3)
            if c:
                cross_values(j, k, 2, 0)
            if b:
                small(("qs",), j, k, qs_lo, j, q_flipped, flip_queries)
            if c:
                cross_values(j, k, 2, 1)
                cross_values(j, k, 2, 2)
                cross_values(j, k, 2, 3)
                cross_flip(j, k, 3, 1)
                cross_flip(j, k, 3, 2)
                cross_values(j, k, 3, 0)
            if b:
                cross_scores(j, k, 0, 0)
            if a:
                self_flip(j, k, 0)
            if c:
                cross_values(j, k, 3, 1)
                cross_flip(j, k, 3, 3)
            if a:
                self_flip(j, k, 1)
            if b:
                cross_scores(j, k, 0, 1)
            if c:
                cross_values(j, k, 3, 2)
            if a:
                self_flip(j, k, 2)
            if b:
                cross_scores(j, k, 1, 0)
            if c:
                cross_values(j, k, 3, 3)
            if a:
                self_values(j, k, 0)
                self_flip(j, k, 3)
            if b:
                cross_scores(j, k, 1, 1)
            if c:
                small(("o",), j, k, o_ready, j - 1, o_flipped, flip_row(o_tile[:, :, :].rearrange("p h d -> p (h d)")))
            if a:
                self_values(j, k, 1)
            if b:
                cross_flip(j, k, 0, 0)
            if c:
                small(("wo",), j, k, ot_lo, j - 1, wo_ready,
                      lambda out: three(out[:, 0:D], lambda a, c: ot[:, a, c, :], lambda b, c: wo_cross[:, b, c, :]))
            if a:
                self_values(j, k, 2)
                self_values(j, k, 3)
            if b:
                cross_flip(j, k, 0, 1)
                cross_flip(j, k, 0, 2)
                cross_values(j, k, 0, 0)
                cross_flip(j, k, 0, 3)
                cross_scores(j, k, 2, 0)
                cross_values(j, k, 0, 1)
                cross_flip(j, k, 1, 0)
                cross_flip(j, k, 1, 1)
            if c:
                small(("x3",), j, k, xn3_ready, j - 1, x3_flipped, flip_row(xn3))
            if b:
                cross_scores(j, k, 2, 1)
                cross_values(j, k, 0, 2)
                cross_values(j, k, 0, 3)
                cross_flip(j, k, 1, 2)
            if c:
                small(("gate",), j, k, x3t_ready, j - 1, gate_ready, gate)
            if b:
                cross_values(j, k, 1, 0)
                cross_scores(j, k, 3, 0)
                cross_flip(j, k, 1, 3)
                cross_values(j, k, 1, 1)
                cross_flip(j, k, 2, 0)
                cross_scores(j, k, 3, 1)
                cross_values(j, k, 1, 2)
                cross_flip(j, k, 2, 1)
                cross_values(j, k, 1, 3)
            if c:
                small(("rank",), j, k, onehot_ready, j - 1, rank_ready, rank)
        run_pipeline(pe, body)
        pe.wait_ge(x2_ready, T)
        pe.wait_ge(table_ready, 3)

        def flip_x(b, k):
            pe.wait_ge(f_xn, b + 1)
            for c in range(C):
                tr = pe.transpose(self_out[:, c * P:(c + 1) * P], xn_f[:, c * P:(c + 1) * P], ident[:, :])
            tr.then_inc(f_x_flipped, 1)

        def blocks(b, k):
            if k == 0:
                flip_x(0, 0)
            if k >= 1:
                for n in range(2):
                    pe.wait_ge(f_gelu, 2 * (b - 1) + n + 1)
                    for c in range(4):
                        f = 4 * n + c
                        tr = pe.transpose(flip[:, n, c * P:(c + 1) * P], hidden[:, f * P:(f + 1) * P], ident[:, :])
                    tr.then_inc(f_h_flipped, 1)
            if k < BLOCKS:
                if k == 0:
                    pe.wait_ge(w_lo, E)
                pe.wait_ge(f_xt_lo, b + 1)
                off = pe.value_load(table[0:1, 1, bass.ds(b, 1)], min_val=0, max_val=(E - 1) * DF)
                for n in range(2):
                    three(scores[:, n, :], lambda a, c: xt_f[:, a, c, :],
                          lambda p, c: w1s[:, p, c, bass.ds(off + n * 512, 512)]).then_inc(f_h, 1)
            if k < BLOCKS - 1:
                flip_x(b + 1, k + 1)
            if k >= 1:
                if k == 1:
                    pe.wait_ge(w_lo, 2 * E)
                off2 = pe.value_load(table[0:1, 2, bass.ds(b - 1, 1)], min_val=0, max_val=(E - 1) * D)
                if k >= 2:
                    pe.wait_ge(f_out, b - 1)
                for f in range(FC):
                    if f % 4 == 0:
                        pe.wait_ge(f_ht_lo, 2 * (b - 1) + f // 4 + 1)
                    for a, p in ((0, 0), (0, 1), (1, 0)):
                        mm = pe.matmul(cross_out[:, 0:D], ht[:, a, f, :], w2s[:, p, f, bass.ds(off2, D)],
                                       start=(f == 0 and a == 0 and p == 0), stop=(f == FC - 1 and a == 1))
                mm.then_inc(f_y, 1)
        run_blocks(pe, blocks)

    @block.scalar
    def _(act):
        def copy(out, in_, **kw):
            return act.activation(out, in_, ACT.Copy, **kw)

        act.wait_ge(s_w0, 16 * 3)
        for n in range(3):
            copy(w_self[:, n, 0, :, :], w_raw[:, n, :, :]).then_inc(s_wsplit_hi, 1)

        def u_hi(g):
            for o in range(C):
                act.wait_ge(s_u, C * g + o + 1)
                if g:
                    act.wait_ge(s_u_st, 16 * g)
                out = self_out if o == 0 else cross_out
                act.activation(u_out[:, :, o, :], out[:, :].rearrange("p (t s) -> p t s", t=4), ACT.Copy,
                               scale=1.0 / 16.0).then_inc(s_uhi, 1)

        for g in range(GROUPS):
            for c in range(C):
                act.wait_ge(s_ptf, C * g + c + 1)
                if g:
                    act.wait_ge(s_v, 4 * g)
                    act.wait_ge(s_q, C * g)
                copy(xt_pro[:, 0, c, :], flip[:, c, :]).then_inc(s_pthi, 1)
            if g:
                u_hi(g - 1)
            if g == 0:
                act.wait_ge(s_w2, 64)
                for dup in range(2):
                    copy(wk_dup[:, 0, :, :, dup, :], w2_raw[:, 0, :, :].rearrange("p c (h d) -> p c h d", h=H)).then_inc(s_w2hi, 1)
                for n, w in ((1, wv_cross), (2, wq_cross), (3, wo_cross)):
                    copy(w[:, 0, :, :], w2_raw[:, n, :, :]).then_inc(s_w2hi, 1)
                act.wait_ge(s_bias_in, 64)
            act.wait_ge(s_ctx, 16 * (g + 1))
            act.wait_ge(s_vsc, 1)
            copy(ctx_t[:, 0, :, g * KB:min((g + 1) * KB, M)], ctx_raw[:, :, 0:min(KB, M - g * KB)]).then_inc(s_ctxhi, 1)
            for o in range(C):
                act.wait_ge(s_q, C * g + o + 1)
                act.activation(keys_self[:, 0, o, g * 512:(g + 1) * 512], scores[:, o, :], ACT.Identity,
                               bias=bq_col[:, o:o + 1]).then_inc(s_qhi, 1)
            for n in range(4):
                act.wait_ge(s_vt, 4 * g + n + 1)
                copy(vals_self[:, 4 * g + n, 0, :], v_tmp[:, n % 2, :]).then_inc(s_vhi, 1)
        u_hi(GROUPS - 1)

        for m in range(MC):
            rows = P if m < MC - 1 else MLAST
            act.wait_ge(s_vx, m + 1)
            act.wait_ge(s_vall, 1)
            copy(v_f32[0:rows, m, :], flip[0:rows, m % 2, 0:D]).then_inc(s_vxf, 1)
        act.wait_ge(s_u_st, 16 * GROUPS)
        act.wait_ge(s_ulo, C * GROUPS)
        act.wait_ge(s_vlo, 4 * GROUPS)
        for g in range(4):
            for h in range(H):
                act.wait_ge(s_k, H * g + h + 1)
                copy(keys_cross[:, 0, h, g * KB:(g + 1) * KB], scores[:, h, 0:KB]).then_inc(s_khi, 1)
                if g >= 2:
                    for m in value_chunks(H * (g - 2) + h):
                        act.wait_ge(s_vsc, 4)
                        act.activation(vals_cross[:, m, :, 0, :], v_f32[:, m, :].rearrange("p (h d) -> p h d", h=H), ACT.Copy,
                                       scale=v_scale[:, 0:1]).then_inc(s_vxhi, 1)
        copy(barrier[:, 0:1], ident[:, 0:1]).then_inc(s_pro1, 1)
        act.wait_ge(s_pro1, 3)

        def weights_hi(n):
            e = n % E
            act.wait_ge(w_loaded[n % 2], 16 * (n // 2 + 1))
            if n < E:
                copy(w1s[:, 0, :, e * DF:(e + 1) * DF], w_stage[:, n % 2, :].rearrange("p (c n) -> p c n", c=C)).then_inc(w_hi, 1)
            else:
                act.wait_ge(x_used, 16 * T)
                copy(w2s[:, 0, :, e * D:(e + 1) * D], w_stage[:, n % 2, :].rearrange("p (c n) -> p c n", c=FC)).then_inc(w_hi, 1)

        def cross_hi(j, k, h, g):
            use = ("x", h, g)
            t = j - stage_of(use)
            act.wait_ge(x_flipped, 16 * t + 4 * h + g + 1)
            if h + g + k > 3 + 0:
                pass
            w = len(XG[g]) * P
            rows = P if g < NG - 1 else MLAST
            if not (k == 1 and h == 0):
                act.wait_ge(x_used, 16 * t + 4 * h + g - 3)
            copy(ps_cross[0:rows, g, 0, 0:w], flip[0:rows, bank(use), 0:w]).then_inc(x_hi, 1)

        def self_hi(j, k, g):
            act.wait_ge(s_flipped, 4 * j + g + 1)
            if k >= 1:
                act.wait_ge(s_used, 4 * j + g - 3)
            copy(ps_self[:, g, 0, :], flip[:, bank(("s", g)), :]).then_inc(s_hi, 1)

        def body(j, k):
            a, b, c = k < T, 1 <= k <= T, k >= 2
            if k == T + 1:
                act.activation(barrier[:, 1:2], ident[:, 0:1], ACT.Gelu).then_inc(gelu_table, 1)
            if c:
                cross_hi(j, k, 2, 2)
            if b:
                act.wait_ge(xn_flipped, j)
                copy(xt[:, 0, :, :], flip[:, bank(("xn",)), 0:D].rearrange("p (c s) -> p c s", c=C)).then_inc(xt_hi, 1)
            if c:
                cross_hi(j, k, 2, 3)
            if k == T:
                weights_hi(0)
            if b:
                act.wait_ge(q_ready, j)
                if k >= 2:
                    act.wait_ge(q_flipped, j - 1)
                copy(qs[:, :, 0, :], flip[:, bank(("xq",)), 0:D].rearrange("p (h d) -> p h d", h=H)).then_inc(qs_hi, 1)
            if c:
                cross_hi(j, k, 3, 0)
            if b:
                act.wait_ge(q_flipped, j)
                if k >= 2:
                    act.wait_ge(xs_ready, 8 * (j - 1))
                act.activation(qt[:, :, :], flip[:, bank(("qs",)), :].rearrange("p (h s) -> p h s", h=H), ACT.Copy,
                               scale=HD ** -0.5).then_inc(qt_ready, 1)
            if a:
                self_exps(j, k, 0)
            if c:
                cross_hi(j, k, 3, 1)
                cross_hi(j, k, 3, 2)
            if a:
                self_exps(j, k, 1)
                self_hi(j, k, 0)
            if c:
                cross_hi(j, k, 3, 3)
            if k == T:
                weights_hi(1)
            if k == T + 1:
                weights_hi(4)
            if a:
                self_hi(j, k, 1)
                self_hi(j, k, 2)
            if b:
                cross_exp(j, k, 0, 0)
            if a:
                self_hi(j, k, 3)
            if c:
                act.wait_ge(o_flipped, j - 1)
                copy(ot[:, 0, :, :], flip[:, bank(("o",)), 0:D].rearrange("p (c s) -> p c s", c=C)).then_inc(ot_hi, 1)
            if k == T + 1:
                weights_hi(5)
            if b:
                cross_hi(j, k, 0, 0)
                cross_exp(j, k, 0, 1)
                cross_exp(j, k, 1, 0)
                cross_hi(j, k, 0, 1)
                cross_hi(j, k, 0, 2)
                cross_hi(j, k, 0, 3)
            if k == T:
                weights_hi(2)
            if b:
                cross_exp(j, k, 1, 1)
                cross_hi(j, k, 1, 0)
                cross_hi(j, k, 1, 1)
            if c:
                act.wait_ge(x3_flipped, j - 1)
                if k > 2:
                    act.wait_ge(gate_ready, j - 2)
                copy(x3t[:, :, :], flip[:, bank(("x3",)), 0:D].rearrange("p (c s) -> p c s", c=C)).then_inc(x3t_ready, 1)
            if b:
                cross_hi(j, k, 1, 2)
                cross_exp(j, k, 2, 0)
                cross_hi(j, k, 1, 3)
            if k == T:
                weights_hi(3)
            if b:
                cross_hi(j, k, 2, 0)
                cross_exp(j, k, 2, 1)
                cross_hi(j, k, 2, 1)
                cross_exp(j, k, 3, 0)
                cross_exp(j, k, 3, 1)

        def self_exps(j, k, half):
            if half == 0:
                act.wait_ge(self_max, j + 1)
                if k >= 1:
                    act.wait_ge(s_used, 4 * j)
                    act.wait_ge(x1_ready, j)
            banks = slice(half * NB // 2, (half + 1) * NB // 2)
            act.activation(exp_self[:, half * N // 2:(half + 1) * N // 2].rearrange("p (n s) -> p n s", n=NB // 2),
                           scores[:, banks, :], ACT.Exp, bias=sneg[:, 0:1],
                           accum_out=sden[:, half:half + 1]).then_inc(self_exp, 1)

        def cross_exp(j, k, h, half):
            if half == 0:
                act.wait_ge(xmax, 4 * (j - 1) + h + 1)
                if h == 0 and k >= 2:
                    act.wait_ge(o_step, 3 * (j - 1))
            cols = slice(XHALF, MP) if half else slice(0, XHALF)
            act.activation(exp_cross[:, h % 2, cols], exp_cross[:, h % 2, cols], ACT.Exp, bias=xneg[:, h % 2, 1:2],
                           scale=-1.0, accum_out=xden[:, half, h:h + 1]).then_inc(xexp, 1)

        run_pipeline(act, body)
        copy(barrier[:, 0:1], ident[:, 0:1]).then_inc(attention_done, 1)
        for n in (E + 2, E + 3):
            weights_hi(n)
        act.wait_ge(attention_done, 3)

        def blocks(b, k):
            def x_hi_f(b):
                act.wait_ge(f_x_flipped, b + 1)
                copy(xt_f[:, 0, :, :], self_out[:, 0:D].rearrange("p (c s) -> p c s", c=C)).then_inc(f_xt_hi, 1)

            def gelu(b, n):
                act.wait_ge(f_bias, 2 * b + n + 1)
                cols = slice(n * 512, (n + 1) * 512)
                act.activation(hidden[:, cols], hidden[:, cols], ACT.Gelu).then_inc(f_gelu, 1)

            if k == 0:
                x_hi_f(0)
            if k >= 1:
                for n in range(2):
                    act.wait_ge(f_h_flipped, 2 * (b - 1) + n + 1)
                    if k >= 2:
                        act.wait_ge(f_y, b - 1)
                    copy(ht[:, 0, 4 * n:4 * n + 4, :], flip[:, n, :].rearrange("p (c s) -> p c s", c=4)).then_inc(f_ht_hi, 1)
            if k < BLOCKS:
                gelu(b, 0)
            if k < BLOCKS - 1:
                x_hi_f(b + 1)
            if k < BLOCKS:
                gelu(b, 1)
        run_blocks(act, blocks)

    @block.vector
    def _(dve):
        def low(out, full, hi):
            return dve.tensor_tensor(out, full, hi, ALU.subtract)

        def statistics_pro(g):
            tiles = range(4 * g, 4 * g + 4)
            dve.wait_ge(s_x_in[g], 16)
            for t in tiles:
                dve.bn_stats(stats_pro[:, t, :], x_all[:, t, :]).then_inc(s_xstat, 1)
            dve.wait_ge(s_xstat, 8 * g + 4)
            for t in tiles:
                dve.bn_aggr(mv_pro[:, t, :], stats_pro[:, t, :]).then_inc(s_xstat, 1)
            dve.wait_ge(s_xstat, 8 * g + 8)
            dve.tensor_scalar(var_eps[:, 4 * g:4 * g + 4], mv_pro[:, 4 * g:4 * g + 4, 1], EPS, None, ALU.add).then_inc(s_lnd, 1)

        def scale_rows(g):
            cols = slice(4 * g, 4 * g + 4)
            dve.wait_ge(s_ln, 2 * g + 2)
            dve.scalar_tensor_tensor(out=norms[:, cols], in0=rstd_pro[:, cols], scalar=float(D) ** 0.5, in1=std_pro[:, cols],
                                     op0=ALU.mult, op1=ALU.mult).then_inc(s_norm, 1)
            dve.wait_ge(s_norm, 4 * g + 1)
            dve.tensor_scalar(norm_eps[:, cols], norms[:, cols], 1e-9, None, ALU.add).then_inc(s_norm, 1)
            dve.wait_ge(s_norm, 4 * g + 2)
            dve.reciprocal(norm_inv[:, cols], norm_eps[:, cols]).then_inc(s_norm, 1)
            dve.wait_ge(s_norm, 4 * g + 3)
            dve.tensor_tensor(row_scale[:, cols], norm_inv[:, cols], rstd_pro[:, cols], ALU.mult).then_inc(s_norm, 1)
            dve.wait_ge(s_norm, 4 * g + 4)
            for t in range(4 * g, 4 * g + 4):
                dve.tensor_scalar(x_all[:, t, :], x_all[:, t, :], mv_pro[:, t, 0:1], row_scale[:, t:t + 1],
                                  ALU.subtract, ALU.mult).then_inc(s_xs, 1)

        def u_lo(g):
            for o in range(C):
                dve.wait_ge(s_uhi, C * g + o + 1)
                out = self_out if o == 0 else cross_out
                dve.scalar_tensor_tensor(out=u_out[:, :, C + o, :], in0=out[:, :].rearrange("p (t s) -> p t s", t=4),
                                         scalar=1.0 / 16.0, in1=u_out[:, :, o, :].bitcast(F32), op0=ALU.mult,
                                         op1=ALU.subtract).then_inc(s_ulo, 1)

        dve.memset(ctx_t[:, :, :, M:MP].bitcast(F32), 0.0).then_inc(s_vsc, 1)
        statistics_pro(0)
        for n in range(3):
            if n == 1:
                scale_rows(0)
            dve.wait_ge(s_wsplit_hi, n + 1)
            low(w_self[:, n, 1, :, :], w_raw[:, n, :, :], w_self[:, n, 0, :, :].bitcast(F32)).then_inc(s_wsplit_lo, 1)
            if n == 1:
                for c in range(C):
                    dve.wait_ge(s_pthi, c + 1)
                    low(xt_pro[:, 1, c, :], flip[:, c, :], xt_pro[:, 0, c, :].bitcast(F32)).then_inc(s_ptlo, 1)
        for g in range(GROUPS):
            if g:
                for c in range(C):
                    dve.wait_ge(s_pthi, C * g + c + 1)
                    low(xt_pro[:, 1, c, :], flip[:, c, :], xt_pro[:, 0, c, :].bitcast(F32)).then_inc(s_ptlo, 1)
                u_lo(g - 1)
            else:
                dve.wait_ge(s_bias_in, 64)
            if g < GROUPS - 1:
                statistics_pro(g + 1)
            if g == 0:
                for dup in range(2):
                    dve.wait_ge(s_w2hi, dup + 1)
                    for c in range(C):
                        op = low(wk_dup[:, 1, c, :, dup, :], w2_raw[:, 0, c, :].rearrange("p (h d) -> p h d", h=H),
                                 wk_dup[:, 0, c, :, dup, :].bitcast(F32))
                    if dup:
                        op.then_inc(s_w2lo, 1)
            if g == 1:
                for n, w in ((1, wv_cross), (2, wq_cross), (3, wo_cross)):
                    dve.wait_ge(s_w2hi, 2 + n)
                    low(w[:, 1, :, :], w2_raw[:, n, :, :], w[:, 0, :, :].bitcast(F32)).then_inc(s_w2lo, 1)
            for o in range(C):
                dve.wait_ge(s_qhi, C * g + o + 1)
                cols = slice(g * 512, (g + 1) * 512)
                dve.scalar_tensor_tensor(out=keys_self[:, 1, o, cols], in0=scores[:, o, :], scalar=bq_col[:, o:o + 1],
                                         in1=keys_self[:, 0, o, cols].bitcast(F32), op0=ALU.add,
                                         op1=ALU.subtract).then_inc(s_qlo, 1)
            if g < GROUPS - 1:
                scale_rows(g + 1)
            dve.wait_ge(s_ctxhi, g + 1)
            cols = slice(g * KB, min((g + 1) * KB, M))
            low(ctx_t[:, 1, :, cols], ctx_raw[:, :, 0:min(KB, M - g * KB)], ctx_t[:, 0, :, cols].bitcast(F32)).then_inc(s_ctxlo, 1)
            for n in range(4):
                dve.wait_ge(s_v, 4 * g + n - n % 2 + 2)
                if 4 * g + n >= 2:
                    dve.wait_ge(s_vhi, 4 * g + n - 1)
                    dve.wait_ge(s_vlo, 4 * g + n - 1)
                dve.tensor_tensor(v_tmp[:, n % 2, :], scores[:, 2 + n // 2, (n % 2) * D:(n % 2 + 1) * D], bv_row[:, :],
                                  ALU.add).then_inc(s_vt, 1)
                if n % 2:
                    for m in (n - 1, n):
                        dve.wait_ge(s_vhi, 4 * g + m + 1)
                        dve.wait_ge(s_vt, 4 * g + m + 1)
                        low(vals_self[:, 4 * g + m, 1, :], v_tmp[:, m % 2, :],
                            vals_self[:, 4 * g + m, 0, :].bitcast(F32)).then_inc(s_vlo, 1)
        u_lo(GROUPS - 1)

        dve.wait_ge(s_u_st, 16 * GROUPS)
        for g in range(4):
            for h in range(H):
                if g == 0:
                    dve.wait_ge(s_vxf, MC)
                    dve.tensor_reduce(v_max[:, 0, h:h + 1], v_f32[:, MC * h // H:MC * (h + 1) // H, :], AX.XY, ALU.max,
                                      apply_absolute_value=True).then_inc(s_vmax, 1)
                dve.wait_ge(s_khi, H * g + h + 1)
                cols = slice(g * KB, (g + 1) * KB)
                low(keys_cross[:, 1, h, cols], scores[:, h, 0:KB], keys_cross[:, 0, h, cols].bitcast(F32)).then_inc(s_klo, 1)
                if g == 1 and h == H - 1:
                    dve.wait_ge(s_vall, 2)
                    dve.tensor_reduce(v_top[:, 0:1], v_max[:, 1, :], AX.X, ALU.max).then_inc(s_vtop, 1)
                    dve.wait_ge(s_vtop, 1)
                    dve.tensor_scalar(v_top[:, 1:2], v_top[:, 0:1], 1e-30, 1.0 / V_TOP, ALU.max, ALU.mult).then_inc(s_vsc, 1)
                    dve.wait_ge(s_vsc, 2)
                    dve.tensor_copy(v_scale[:, 1:2], v_top[:, 1:2]).then_inc(s_vsc, 1)
                    dve.reciprocal(v_scale[:, 0:1], v_top[:, 1:2]).then_inc(s_vsc, 1)
                if g >= 2:
                    for m in value_chunks(H * (g - 2) + h):
                        dve.wait_ge(s_vxhi, m + 1)
                        dve.wait_ge(s_vsc, 4)
                        dve.scalar_tensor_tensor(out=vals_cross[:, m, :, 1, :], in0=v_f32[:, m, :].rearrange("p (h d) -> p h d", h=H),
                                                 scalar=v_scale[:, 0:1], in1=vals_cross[:, m, :, 0, :], op0=ALU.mult,
                                                 op1=ALU.subtract).then_inc(s_vxlo, 1)
        dve.wait_ge(s_vxlo, MC)
        dve.wait_ge(s_klo, 4 * H)
        dve.tensor_copy(barrier[:, 1:2], ident[:, 0:1]).then_inc(s_pro1, 2)
        dve.wait_ge(s_pro1, 3)

        def weights_lo(n):
            e = n % E
            dve.wait_ge(w_hi, n + 1)
            if n < E:
                w, cols, ch = w1s, slice(e * DF, (e + 1) * DF), C
            else:
                w, cols, ch = w2s, slice(e * D, (e + 1) * D), FC
            low(w[:, 1, :, cols], w_stage[:, n % 2, :].rearrange("p (c n) -> p c n", c=ch),
                w[:, 0, :, cols].bitcast(F32)).then_inc(w_lo, 1)

        def cross_lo(j, k, h, g):
            use = ("x", h, g)
            t = j - stage_of(use)
            w = len(XG[g]) * P
            rows = P if g < NG - 1 else MLAST
            dve.wait_ge(x_hi, 16 * t + 4 * h + g + 1)
            low(ps_cross[0:rows, g, 1, 0:w], flip[0:rows, bank(use), 0:w], ps_cross[0:rows, g, 0, 0:w]).then_inc(x_lo, 1)

        def self_lo(j, k, g):
            dve.wait_ge(s_hi, 4 * j + g + 1)
            low(ps_self[:, g, 1, :], flip[:, bank(("s", g)), :], ps_self[:, g, 0, :].bitcast(F32)).then_inc(s_lo, 1)

        def part_max(j, k, n):
            dve.wait_ge(scores_ready, 4 * j + n + 1)
            dve.tensor_reduce(smax[:, n:n + 1], scores[:, n, :], AX.X, ALU.max).then_inc(max_part, 1)

        def cross_max(j, k, h, half):
            dve.wait_ge(xs_ready, 8 * (j - 1) + 2 * h + half + 1)
            if half == 0:
                if h == 0:
                    dve.wait_ge(bias_ready, j)
                if h >= 2 or k >= 2:
                    dve.wait_ge(x_flipped, 16 * (j - 1) + 4 * (h - 1))
            else:
                dve.wait_ge(xmax_a, 4 * (j - 1) + h + 1)
            cols = slice(2 * half * KB, 2 * (half + 1) * KB)
            dve.tensor_tensor_reduce(exp_cross[:, h % 2, cols].rearrange("p (n s) -> p n s", n=2),
                                     scores[:, 2 * half:2 * half + 2, 0:KB],
                                     mask_bias[:, cols].rearrange("p (n s) -> p n s", n=2), -1.0,
                                     xneg[:, h % 2, 0:1] if half else MAX_CAP, ALU.add, ALU.min,
                                     xneg[:, h % 2, half:half + 1]).then_inc(xmax if half else xmax_a, 1)

        def body(j, k):
            a, b, c = k < T, 1 <= k <= T, k >= 2
            if k == T + 1:
                pad_rows()
            if a:
                part_max(j, k, 0)
            if c:
                cross_lo(j, k, 2, 2)
            if b:
                dve.wait_ge(xt_hi, j)
                low(xt[:, 1, :, :], flip[:, bank(("xn",)), 0:D].rearrange("p (c s) -> p c s", c=C),
                    xt[:, 0, :, :].bitcast(F32)).then_inc(xt_lo, 1)
            if a:
                part_max(j, k, 1)
                part_max(j, k, 2)
            if c:
                cross_lo(j, k, 2, 3)
            if k == T:
                weights_lo(0)
            if b:
                dve.wait_ge(qs_hi, j)
                low(qs[:, :, 1, :], flip[:, bank(("xq",)), 0:D].rearrange("p (h d) -> p h d", h=H),
                    qs[:, :, 0, :].bitcast(F32)).then_inc(qs_lo, 1)
            if a:
                part_max(j, k, 3)
                dve.wait_ge(max_part, 4 * j + 4)
                dve.tensor_reduce(sneg[:, 0:1], smax[:, :], AX.X, ALU.max, negate=True).then_inc(self_max, 1)
            if c:
                dve.wait_ge(xexp, 8 * (j - 1))
                dve.tensor_tensor(xcoef[:, 2, :], xden[:, 0, :], xden[:, 1, :], ALU.add).then_inc(o_step, 1)
                dve.wait_ge(o_step, 3 * (j - 1) - 2)
                dve.reciprocal(xcoef[:, 0, :], xcoef[:, 2, :]).then_inc(o_step, 1)
                dve.wait_ge(o_step, 3 * (j - 1) - 1)
                dve.tensor_scalar(xcoef[:, 1, :], xcoef[:, 0, :], v_scale[:, 1:2], None, ALU.mult).then_inc(o_step, 1)
                cross_lo(j, k, 3, 0)
                cross_lo(j, k, 3, 1)
                cross_lo(j, k, 3, 2)
            if b:
                cross_max(j, k, 0, 0)
            if a:
                self_lo(j, k, 0)
            if c:
                cross_lo(j, k, 3, 3)
            if k == T:
                weights_lo(1)
            if a:
                self_lo(j, k, 1)
            if b:
                cross_max(j, k, 0, 1)
            if a:
                self_lo(j, k, 2)
            if c:
                dve.wait_ge(x_used, 16 * (j - 1))
                dve.tensor_reduce(o_tile[:, :, :], cross_out[:, :].rearrange("p (h two d) -> p h d two", h=H, two=2),
                                  AX.X, ALU.add).then_inc(o_summed, 1)
                dve.wait_ge(o_step, 3 * (j - 1))
                dve.wait_ge(o_summed, j - 1)
                dve.tensor_tensor(o_tile[:, :, :], o_tile[:, :, :],
                                  xcoef[:, 1, :].unsqueeze(2).broadcast_to([P, H, HD]), ALU.mult).then_inc(o_ready, 1)
            if k == T + 1:
                weights_lo(4)
            if b:
                cross_max(j, k, 1, 0)
            if a:
                self_lo(j, k, 3)
            if c:
                dve.wait_ge(ot_hi, j - 1)
                low(ot[:, 1, :, :], flip[:, bank(("o",)), 0:D].rearrange("p (c s) -> p c s", c=C),
                    ot[:, 0, :, :].bitcast(F32)).then_inc(ot_lo, 1)
            if a:
                dve.wait_ge(self_exp, 2 * j + 2)
                dve.tensor_tensor(ssum[:, :], sden[:, 0:1], sden[:, 1:2], ALU.add).then_inc(sum_ready, 1)
                dve.wait_ge(sum_ready, j + 1)
                dve.reciprocal(scoef[:, 0:1], ssum[:, :]).then_inc(coef_step, 1)
                dve.wait_ge(coef_step, 2 * j + 1)
                dve.wait_ge(norm_ready, j + 1)
                dve.tensor_tensor(scoef[:, 1:2], scoef[:, 0:1], norm_col[:, :], ALU.mult).then_inc(coef_step, 1)
            if b:
                cross_max(j, k, 1, 1)
            if c:
                dve.wait_ge(wo_ready, j - 1)
                dve.wait_ge(record_filled, j - 1)
                dve.tensor_tensor(record[:, 0:D], flip[:, bank(("wo",)), 0:D], record[:, 0:D], ALU.add).then_inc(x2_ready, 1)
                dve.wait_ge(x2_ready, j - 1)
                dve.bn_stats(bs3[:, :], record[:, 0:D]).then_inc(stats3, 1)
                dve.wait_ge(stats3, 2 * (j - 1) - 1)
                dve.bn_aggr(mv3[:, :], bs3[:, :]).then_inc(mean3, 1)
                dve.wait_ge(mean3, j - 1)
                dve.tensor_scalar(rs3[:, 0:1], mv3[:, 1:2], EPS, None, ALU.add).then_inc(stats3, 1)
            if k == T + 1:
                weights_lo(5)
            if b:
                cross_lo(j, k, 0, 0)
            if a:
                dve.wait_ge(coef_step, 2 * j + 2)
                dve.wait_ge(s_used, 4 * j + 4)
                dve.wait_ge(x_loaded, 16 * (j + 1))
                if k >= 1:
                    dve.wait_ge(x1_copied, j)
                dve.scalar_tensor_tensor(out=x1[:, :], in0=self_out[:, 0:D], scalar=scoef[:, 1:2], in1=x_tile[:, :],
                                         op0=ALU.mult, op1=ALU.add).then_inc(x1_ready, 1)
            if c:
                dve.wait_ge(rstd3, j - 1)
                dve.tensor_scalar(xn3[:, :], record[:, 0:D], mv3[:, 0:1], rs3[:, 1:2], ALU.subtract,
                                  ALU.mult).then_inc(xn3_ready, 1)
            if a:
                dve.wait_ge(x1_ready, j + 1)
                dve.bn_stats(bs1[:, :], x1[:, :]).then_inc(stats1, 1)
            if b:
                cross_lo(j, k, 0, 1)
                cross_lo(j, k, 0, 2)
                cross_lo(j, k, 0, 3)
            if k == T:
                weights_lo(2)
            if b:
                cross_max(j, k, 2, 0)
                cross_lo(j, k, 1, 0)
                cross_max(j, k, 2, 1)
                cross_lo(j, k, 1, 1)
            if c:
                gates(j, k, 0)
            if b:
                cross_lo(j, k, 1, 2)
            if c:
                gates(j, k, 1)
            if b:
                cross_max(j, k, 3, 0)
                cross_lo(j, k, 1, 3)
            if k == T:
                weights_lo(3)
            if c:
                gates(j, k, 2)
            if b:
                cross_max(j, k, 3, 1)
            if c:
                ranks(j, k)
            if a:
                dve.wait_ge(stats1, 2 * j + 1)
                dve.bn_aggr(mv1[:, :], bs1[:, :]).then_inc(mean1, 1)
            if b:
                cross_lo(j, k, 2, 0)
            if a:
                dve.wait_ge(mean1, j + 1)
                dve.tensor_scalar(rs1[:, 0:1], mv1[:, 1:2], EPS, None, ALU.add).then_inc(stats1, 1)
            if b:
                cross_lo(j, k, 2, 1)
            if a:
                dve.wait_ge(rstd1, j + 1)
                dve.tensor_scalar(xn[:, :], x1[:, :], mv1[:, 0:1], rs1[:, 1:2], ALU.subtract, ALU.mult).then_inc(xn_ready, 1)
            if c:
                destination(j, k)

        def pad_rows():
            dve.wait_ge(rank_used, T - 1)
            for n in range(2):
                dve.tensor_scalar(pad_f[:, n, :], seen[:, :], lane[:, 0:1], float(n * P), ALU.add, ALU.add).then_inc(pad_dest, 1)
            dve.wait_ge(pad_dest, 2)
            dve.tensor_copy(pad_i[:, :, :], pad_f[:, :, :]).then_inc(pad_dest_i, 1)

        def gates(j, k, part):
            def after(n):
                dve.wait_ge(gate_step, 6 * (j - 2) + n)

            if part == 0:
                dve.wait_ge(gate_ready, j - 1)
                dve.tensor_tensor(logits[:, :], flip[:, bank(("gate",)), 0:E], bg_row[:, :], ALU.add).then_inc(logits_ready, 1)
                dve.wait_ge(logits_ready, j - 1)
                dve.tensor_reduce(gsc[:, 0, 0:1], logits[:, :], AX.X, ALU.max).then_inc(gate_step, 1)
            elif part == 1:
                after(1)
                dve.scalar_tensor_tensor(out=gsc[:, 1, :], in0=logits[:, :], scalar=gsc[:, 0, 0:1], in1=expert_w[:, :],
                                         op0=ALU.is_equal, op1=ALU.mult).then_inc(gate_step, 1)
                after(2)
                dve.tensor_reduce(gsc[:, 2, 0:1], gsc[:, 1, :], AX.X, ALU.max).then_inc(gate_step, 1)
            else:
                after(3)
                dve.tensor_scalar(gsc[:, 3, 0:1], gsc[:, 2, 0:1], 0.0, float(E), ALU.is_equal, ALU.mult).then_inc(gate_step, 1)
                after(4)
                dve.tensor_tensor(gsc[:, 4, 0:1], gsc[:, 3, 0:1], gsc[:, 2, 0:1], ALU.add).then_inc(gate_step, 1)
                after(5)
                dve.tensor_scalar(onehot[:, :], expert_w[:, :], gsc[:, 4, 0:1], None, ALU.is_equal).then_inc(gate_step, 1)
                after(6)
                if k > 2:
                    dve.wait_ge(rank_ready, j - 2)
                dve.tensor_copy(onehot16[:, :], onehot[:, :]).then_inc(onehot_ready, 1)

        def ranks(j, k):
            dve.wait_ge(rank_ready, j - 1)
            dve.tensor_tensor(rank_e[:, :], flip[:, bank(("rank",)), 0:E], seen[:, :], ALU.add).then_inc(rank_added, 1)
            dve.wait_ge(rank_added, j - 1)
            dve.tensor_tensor(seen[:, :], flip[:, bank(("rank",)), E:2 * E], seen[:, :], ALU.add).then_inc(rank_used, 1)

        def destination(j, k):
            dve.tensor_tensor_reduce(gsc[:, 5, :], rank_e[:, :], onehot[:, :], 1.0, 0.0, ALU.mult, ALU.add,
                                     dest[:, 0:1]).then_inc(dest_step, 1)
            dve.wait_ge(dest_step, j - 1)
            if k > 2:
                dve.wait_ge(routed, 16 * (j - 2))
            dve.tensor_copy(dest_i[:, :], dest[:, :]).then_inc(dest_ready, 1)

        run_pipeline(dve, body)

        dve.tensor_copy(barrier[:, 2:3], ident[:, 0:1]).then_inc(attention_done, 2)
        steps = [0]

        def step(op):
            steps[0] += 1
            op.then_inc(table_step, 1)
            dve.wait_ge(table_step, steps[0])

        step(dve.tensor_tensor(count[:, :], seen[:, :], region_base[:, :], ALU.subtract))
        step(dve.tensor_tensor(over[:, :, :], count[:, :].unsqueeze(2).broadcast_to([P, E, T]), sixteenth[:, :].unsqueeze(1).broadcast_to([P, E, T]), ALU.is_gt))
        step(dve.tensor_reduce(need[:, :], over[:, :, :], AX.X, ALU.add))
        step(dve.tensor_copy(ends[:, 0:1], need[:, 0:1]))
        for e in range(1, E):
            step(dve.tensor_tensor(ends[:, e:e + 1], ends[:, e - 1:e], need[:, e:e + 1], ALU.add))
        step(dve.tensor_tensor(past[:, :, :], block_no[:, 0, :].unsqueeze(2).broadcast_to([P, BLOCKS, E]),
                               ends[:, :].unsqueeze(1).broadcast_to([P, BLOCKS, E]), ALU.is_ge))
        step(dve.tensor_reduce(tab[:, 0, :], past[:, :, :], AX.X, ALU.add))
        step(dve.tensor_tensor(past[:, :, :], past[:, :, :], need[:, :].unsqueeze(1).broadcast_to([P, BLOCKS, E]), ALU.mult))
        step(dve.tensor_reduce(tab[:, 1, :], past[:, :, :], AX.X, ALU.add))
        step(dve.scalar_tensor_tensor(out=tab[:, 2, :], in0=tab[:, 0, :], scalar=float(REGION), in1=block_no[:, 1, :],
                                      op0=ALU.mult, op1=ALU.add))
        step(dve.scalar_tensor_tensor(out=tab[:, 3, :], in0=tab[:, 1, :], scalar=-float(P), in1=tab[:, 2, :],
                                      op0=ALU.mult, op1=ALU.add))
        dve.tensor_copy(table[:, 0, :], tab[:, 3, :]).then_inc(table_ready, 1)
        step(dve.tensor_scalar(tab[:, 4, :], tab[:, 0, :], float(E - 1), float(DF), ALU.min, ALU.mult))
        dve.tensor_copy(table[:, 1, :], tab[:, 4, :]).then_inc(table_ready, 1)
        dve.wait_ge(table_ready, 2)
        step(dve.tensor_scalar(tab[:, 4, :], tab[:, 0, :], float(E - 1), float(D), ALU.min, ALU.mult))
        dve.tensor_copy(table[:, 2, :], tab[:, 4, :]).then_inc(table_ready, 1)
        dve.wait_ge(table_ready, 3)

        dve.wait_ge(attention_done, 3)
        dve.wait_ge(b_loaded, 32)

        def statistics(b, k):
            dve.wait_ge(rows_loaded, 16 * (b + 1))
            if k >= 1:
                dve.wait_ge(f_mean, b)
            dve.bn_stats(bs_f[:, :], rows[:, k % RING, 0:D]).then_inc(f_stats, 1)
            dve.wait_ge(f_stats, b + 1)
            if k >= 1:
                dve.wait_ge(f_xn, b)
            dve.bn_aggr(mv_f[:, :], bs_f[:, :]).then_inc(f_mean, 1)
            dve.wait_ge(f_mean, b + 1)
            if k >= 1:
                dve.wait_ge(f_rstd, b)
            dve.tensor_scalar(rs_f[:, 0:1], mv_f[:, 1:2], EPS, None, ALU.add).then_inc(f_eps, 1)

        def normalise(b, k):
            dve.wait_ge(f_rstd, b + 1)
            if k >= 1:
                dve.wait_ge(f_x_flipped, b)
            dve.tensor_scalar(xn_f[:, :], rows[:, k % RING, 0:D], mv_f[:, 0:1], rs_f[:, 1:2], ALU.subtract,
                              ALU.mult).then_inc(f_xn, 1)

        def blocks(b, k):
            def x_lo_f(b):
                dve.wait_ge(f_xt_hi, b + 1)
                low(xt_f[:, 1, :, :], self_out[:, 0:D].rearrange("p (c s) -> p c s", c=C),
                    xt_f[:, 0, :, :].bitcast(F32)).then_inc(f_xt_lo, 1)

            if k == 0:
                statistics(0, 0)
                normalise(0, 0)
                x_lo_f(0)
                for n in range(E + 2, 2 * E):
                    weights_lo(n)
                statistics(b + 1, 1)
                normalise(b + 1, 1)
            if k >= 1:
                for n in range(2):
                    dve.wait_ge(f_ht_hi, 2 * (b - 1) + n + 1)
                    low(ht[:, 1, 4 * n:4 * n + 4, :], flip[:, n, :].rearrange("p (c s) -> p c s", c=4),
                        ht[:, 0, 4 * n:4 * n + 4, :].bitcast(F32)).then_inc(f_ht_lo, 1)
            if k < BLOCKS - 2:
                statistics(b + 2, k + 2)
            if k < BLOCKS:
                off = dve.value_load(table[0:1, 1, bass.ds(b, 1)], min_val=0, max_val=(E - 1) * DF)
                for n in range(2):
                    if k >= 1:
                        dve.wait_ge(f_h_flipped, 2 * (b - 1) + n + 1)
                    dve.wait_ge(f_h, 2 * b + n + 1)
                    dve.tensor_tensor(hidden[:, n * 512:(n + 1) * 512], scores[:, n, :],
                                      b1_row[:, bass.ds(off + n * 512, 512)], ALU.add).then_inc(f_bias, 1)
            if k < BLOCKS - 1:
                x_lo_f(b + 1)
            if k < BLOCKS - 2:
                normalise(b + 2, k + 2)
            if k >= 1:
                off2 = dve.value_load(table[0:1, 2, bass.ds(b - 1, 1)], min_val=0, max_val=(E - 1) * D)
                if k >= 2:
                    dve.wait_ge(f_out, b - 1)
                dve.tensor_tensor(base_f[:, :], rows[:, (k - 1) % RING, 0:D], b2_row[:, bass.ds(off2, D)],
                                  ALU.add).then_inc(f_base, 1)
                dve.wait_ge(f_base, b)
                dve.wait_ge(f_y, b)
                if k >= 3:
                    dve.wait_ge(f_stored, 16 * (b - 2))
                dve.tensor_tensor(out_f[:, (k - 1) % 2, :], cross_out[:, 0:D], base_f[:, :], ALU.add).then_inc(f_out, 1)
        run_blocks(dve, blocks)


def kernel(**inputs):
    import numpy as _np
    import concourse.bacc as _bacc
    from concourse import mybir as _mybir
    from concourse.bass_utils import run_bass_kernel_spmd as _run

    def array(name):
        return _np.asarray(inputs[name])

    laid_out = {
        "x": array("x")[0],
        "ctxT": array("ctx_1024")[0].T,
        "mask": array("mask_BxSxS2_bf1")[0].view(_np.uint8),
        "WqT": array("L0_attn_Wq").T,
        "AT": array("L0_attn_anomaly_matrix").T,
        "WvT": array("L0_attn_Wv").T,
        "bq": array("L0_attn_bq"),
        "bv": array("L0_attn_bv"),
        "xWq": array("L0_xattn_Wq"),
        "Wkv": array("L0_xattn_Wkv"),
        "Wo": array("L0_xattn_Wo"),
        "Wg": array("L0_ffn_Wg"),
        "bg": array("L0_ffn_bg"),
        "W1": array("L0_ffn_W1"),
        "b1": array("L0_ffn_b1"),
        "W2": array("L0_ffn_W2"),
        "b2": array("L0_ffn_b2"),
    }
    nc = _bacc.Bacc("TRN2", target_bir_lowering=False, num_devices=1)
    arrays, io = {}, {}
    for name, a in laid_out.items():
        arrays[name] = _np.ascontiguousarray(a)
        io[name] = nc.dram_tensor(name, arrays[name].shape, _mybir.dt.from_np(arrays[name].dtype), kind="ExternalInput").ap()
    io["out"] = nc.dram_tensor("out", (N, D), F32, kind="ExternalOutput").ap()
    build(nc, io)
    r = _run(nc, [arrays], core_ids=[0])
    return r.results[0]["out"].reshape(1, N, D)
```

```python
from contextlib import ExitStack

import numpy as np

import concourse.bass as bass
from concourse import mybir

ALU = mybir.AluOpType
ACT = mybir.ActivationFunctionType
AX = mybir.AxisListType
F32 = mybir.dt.float32
F32R = mybir.dt.float32r
F16 = mybir.dt.float16
BF16 = mybir.dt.bfloat16
U8 = mybir.dt.uint8
I32 = mybir.dt.int32
U32 = mybir.dt.uint32

P = 128
N = 2048
D = 256
C = D // P
T = N // P
M = 1601
H = 4
HD = D // H
KB = 402
MP = 4 * KB
MC = -(-M // P)
MLAST = M - (MC - 1) * P
NB = N // 512
E = 4
DF = 1024
FC = DF // P
EPS = 1e-5
PAD_BIAS = -3.38e38
MAX_CAP = 3.0e38
MASKED = 3.4e38
REGION = N + P
SPARE = E * REGION
REC = D + 4
BLOCKS = T + E - 1
XROWS = SPARE + E * P
V_TOP = 4096.0
XHALF = 2 * 512
RING = 4
NOBODY = 65536.0


NG = -(-MC // 4)
XG = [range(4 * g, min(4 * g + 4, MC)) for g in range(NG)]

BANKS = {("x", 2, 2): 0, ("x", 2, 3): 1, ("xn",): 2, ("x", 3, 0): 0, ("xq",): 2, ("qs",): 2,
         ("x", 3, 1): 1, ("x", 3, 2): 2, ("s", 0): 0, ("x", 3, 3): 1, ("s", 1): 2, ("s", 2): 0,
         ("sum",): 2, ("s", 3): 0, ("o",): 1, ("x", 0, 0): 0, ("wo",): 1, ("x", 0, 1): 1,
         ("x", 0, 2): 0, ("x", 0, 3): 2, ("x", 1, 0): 1, ("x", 1, 1): 0, ("x3",): 2, ("x", 1, 2): 1,
         ("gate",): 2, ("x", 1, 3): 0, ("x", 2, 0): 1, ("x", 2, 1): 2, ("rank",): 0}


def stage_of(use):
    if use[0] in ("s", "sum"):
        return 0
    if use[0] in ("xn", "xq", "qs") or (use[0] == "x" and (use[1] < 2 or use[1:] in ((2, 0), (2, 1)))):
        return 1
    return 2


def build(nc, io):
    with ExitStack() as ctx:
        emit(nc, io, ctx)


def emit(nc, io, ctx):
    def sb(name, shape, dt, on=None):
        return (on or ctx).enter_context(nc.sbuf_tensor(name, shape, dt))

    def sem(name):
        return ctx.enter_context(nc.semaphore(name))

    u_dram = nc.dram_tensor("u_dram", [T, P, 2 * C, P], F32, kind="Internal").ap()
    rows_dram = nc.dram_tensor("rows_dram", [XROWS, REC], F32, kind="Internal").ap()

    scores = ctx.enter_context(nc.psum_tensor("scores", [P, 4, 512], F32))
    flip = ctx.enter_context(nc.psum_tensor("flip", [P, 3, 512], F32))
    self_out = flip[:, 2, :]
    cross_out = ctx.enter_context(nc.psum_tensor("cross_out", [P, 512], F32))

    ident = sb("ident", [P, P], F32)
    barrier = sb("barrier", [P, 4], F32)
    below = sb("below", [P, P], BF16)
    ones = sb("ones", [P, P], BF16)
    minus_half = sb("minus_half", [P, T], F32)
    plus_half = sb("plus_half", [P, T], F32)
    token = sb("token", [P, 1], F32)
    expert_w = sb("expert_w", [P, E], F32)
    seen = sb("seen", [P, E], F32)
    norms = sb("norms", [P, T], F32)
    v_scale = sb("v_scale", [P, 2], F32)
    bg_row = sb("bg_row", [P, E], F32)
    wg = sb("wg", [P, C, E], F32)
    wq_cross = sb("wq_cross", [P, 2, C, D], F32R)
    wo_cross = sb("wo_cross", [P, 2, C, D], F32R)
    region_base = sb("region_base", [P, E], F32)
    lane = sb("lane", [P, 1], F32)
    sixteenth = sb("sixteenth", [P, T], F32)
    block_no = sb("block_no", [P, 2, BLOCKS], F32)

    count = sb("count", [P, E], F32)
    over = sb("over", [P, E, T], F32)
    pad_f = sb("pad_f", [P, 2, E], F32)
    pad_i = sb("pad_i", [P, 2, E], U32)
    need = sb("need", [P, E], F32)
    ends = sb("ends", [P, E], F32)
    past = sb("past", [P, BLOCKS, E], F32)
    tab = sb("tab", [P, 5, BLOCKS], F32)
    table = sb("table", [P, 3, BLOCKS], I32)

    ffn = ExitStack()
    w1s = sb("w1s", [P, 2, C, E * DF], F32R, ffn)
    w2s = sb("w2s", [P, 2, FC, E * D], F32R, ffn)
    w_stage = sb("w_stage", [P, 2, C * DF], F32, ffn)
    b1_row = sb("b1_row", [P, E * DF], F32, ffn)
    b2_row = sb("b2_row", [P, E * D], F32, ffn)
    rows = sb("rows", [P, RING, REC], F32, ffn)
    xn_f = sb("xn_f", [P, D], F32, ffn)
    xt_f = sb("xt_f", [P, 2, C, P], F32R, ffn)
    hidden = sb("hidden", [P, DF], F32, ffn)
    ht = sb("ht", [P, 2, FC, P], F32R, ffn)
    base_f = sb("base_f", [P, D], F32, ffn)
    out_f = sb("out_f", [P, 2, D], F32, ffn)
    who = sb("who", [P, RING, 1], U32, ffn)
    bs_f = sb("bs_f", [P, 6], F32, ffn)
    mv_f = sb("mv_f", [P, 2], F32, ffn)
    rs_f = sb("rs_f", [P, 2], F32, ffn)
    ffn.close()

    keep = ctx.enter_context(ExitStack())
    keys_self = sb("keys_self", [P, 2, C, N], F32R, keep)
    vals_self = sb("vals_self", [P, T, 2, D], F32R, keep)

    constants_set = sem("constants_set")
    s_wload = [sem(f"s_wload{i}") for i in range(8)]
    x_rows_loaded = [sem(f"x_rows_loaded{g}") for g in range(4)]
    biases_loaded = sem("biases_loaded")

    pro = ExitStack()
    w_raw = sb("w_raw", [P, 3, C, D], F32, pro)
    w_self = sb("w_self", [P, 3, 2, C, D], F32R, pro)
    x_all = sb("x_all", [P, T, D], F32, pro)
    xt_pro = sb("xt_pro", [P, 2, 2, C, 512], F32R, pro)
    u_out = sb("u_out", [P, 4, 2 * C, P], F32R, pro)
    v_tmp = sb("v_tmp", [P, 2, D], F32, pro)
    stats_pro = sb("stats_pro", [P, T, 6], F32, pro)
    mv_pro = sb("mv_pro", [P, T, 2], F32, pro)
    var_eps = sb("var_eps", [P, T], F32, pro)
    rstd_pro = sb("rstd_pro", [P, T], F32, pro)
    std_pro = sb("std_pro", [P, T], F32, pro)
    norm_eps = sb("norm_eps", [P, T], F32, pro)
    norm_inv = sb("norm_inv", [P, T], F32, pro)
    row_scale = sb("row_scale", [P, T], F32, pro)
    bq_col = sb("bq_col", [P, C], F32, pro)
    bv_row = sb("bv_row", [P, D], F32, pro)
    pro.close()
    keys_cross = sb("keys_cross", [P, 2, H, MP], F32R, keep)
    vals_cross = sb("vals_cross", [P, MC, H, 2, HD], F16, keep)

    pro2 = ExitStack()
    w2_raw = sb("w2_raw", [P, 4, C, D], F32, pro2)
    wk_dup = sb("wk_dup", [P, 2, C, H, 2, HD], F32R, pro2)
    wv_cross = sb("wv_cross", [P, 2, C, D], F32R, pro2)
    ctx_raw = sb("ctx_raw", [P, C, KB], F32, pro2)
    ctx_t = sb("ctx_t", [P, 2, C, MP], F32R, pro2)
    v_f32 = sb("v_f32", [P, MC, D], F32, pro2)
    v_max = sb("v_max", [P, 2, 4], F32, pro2)
    v_top = sb("v_top", [P, 2], F32, pro2)
    pro2.close()

    loop = ExitStack()
    u_tile = sb("u_tile", [P, 2 * C, P], F32R, loop)
    x_tile = sb("x_tile", [P, D], F32, loop)
    exp_self = sb("exp_self", [P, N], F32, loop)
    ps_self = sb("ps_self", [P, 4, 2, 512], F32R, loop)
    mask_tile = sb("mask_tile", [P, M], U8, loop)
    mask_bias = sb("mask_bias", [P, MP], BF16, loop)
    exp_cross = sb("exp_cross", [P, 2, MP], F32, loop)
    ps_cross = sb("ps_cross", [P, 4, 2, 512], F16, loop)
    x1 = sb("x1", [P, D], F32, loop)
    x1_old = sb("x1_old", [P, D], F32, loop)
    xn = sb("xn", [P, D], F32, loop)
    xt = sb("xt", [P, 2, C, P], F32R, loop)
    qs = sb("qs", [P, H, 2, HD], F32R, loop)
    qt = sb("qt", [P, H, P], F32R, loop)
    o_tile = sb("o_tile", [P, H, HD], F32, loop)
    ot = sb("ot", [P, 2, C, P], F32R, loop)
    xn3 = sb("xn3", [P, D], F32, loop)
    x3t = sb("x3t", [P, C, P], F32, loop)
    bs1 = sb("bs1", [P, 6], F32, loop)
    mv1 = sb("mv1", [P, 2], F32, loop)
    rs1 = sb("rs1", [P, 2], F32, loop)
    bs3 = sb("bs3", [P, 6], F32, loop)
    mv3 = sb("mv3", [P, 2], F32, loop)
    rs3 = sb("rs3", [P, 2], F32, loop)
    norm_col = sb("norm_col", [P, 1], F32, loop)
    smax = sb("smax", [P, NB], F32, loop)
    sneg = sb("sneg", [P, 1], F32, loop)
    sden = sb("sden", [P, 2], F32, loop)
    ssum = sb("ssum", [P, 1], F32, loop)
    scoef = sb("scoef", [P, 2], F32, loop)
    xneg = sb("xneg", [P, 2, 2], F32, loop)
    xden = sb("xden", [P, 2, H], F32, loop)
    xcoef = sb("xcoef", [P, 3, H], F32, loop)
    logits = sb("logits", [P, E], F32, loop)
    gsc = sb("gsc", [P, 6, E], F32, loop)
    onehot = sb("onehot", [P, E], F32, loop)
    onehot16 = sb("onehot16", [P, E], BF16, loop)
    rank_e = sb("rank_e", [P, E], F32, loop)
    record = sb("record", [P, REC], F32, loop)
    pads = sb("pads", [P, REC], F32, loop)
    dest = sb("dest", [P, 1], F32, loop)
    dest_i = sb("dest_i", [P, 1], U32, loop)
    loop.close()

    self_w_loaded = sem("self_w_loaded")
    pro_stats = sem("pro_stats")
    pro_powers = sem("pro_powers")
    pro_var_ready = sem("pro_var_ready")
    rows_scaled = sem("rows_scaled")
    self_w_hi = sem("self_w_hi")
    self_w_lo = sem("self_w_lo")
    pro_flipped = sem("pro_flipped")
    pro_xt_hi = sem("pro_xt_hi")
    pro_xt_lo = sem("pro_xt_lo")
    pro_q_ready = sem("pro_q_ready")
    pro_q_hi = sem("pro_q_hi")
    pro_q_lo = sem("pro_q_lo")
    pro_u_ready = sem("pro_u_ready")
    u_hi_ready = sem("u_hi_ready")
    u_lo_ready = sem("u_lo_ready")
    u_stored = sem("u_stored")
    pro_v_ready = sem("pro_v_ready")
    pro_v_biased = sem("pro_v_biased")
    pro_v_hi = sem("pro_v_hi")
    pro_v_lo = sem("pro_v_lo")
    prologue_done = sem("prologue_done")
    cross_w_loaded = sem("cross_w_loaded")
    cross_w_hi = sem("cross_w_hi")
    cross_w_lo = sem("cross_w_lo")
    ctx_loaded = sem("ctx_loaded")
    ctx_hi = sem("ctx_hi")
    ctx_lo = sem("ctx_lo")
    cross_k_ready = sem("cross_k_ready")
    cross_k_hi = sem("cross_k_hi")
    cross_k_lo = sem("cross_k_lo")
    cross_v_ready = sem("cross_v_ready")
    cross_v_copied = sem("cross_v_copied")
    v_max_part = sem("v_max_part")
    v_top_ready = sem("v_top_ready")
    norm_step = sem("norm_step")
    v_pool_step = sem("v_pool_step")
    v_scale_step = sem("v_scale_step")
    cross_v_hi = sem("cross_v_hi")
    cross_v_lo = sem("cross_v_lo")

    u_loaded = sem("u_loaded")
    x_loaded = sem("x_loaded")
    mask_loaded = sem("mask_loaded")
    scores_ready = sem("scores_ready")
    max_part = sem("max_part")
    self_max = sem("self_max")
    self_exp = sem("self_exp")
    sum_ready = sem("sum_ready")
    self_flipped = sem("self_flipped")
    self_p_hi = sem("self_p_hi")
    self_p_lo = sem("self_p_lo")
    self_p_used = sem("self_p_used")
    norm_ready = sem("norm_ready")
    coef_step = sem("coef_step")
    x1_ready = sem("x1_ready")
    stats1 = sem("stats1")
    rstd1 = sem("rstd1")
    xn_ready = sem("xn_ready")
    xn_flipped = sem("xn_flipped")
    xt_hi = sem("xt_hi")
    xt_lo = sem("xt_lo")
    q_ready = sem("q_ready")
    qs_hi = sem("qs_hi")
    qs_lo = sem("qs_lo")
    q_flipped = sem("q_flipped")
    qt_ready = sem("qt_ready")
    bias_ready = sem("bias_ready")
    cross_scores_ready = sem("cross_scores_ready")
    cross_max_half = sem("cross_max_half")
    cross_max_ready = sem("cross_max_ready")
    cross_exp_ready = sem("cross_exp_ready")
    cross_flipped = sem("cross_flipped")
    cross_p_hi = sem("cross_p_hi")
    cross_p_lo = sem("cross_p_lo")
    cross_p_used = sem("cross_p_used")
    o_summed = sem("o_summed")
    o_step = sem("o_step")
    o_ready = sem("o_ready")
    o_flipped = sem("o_flipped")
    ot_hi = sem("ot_hi")
    ot_lo = sem("ot_lo")
    wo_ready = sem("wo_ready")
    x2_ready = sem("x2_ready")
    x1_copied = sem("x1_copied")
    record_filled = sem("record_filled")
    stats3 = sem("stats3")
    mean1 = sem("mean1")
    mean3 = sem("mean3")
    rstd3 = sem("rstd3")
    xn3_ready = sem("xn3_ready")
    x3_flipped = sem("x3_flipped")
    x3t_ready = sem("x3t_ready")
    gate_ready = sem("gate_ready")
    logits_ready = sem("logits_ready")
    gate_step = sem("gate_step")
    onehot_ready = sem("onehot_ready")
    rank_ready = sem("rank_ready")
    rank_added = sem("rank_added")
    rank_used = sem("rank_used")
    dest_step = sem("dest_step")
    dest_ready = sem("dest_ready")
    token_set = sem("token_set")
    token_next = sem("token_next")
    routed = sem("routed")
    padding_set = sem("padding_set")
    spare_stored = sem("spare_stored")

    gelu_table = sem("gelu_table")
    attention_done = sem("attention_done")
    pad_dest = sem("pad_dest")
    pad_dest_i = sem("pad_dest_i")
    pads_out = sem("pads_out")
    table_step = sem("table_step")
    table_ready = sem("table_ready")
    w_loaded = [sem("w_loaded_even"), sem("w_loaded_odd")]
    b_loaded = sem("b_loaded")
    w_hi = sem("w_hi")
    w_lo = sem("w_lo")
    rows_loaded = sem("rows_loaded")
    f_stats = sem("f_stats")
    f_mean = sem("f_mean")
    f_eps = sem("f_eps")
    f_rstd = sem("f_rstd")
    f_xn = sem("f_xn")
    f_who = sem("f_who")
    f_x_flipped = sem("f_x_flipped")
    f_xt_hi = sem("f_xt_hi")
    f_xt_lo = sem("f_xt_lo")
    f_h = sem("f_h")
    f_bias = sem("f_bias")
    f_gelu = sem("f_gelu")
    f_h_flipped = sem("f_h_flipped")
    f_ht_hi = sem("f_ht_hi")
    f_ht_lo = sem("f_ht_lo")
    f_y = sem("f_y")
    f_base = sem("f_base")
    f_out = sem("f_out")
    f_stored = sem("f_stored")

    def bank(use):
        return BANKS[use]

    GROUPS = N // 512

    def value_chunks(n):
        return range(MC * n // (2 * H), MC * (n + 1) // (2 * H))

    block = ctx.enter_context(nc.Block())

    CONSTANTS = 15

    MIDDLE = 5

    def run_pipeline(eng, body):
        for j in (0, 1, 2):
            body(j, j)
        with eng.Fori(3, T - 1) as j:
            body(j, MIDDLE)
        for j in (T - 1, T, T + 1):
            body(j, j)

    def run_blocks(eng, body):
        for b in range(RING + 1):
            body(b, b)
        with eng.Fori(RING + 1, BLOCKS - 1 - RING, RING) as b:
            for n in range(RING):
                body(b + n, RING + 1 + n)
        for b in (BLOCKS - 2, BLOCKS - 1, BLOCKS):
            body(b, b)

    @block.sync
    def _(sp):
        x_rows = io["x"].rearrange("(t p) d -> p t d", p=P)
        sp.dma_start(x_all[:, 0:4, :], x_rows[:, 0:4, :]).then_inc(x_rows_loaded[0], 16)
        for n, w in enumerate(("WqT", "WvT", "AT")):
            sp.dma_start(w_raw[:, n, :, :], io[w].rearrange("(c p) n -> p c n", p=P)).then_inc(self_w_loaded, 16)
        for g in range(1, 4):
            sp.dma_start(x_all[:, 4 * g:4 * g + 4, :], x_rows[:, 4 * g:4 * g + 4, :]).then_inc(x_rows_loaded[g], 16)
        sp.dma_start(bq_col[:, :], io["bq"].rearrange("(c p) -> p c", p=P), allow_slow_non_contiguous=True).then_inc(
            biases_loaded, 16)
        sp.dma_start(bv_row[:, :], bass.AP(io["bv"].tensor, 0, [[0, P], [1, D]])).then_inc(biases_loaded, 16)
        sp.dma_start(bg_row[:, :], bass.AP(io["bg"].tensor, 0, [[0, P], [1, E]])).then_inc(biases_loaded, 16)
        sp.dma_start(wg[:, :, :], io["Wg"].rearrange("(c p) e -> p c e", p=P)).then_inc(biases_loaded, 16)
        wkv = io["Wkv"].rearrange("(c p) n -> p c n", p=P)
        sp.dma_start(w2_raw[:, 0, :, :], wkv[:, :, 0:D]).then_inc(cross_w_loaded, 16)
        sp.dma_start(w2_raw[:, 1, :, :], wkv[:, :, D:2 * D]).then_inc(cross_w_loaded, 16)
        sp.dma_start(w2_raw[:, 2, :, :], io["xWq"].rearrange("(c p) n -> p c n", p=P)).then_inc(cross_w_loaded, 16)
        sp.dma_start(w2_raw[:, 3, :, :], io["Wo"].rearrange("(c p) n -> p c n", p=P)).then_inc(cross_w_loaded, 16)
        def store_u(g):
            sp.wait_ge(u_lo_ready, C * (g + 1))
            sp.wait_ge(u_hi_ready, C * (g + 1))
            sp.dma_start(u_dram[4 * g:4 * g + 4].rearrange("t p c s -> p t c s"), u_out[:, :, :, :].bitcast(F32)).then_inc(
                u_stored, 16)

        ctx_v = io["ctxT"].rearrange("(c p) m -> p c m", p=P)
        for g in range(GROUPS):
            lo, hi = g * KB, min((g + 1) * KB, M)
            if g:
                sp.wait_ge(ctx_lo, g)
            sp.dma_start(ctx_raw[:, :, 0:hi - lo], ctx_v[:, :, lo:hi]).then_inc(ctx_loaded, 16)
            if g:
                store_u(g - 1)
        store_u(GROUPS - 1)
        sp.wait_ge(u_stored, 16 * GROUPS)
        sp.wait_ge(cross_w_lo, 4)
        def loads_a(t):
            sp.dma_start(u_tile[:, :, :].bitcast(F32), u_dram[bass.ds(t, 1), :, :, :].rearrange("a p c s -> p (a c) s")).then_inc(
                u_loaded, 16)

        def loads_x(t):
            sp.dma_start(x_tile[:, :], io["x"][bass.ds(t * P, P), :]).then_inc(x_loaded, 16)

        def loads_m(t):
            sp.dma_start(mask_tile[:, :], io["mask"][bass.ds(t * P, P), :]).then_inc(mask_loaded, 16)

        loads_a(0)
        loads_x(0)
        sp.wait_ge(prologue_done, 3)
        loads_m(0)

        def body(j, k):
            if 1 <= k <= T - 1:
                sp.wait_ge(bias_ready, j)
                loads_m(j)
            if k < T - 1:
                sp.wait_ge(scores_ready, 4 * j + 4)
                loads_a(j + 1)
                sp.wait_ge(x1_ready, j + 1)
                loads_x(j + 1)
        run_pipeline(sp, body)

        sp.wait_ge(x1_ready, T)
        for n in range(2 * E):
            e = n % E
            if n >= 2:
                sp.wait_ge(w_hi, n - 1)
                sp.wait_ge(w_lo, n - 1)
            if n < E:
                sp.dma_start(w_stage[:, n % 2, :].rearrange("p (c n) -> p c n", c=C),
                             io["W1"][e].rearrange("(c p) n -> p c n", p=P)).then_inc(w_loaded[n % 2], 16)
            else:
                sp.dma_start(w_stage[:, n % 2, :].rearrange("p (c n) -> p c n", c=FC),
                             io["W2"][e].rearrange("(c p) n -> p c n", p=P)).then_inc(w_loaded[n % 2], 16)
            if n == E + 1:
                sp.wait_ge(cross_p_used, 16 * T)
                sp.dma_start(b2_row[:, :], bass.AP(io["b2"].tensor, 0, [[0, P], [1, E * D]])).then_inc(b_loaded, 16)
                sp.dma_start(b1_row[:, :], bass.AP(io["b1"].tensor, 0, [[0, P], [1, E * DF]])).then_inc(b_loaded, 16)

        sp.wait_ge(spare_stored, 16 * E)
        sp.wait_ge(routed, 16 * T)
        sp.wait_ge(table_ready, 3)

        def load_rows(b, k):
            if k >= 1:
                sp.wait_ge(rows_loaded, 16 * b)
            row = sp.value_load(table[0:1, 0, bass.ds(b, 1)], min_val=0, max_val=XROWS - P)
            sp.dma_start(rows[:, k % RING, :], rows_dram[bass.ds(row, P), :]).then_inc(rows_loaded, 16)

        for b in range(2):
            load_rows(b, b)

        def blocks(b, k):
            if k < BLOCKS - 2:
                if k >= 2:
                    sp.wait_ge(f_base, b - 1)
                    sp.wait_ge(f_who, b - 1)
                load_rows(b + 2, k + 2)
        run_blocks(sp, blocks)
        sp.wait_ge(f_stored, 16 * BLOCKS)

    @block.gpsimd
    def _(pool):
        pool.memset(ident[:, :], 0.0).then_inc(constants_set, 1)
        pool.memset(below[:, :], 1.0).then_inc(constants_set, 1)
        pool.memset(ones[:, :], 1.0).then_inc(constants_set, 1)
        pool.memset(minus_half[:, :], -0.5).then_inc(constants_set, 1)
        pool.memset(plus_half[:, :], 0.5).then_inc(constants_set, 1)
        pool.iota(token[:, :], pattern=[[0, 1]], base=0, channel_multiplier=1,
                  allow_small_or_imprecise_dtypes=True).then_inc(constants_set, 1)
        pool.iota(expert_w[:, :], pattern=[[-1, E]], base=E, channel_multiplier=0,
                  allow_small_or_imprecise_dtypes=True).then_inc(constants_set, 1)
        pool.iota(seen[:, :], pattern=[[REGION, E]], base=0, channel_multiplier=0,
                  allow_small_or_imprecise_dtypes=True).then_inc(constants_set, 1)
        pool.iota(region_base[:, :], pattern=[[REGION, E]], base=0, channel_multiplier=0,
                  allow_small_or_imprecise_dtypes=True).then_inc(constants_set, 1)
        pool.iota(lane[:, :], pattern=[[0, 1]], base=0, channel_multiplier=1,
                  allow_small_or_imprecise_dtypes=True).then_inc(constants_set, 1)
        pool.iota(sixteenth[:, :], pattern=[[P, T]], base=0, channel_multiplier=0,
                  allow_small_or_imprecise_dtypes=True).then_inc(constants_set, 1)
        pool.iota(block_no[:, 0, :], pattern=[[1, BLOCKS]], base=0, channel_multiplier=0,
                  allow_small_or_imprecise_dtypes=True).then_inc(constants_set, 1)
        pool.iota(block_no[:, 1, :], pattern=[[P, BLOCKS]], base=0, channel_multiplier=0,
                  allow_small_or_imprecise_dtypes=True).then_inc(constants_set, 1)
        pool.wait_ge(constants_set, 2)
        pool.affine_select(out=ident[:, :], in_=ident[:, :], compare_op=ALU.not_equal, fill=1.0, base=0,
                           pattern=[[-1, P]], channel_multiplier=1).then_inc(constants_set, 1)
        pool.affine_select(out=below[:, :], in_=below[:, :], compare_op=ALU.is_gt, fill=0.0, base=0,
                           pattern=[[1, P]], channel_multiplier=-1).then_inc(constants_set, 1)
        pool.memset(v_f32[:, MC - 1, :], 0.0).then_inc(v_pool_step, 1)
        pool.wait_ge(constants_set, CONSTANTS)
        for g in range(4):
            cols = slice(4 * g, 4 * g + 4)
            pool.wait_ge(pro_var_ready, g + 1)
            pool.tensor_tensor(rstd_pro[:, cols], var_eps[:, cols], minus_half[:, cols], ALU.pow).then_inc(
                pro_powers, 1)
            pool.tensor_tensor(std_pro[:, cols], mv_pro[:, cols, 1], plus_half[:, cols], ALU.pow).then_inc(
                pro_powers, 1)
        pool.wait_ge(v_max_part, 4)
        pool.partition_all_reduce(v_max[:, 1, :], v_max[:, 0, :], P, bass.bass_isa.ReduceOp.max).then_inc(
            v_pool_step, 1)

        pool.wait_ge(prologue_done, 3)
        pool.memset(mask_bias[:, M:MP], PAD_BIAS).then_inc(padding_set, 1)
        pool.memset(pads[:, :], 0.0).then_inc(padding_set, 1)
        pool.wait_ge(padding_set, 2)
        pool.memset(pads[:, D:REC], NOBODY).then_inc(padding_set, 1)
        pool.memset(record[:, D + 1:REC], 0.0).then_inc(padding_set, 1)
        pool.wait_ge(padding_set, 4)
        for n in range(E):
            pool.dma_start(rows_dram[SPARE + n * P:SPARE + (n + 1) * P, :], pads[:, :]).then_inc(spare_stored, 16)

        def body(j, k):
            a, b, c = k < T, 1 <= k <= T, k >= 2
            if c:
                if k > 2:
                    pool.wait_ge(routed, 16 * (j - 2))
                pool.wait_ge(x1_copied, j - 1)
                pool.tensor_copy(record[:, 0:D], x1_old[:, :]).wait_op(
                    constants_set, CONSTANTS, "sem-ge").then_inc(record_filled, 1)
            if b:
                if c:
                    pool.wait_ge(record_filled, j - 1)
                pool.wait_ge(x1_ready, j)
                pool.tensor_copy(x1_old[:, :], x1[:, :]).wait_op(
                    constants_set, CONSTANTS, "sem-ge").then_inc(x1_copied, 1)
                if c:
                    pool.wait_ge(cross_max_ready, 4 * (j - 1))
                pool.wait_ge(mask_loaded, 16 * j)
                pool.tensor_scalar(mask_bias[:, 0:M], mask_tile[:, :], -1.0, MASKED, ALU.add, ALU.mult).wait_op(
                    constants_set, CONSTANTS, "sem-ge").then_inc(bias_ready, 1)
            if k == T + 1:
                for n in range(2):
                    for e in range(E):
                        pool.wait_ge(pad_dest_i, 1)
                        pool.indirect_dma_start(out=rows_dram[:, :],
                                                out_offset=bass.IndirectOffsetOnAxis(ap=pad_i[:, n, e:e + 1], axis=0),
                                                in_=pads[:, :], in_offset=None).then_inc(pads_out, 16)
            if a:
                if b:
                    pool.wait_ge(coef_step, 2 * j)
                pool.tensor_copy(norm_col[:, :], norms[:, bass.ds(j, 1)]).wait_op(
                    constants_set, CONSTANTS, "sem-ge").then_inc(norm_ready, 1)
            if c:
                pool.wait_ge(stats3, 2 * (j - 1))
                pool.tensor_tensor(rs3[:, 1:2], rs3[:, 0:1], minus_half[:, 0:1], ALU.pow).then_inc(rstd3, 1)
            if a:
                pool.wait_ge(stats1, 2 * j + 2)
                pool.tensor_tensor(rs1[:, 1:2], rs1[:, 0:1], minus_half[:, 0:1], ALU.pow).then_inc(rstd1, 1)
            if c:
                if k > 2:
                    pool.wait_ge(token_next, j - 2)
                pool.tensor_copy(record[:, D:D + 1], token[:, :]).wait_op(
                    constants_set, CONSTANTS, "sem-ge").then_inc(token_set, 1)
                pool.wait_ge(token_set, j - 1)
                pool.tensor_scalar(token[:, :], token[:, :], float(P), 1.0, ALU.add, ALU.mult).wait_op(
                    constants_set, CONSTANTS, "sem-ge").then_inc(token_next, 1)
                pool.wait_ge(x2_ready, j - 1)
                pool.wait_ge(dest_ready, j - 1)
                if k == T + 1:
                    pool.wait_ge(pads_out, 16 * 2 * E)
                pool.indirect_dma_start(out=rows_dram[:, :], out_offset=bass.IndirectOffsetOnAxis(ap=dest_i[:, 0:1], axis=0),
                                        in_=record[:, :], in_offset=None).wait_op(
                                            constants_set, CONSTANTS, "sem-ge").then_inc(routed, 16)
        run_pipeline(pool, body)

        last_row = pool.to_reg(N - 1)

        def blocks(b, k):
            def norm(b, k):
                pool.wait_ge(f_eps, b + 1)
                pool.tensor_tensor(rs_f[:, 1:2], rs_f[:, 0:1], minus_half[:, 0:1], ALU.pow).then_inc(f_rstd, 1)
                if k >= RING:
                    pool.wait_ge(f_stored, 16 * (b - RING + 1))
                pool.wait_ge(rows_loaded, 16 * (b + 1))
                pool.tensor_copy(who[:, k % RING, :], rows[:, k % RING, D:D + 1]).wait_op(
                    constants_set, CONSTANTS, "sem-ge").then_inc(f_who, 1)

            if k == 0:
                norm(0, 0)
                norm(1, 1)
            if k < BLOCKS - 2:
                norm(b + 2, k + 2)
            if k >= 1:
                if k >= 2:
                    pool.wait_ge(f_stored, 16 * (b - 1))
                pool.wait_ge(f_who, b)
                pool.wait_ge(f_out, b)
                pool.indirect_dma_start(out=io["out"][:, :],
                                        out_offset=bass.IndirectOffsetOnAxis(ap=who[:, (k - 1) % RING, 0:1], axis=0),
                                        in_=out_f[:, (k - 1) % 2, :], in_offset=None, bounds_check=last_row,
                                        oob_is_err=False).wait_op(
                                            constants_set, CONSTANTS, "sem-ge").then_inc(f_stored, 16)
        run_blocks(pool, blocks)

    @block.tensor
    def _(pe):
        def three(out, lhs, rhs, first=True, last=True):
            n = 0
            for c in range(C):
                for a, b in ((0, 0), (0, 1), (1, 0)):
                    mm = pe.matmul(out, lhs(a, c), rhs(b, c), start=(n == 0 and first), stop=(n == 3 * C - 1 and last))
                    n += 1
            return mm

        def self_u(g):
            for o in range(C):
                if g == 0:
                    pe.wait_ge(self_w_lo, 3)
                pe.wait_ge(pro_q_lo, C * (g + 1))
                if g:
                    pe.wait_ge(u_lo_ready, C * (g - 1) + o + 1)
                out = self_out if o == 0 else cross_out
                three(out[:, :], lambda a, c: w_self[:, 2, a, c, o * P:(o + 1) * P],
                      lambda b, c: keys_self[:, b, c, g * 512:(g + 1) * 512]).then_inc(pro_u_ready, 1)

        pe.wait_ge(constants_set, CONSTANTS)
        def flip_x_pro(g):
            for c in range(C):
                pe.wait_ge(rows_scaled, 4 * (g + 1))
                if g:
                    pe.wait_ge(pro_xt_lo, C * (g - 1) + c + 1)
                for n in range(4):
                    tr = pe.transpose(flip[:, c, n * P:(n + 1) * P], x_all[:, 4 * g + n, c * P:(c + 1) * P], ident[:, :])
                tr.then_inc(pro_flipped, 1)

        flip_x_pro(0)
        for g in range(GROUPS):
            if g == 0:
                pe.wait_ge(self_w_lo, 1)
            pe.wait_ge(pro_xt_lo, C * (g + 1))
            for o in range(C):
                if g:
                    pe.wait_ge(pro_q_lo, C * (g - 1) + o + 1)
                three(scores[:, o, :], lambda a, c: w_self[:, 0, a, c, o * P:(o + 1) * P],
                      lambda b, c: xt_pro[:, g % 2, b, c, :]).then_inc(pro_q_ready, 1)
            if g < GROUPS - 1:
                flip_x_pro(g + 1)
            if g == 0:
                pe.wait_ge(self_w_lo, 2)
            for n in range(4):
                if g and n % 2 == 0:
                    pe.wait_ge(pro_v_biased, 4 * (g - 1) + n + 2)
                three(scores[:, 2 + n // 2, (n % 2) * D:(n % 2 + 1) * D] , lambda a, c: xt_pro[:, g % 2, a, c, n * P:(n + 1) * P],
                      lambda b, c: w_self[:, 1, b, c, :]).then_inc(pro_v_ready, 1)
            self_u(g)

        for m in range(MC):
            rows = P if m < MC - 1 else MLAST
            if m == 0:
                pe.wait_ge(cross_w_lo, 2)
            pe.wait_ge(ctx_lo, (m * P + rows - 1) // KB + 1)
            if m >= 2:
                pe.wait_ge(cross_v_copied, m - 1)
            three(flip[0:rows, m % 2, 0:D], lambda a, c: ctx_t[:, a, c, m * P:m * P + rows],
                  lambda b, c: wv_cross[:, b, c, :]).then_inc(cross_v_ready, 1)
        for g in range(4):
            for h in range(H):
                if g:
                    pe.wait_ge(cross_k_lo, H * (g - 1) + h + 1)
                elif h < 2:
                    pe.wait_ge(pro_q_lo, C * GROUPS)
                else:
                    pe.wait_ge(pro_v_biased, 4 * GROUPS)
                three(scores[:, h, 0:KB], lambda a, c: wk_dup[:, a, c, h, :, :],
                      lambda b, c: ctx_t[:, b, c, g * KB:(g + 1) * KB]).then_inc(cross_k_ready, 1)

        pe.wait_ge(cross_k_lo, 4 * H)

        def self_scores(j, k, n):
            if n == 0:
                pe.wait_ge(u_loaded, 16 * (j + 1))
            if k >= 2:
                pe.wait_ge(cross_max_half if n < 2 else cross_max_ready, 4 * (j - 1))
            elif k == 1:
                pe.wait_ge(self_exp, 1 + n // 2)
            three(scores[:, n, :], lambda a, c: u_tile[:, a * C + c, :],
                  lambda b, c: keys_self[:, b, c, n * 512:(n + 1) * 512]).then_inc(scores_ready, 1)

        def self_flip(j, k, g):
            use = ("s", g)
            if g % 2 == 0:
                pe.wait_ge(self_exp, 2 * j + g // 2 + 1)
            for n in range(4):
                m = 4 * g + n
                tr = pe.transpose(flip[:, bank(use), n * P:(n + 1) * P], exp_self[:, m * P:(m + 1) * P], ident[:, :])
            tr.then_inc(self_flipped, 1)

        def self_values(j, k, g):
            pe.wait_ge(self_p_lo, 4 * j + g + 1)
            for n in range(4):
                m = 4 * g + n
                for a, b in ((0, 0), (0, 1), (1, 0)):
                    mm = pe.matmul(self_out[:, 0:D], ps_self[:, g, a, n * P:(n + 1) * P], vals_self[:, m, b, :],
                                   start=(m == 0 and a == 0 and b == 0), stop=(m == T - 1 and a == 1))
            mm.then_inc(self_p_used, 1)

        def cross_scores(j, k, h, half):
            if h == 0 and half == 0:
                pe.wait_ge(qt_ready, j)
            if h == 0 and k < T:
                pe.wait_ge(self_exp, 2 * j + half + 1)
            if h > 0 or k >= T:
                pe.wait_ge(cross_max_ready if half else cross_max_half, 4 * (j - 1) + h)
            for n in (2 * half, 2 * half + 1):
                for part in range(2):
                    mm = pe.matmul(scores[:, n, 0:KB], qt[:, h, :], keys_cross[:, part, h, n * KB:(n + 1) * KB],
                                   start=(part == 0), stop=(part == 1))
            mm.then_inc(cross_scores_ready, 1)

        def cross_flip(j, k, h, g):
            use = ("x", h, g)
            t = j - stage_of(use)
            if g % 2 == 0:
                pe.wait_ge(cross_exp_ready, 8 * t + 2 * h + g // 2 + 1)
            for n, m in enumerate(XG[g]):
                rows = P if m < MC - 1 else MLAST
                tr = pe.transpose(flip[0:rows, bank(use), n * P:(n + 1) * P], exp_cross[:, h % 2, m * P:m * P + rows], ident[:, :])
            tr.then_inc(cross_flipped, 1)

        def cross_values(j, k, h, g):
            t = j - (2 if (h, g) in ((2, 0), (2, 1)) else stage_of(("x", h, g)))
            pe.wait_ge(cross_p_lo, 16 * t + 4 * h + g + 1)
            if h == 0 and g == 0 and k >= 2:
                pe.wait_ge(o_summed, t)
            for n, m in enumerate(XG[g]):
                rows = P if m < MC - 1 else MLAST
                pe.matmul(cross_out[:, h * P:(h + 1) * P], ps_cross[0:rows, g, 0, n * P:(n + 1) * P],
                          vals_cross[0:rows, m, h, :, :], start=(m == 0), stop=False, skip_group_check=True)
                mm = pe.matmul(cross_out[:, h * P:h * P + HD], ps_cross[0:rows, g, 1, n * P:(n + 1) * P],
                               vals_cross[0:rows, m, h, 0, :], start=False, stop=(m == MC - 1), skip_group_check=True)
            mm.then_inc(cross_p_used, 1)

        def small(use, j, k, ready, value, filled, work):
            pe.wait_ge(ready, value)
            work(flip[:, bank(use), :]).then_inc(filled, 1)

        def flip_row(src):
            def work(out):
                for c in range(C):
                    tr = pe.transpose(out[:, c * P:(c + 1) * P], src[:, c * P:(c + 1) * P], ident[:, :])
                return tr
            return work

        def flip_queries(out):
            for h in range(H):
                tr = pe.transpose(out[:, h * P:(h + 1) * P], qs[:, h, :, :].bitcast(F32), ident[:, :])
            return tr

        def gate(out):
            for c in range(C):
                mm = pe.matmul(out[:, 0:E], x3t[:, c, :], wg[:, c, :], start=(c == 0), stop=(c == C - 1))
            return mm

        def rank(out):
            pe.matmul(out[:, 0:E], below[:, :], onehot16[:, :], start=True, stop=True)
            return pe.matmul(out[:, E:2 * E], ones[:, :], onehot16[:, :], start=True, stop=True)

        def body(j, k):
            a, b, c = k < T, 1 <= k <= T, k >= 2
            if a:
                self_scores(j, k, 0)
            if c:
                if k == 2:
                    pe.wait_ge(cross_p_lo, 16 * j - 24)
                else:
                    pe.wait_ge(rank_used, j - 2)
                cross_flip(j, k, 2, 2)
            if a:
                self_scores(j, k, 1)
            if c:
                pe.wait_ge(cross_p_lo, 16 * j - 23)
                cross_flip(j, k, 2, 3)
            if b:
                if k == 1:
                    pe.wait_ge(x1_ready, j)
                else:
                    pe.wait_ge(cross_p_lo, 16 * j - 22)
                small(("xn",), j, k, xn_ready, j, xn_flipped, flip_row(xn))
            if a:
                self_scores(j, k, 2)
            if c:
                pe.wait_ge(cross_p_lo, 16 * j - 21)
                cross_flip(j, k, 3, 0)
            if b:
                pe.wait_ge(xt_lo, j)
                small(("xq",), j, k, xt_lo, j, q_ready,
                      lambda out: three(out[:, 0:D], lambda a, c: xt[:, a, c, :], lambda b, c: wq_cross[:, b, c, :]))
            if a:
                self_scores(j, k, 3)
            if c:
                cross_values(j, k, 2, 0)
            if b:
                pe.wait_ge(qs_lo, j)
                small(("qs",), j, k, qs_lo, j, q_flipped, flip_queries)
            if c:
                cross_values(j, k, 2, 1)
                cross_values(j, k, 2, 2)
                cross_values(j, k, 2, 3)
                pe.wait_ge(cross_p_lo, 16 * j - 20)
                cross_flip(j, k, 3, 1)
                if k == T + 1:
                    pe.wait_ge(cross_p_lo, 16 * j - 22)
                else:
                    pe.wait_ge(qt_ready, j)
                cross_flip(j, k, 3, 2)
                cross_values(j, k, 3, 0)
            if b:
                cross_scores(j, k, 0, 0)
            if a:
                if k == 1:
                    pe.wait_ge(self_p_lo, 4 * j)
                elif k > 0:
                    pe.wait_ge(cross_p_lo, 16 * j - 19)
                self_flip(j, k, 0)
            if c:
                cross_values(j, k, 3, 1)
                pe.wait_ge(cross_p_lo, 16 * j - 18)
                cross_flip(j, k, 3, 3)
            if a:
                if k == 1:
                    pe.wait_ge(qt_ready, j)
                elif k > 0:
                    pe.wait_ge(cross_p_lo, 16 * j - 17)
                self_flip(j, k, 1)
            if b:
                cross_scores(j, k, 0, 1)
            if c:
                cross_values(j, k, 3, 2)
            if a:
                pe.wait_ge(self_p_lo, 4 * j + 1)
                self_flip(j, k, 2)
            if b:
                cross_scores(j, k, 1, 0)
            if c:
                cross_values(j, k, 3, 3)
            if a:
                pe.wait_ge(self_p_lo, 4 * j + 2)
                self_values(j, k, 0)
                pe.wait_ge(self_p_lo, 4 * j + 3)
                self_flip(j, k, 3)
            if b:
                cross_scores(j, k, 1, 1)
            if c:
                pe.wait_ge(cross_p_lo, 16 * j - 16)
                small(("o",), j, k, o_ready, j - 1, o_flipped, flip_row(o_tile[:, :, :].rearrange("p h d -> p (h d)")))
            if a:
                self_values(j, k, 1)
            if b:
                if k == T:
                    pe.wait_ge(cross_p_lo, 16 * j - 19)
                else:
                    pe.wait_ge(self_p_lo, 4 * j + 4)
                cross_flip(j, k, 0, 0)
            if c:
                pe.wait_ge(ot_lo, j - 1)
                small(("wo",), j, k, ot_lo, j - 1, wo_ready,
                      lambda out: three(out[:, 0:D], lambda a, c: ot[:, a, c, :], lambda b, c: wo_cross[:, b, c, :]))
            if a:
                self_values(j, k, 2)
                self_values(j, k, 3)
            if b:
                if k > 1:
                    pe.wait_ge(x2_ready, j - 1)
                cross_flip(j, k, 0, 1)
                pe.wait_ge(cross_p_lo, 16 * j - 15)
                cross_flip(j, k, 0, 2)
                cross_values(j, k, 0, 0)
                if k == T:
                    pe.wait_ge(cross_p_lo, 16 * j - 17)
                else:
                    pe.wait_ge(x1_ready, j + 1)
                cross_flip(j, k, 0, 3)
                cross_scores(j, k, 2, 0)
                cross_values(j, k, 0, 1)
                pe.wait_ge(cross_p_lo, 16 * j - 14)
                cross_flip(j, k, 1, 0)
                pe.wait_ge(cross_p_lo, 16 * j - 13)
                cross_flip(j, k, 1, 1)
            if c:
                if k == T + 1:
                    pe.wait_ge(cross_p_lo, 16 * j - 17)
                else:
                    pe.wait_ge(cross_p_lo, 16 * j - 12)
                small(("x3",), j, k, xn3_ready, j - 1, x3_flipped, flip_row(xn3))
            if b:
                cross_scores(j, k, 2, 1)
                cross_values(j, k, 0, 2)
                cross_values(j, k, 0, 3)
                pe.wait_ge(cross_p_lo, 16 * j - 11)
                cross_flip(j, k, 1, 2)
            if c:
                pe.wait_ge(x3t_ready, j - 1)
                small(("gate",), j, k, x3t_ready, j - 1, gate_ready, gate)
            if b:
                cross_values(j, k, 1, 0)
                cross_scores(j, k, 3, 0)
                pe.wait_ge(cross_p_lo, 16 * j - 10)
                cross_flip(j, k, 1, 3)
                cross_values(j, k, 1, 1)
                pe.wait_ge(cross_p_lo, 16 * j - 9)
                cross_flip(j, k, 2, 0)
                cross_scores(j, k, 3, 1)
                cross_values(j, k, 1, 2)
                if k == 1:
                    pe.wait_ge(cross_p_lo, 16 * j - 12)
                else:
                    pe.wait_ge(logits_ready, j - 1)
                cross_flip(j, k, 2, 1)
                cross_values(j, k, 1, 3)
            if c:
                if k == T + 1:
                    pe.wait_ge(cross_p_lo, 16 * j - 19)
                else:
                    pe.wait_ge(cross_p_lo, 16 * j - 8)
                small(("rank",), j, k, onehot_ready, j - 1, rank_ready, rank)
        run_pipeline(pe, body)
        pe.wait_ge(x2_ready, T)
        pe.wait_ge(table_ready, 3)

        def flip_x(b, k):
            pe.wait_ge(f_xn, b + 1)
            for c in range(C):
                tr = pe.transpose(self_out[:, c * P:(c + 1) * P], xn_f[:, c * P:(c + 1) * P], ident[:, :])
            tr.then_inc(f_x_flipped, 1)

        def blocks(b, k):
            if k == 0:
                flip_x(0, 0)
            if k >= 1:
                for n in range(2):
                    pe.wait_ge(f_gelu, 2 * (b - 1) + n + 1)
                    for c in range(4):
                        f = 4 * n + c
                        tr = pe.transpose(flip[:, n, c * P:(c + 1) * P], hidden[:, f * P:(f + 1) * P], ident[:, :])
                    tr.then_inc(f_h_flipped, 1)
            if k < BLOCKS:
                if k == 0:
                    pe.wait_ge(w_lo, E)
                pe.wait_ge(f_xt_lo, b + 1)
                off = pe.value_load(table[0:1, 1, bass.ds(b, 1)], min_val=0, max_val=(E - 1) * DF)
                for n in range(2):
                    three(scores[:, n, :], lambda a, c: xt_f[:, a, c, :],
                          lambda p, c: w1s[:, p, c, bass.ds(off + n * 512, 512)]).then_inc(f_h, 1)
            if k < BLOCKS - 1:
                flip_x(b + 1, k + 1)
            if k >= 1:
                if k == 1:
                    pe.wait_ge(w_lo, 2 * E)
                off2 = pe.value_load(table[0:1, 2, bass.ds(b - 1, 1)], min_val=0, max_val=(E - 1) * D)
                if k >= 2:
                    pe.wait_ge(f_out, b - 1)
                for f in range(FC):
                    if f % 4 == 0:
                        pe.wait_ge(f_ht_lo, 2 * (b - 1) + f // 4 + 1)
                    for a, p in ((0, 0), (0, 1), (1, 0)):
                        mm = pe.matmul(cross_out[:, 0:D], ht[:, a, f, :], w2s[:, p, f, bass.ds(off2, D)],
                                       start=(f == 0 and a == 0 and p == 0), stop=(f == FC - 1 and a == 1))
                mm.then_inc(f_y, 1)
        run_blocks(pe, blocks)

    @block.scalar
    def _(act):
        def copy(out, in_, **kw):
            return act.activation(out, in_, ACT.Copy, **kw)

        act.wait_ge(self_w_loaded, 16 * 3)
        for n in range(3):
            copy(w_self[:, n, 0, :, :], w_raw[:, n, :, :]).then_inc(self_w_hi, 1)

        def u_hi(g):
            for o in range(C):
                act.wait_ge(pro_u_ready, C * g + o + 1)
                if g:
                    act.wait_ge(u_stored, 16 * g)
                out = self_out if o == 0 else cross_out
                act.activation(u_out[:, :, o, :], out[:, :].rearrange("p (t s) -> p t s", t=4), ACT.Copy,
                               scale=1.0 / 16.0).then_inc(u_hi_ready, 1)

        def xt_hi_pro(g):
            for c in range(C):
                act.wait_ge(pro_flipped, C * g + c + 1)
                if g >= 2:
                    act.wait_ge(pro_v_ready, 4 * (g - 1))
                    act.wait_ge(pro_q_ready, C * (g - 1))
                copy(xt_pro[:, g % 2, 0, c, :], flip[:, c, :]).then_inc(pro_xt_hi, 1)

        xt_hi_pro(0)
        act.wait_ge(biases_loaded, 64)
        for g in range(GROUPS):
            for o in range(C):
                act.wait_ge(pro_q_ready, C * g + o + 1)
                act.activation(keys_self[:, 0, o, g * 512:(g + 1) * 512], scores[:, o, :], ACT.Identity,
                               bias=bq_col[:, o:o + 1]).then_inc(pro_q_hi, 1)
            if g < GROUPS - 1:
                xt_hi_pro(g + 1)
            for n in range(4):
                act.wait_ge(pro_v_biased, 4 * g + n + 1)
                copy(vals_self[:, 4 * g + n, 0, :], v_tmp[:, n % 2, :]).then_inc(pro_v_hi, 1)
            u_hi(g)
            if g == 0:
                act.wait_ge(cross_w_loaded, 64)
                for dup in range(2):
                    copy(wk_dup[:, 0, :, :, dup, :], w2_raw[:, 0, :, :].rearrange("p c (h d) -> p c h d", h=H)).then_inc(
                        cross_w_hi, 1)
                for n, w in ((1, wv_cross), (2, wq_cross), (3, wo_cross)):
                    copy(w[:, 0, :, :], w2_raw[:, n, :, :]).then_inc(cross_w_hi, 1)
            act.wait_ge(ctx_loaded, 16 * (g + 1))
            act.wait_ge(v_scale_step, 1)
            copy(ctx_t[:, 0, :, g * KB:min((g + 1) * KB, M)], ctx_raw[:, :, 0:min(KB, M - g * KB)]).then_inc(ctx_hi, 1)

        for m in range(MC):
            rows = P if m < MC - 1 else MLAST
            act.wait_ge(cross_v_ready, m + 1)
            act.wait_ge(v_pool_step, 1)
            copy(v_f32[0:rows, m, :], flip[0:rows, m % 2, 0:D]).then_inc(cross_v_copied, 1)
        act.wait_ge(u_stored, 16 * GROUPS)
        act.wait_ge(u_lo_ready, C * GROUPS)
        act.wait_ge(pro_v_lo, 4 * GROUPS)
        for g in range(4):
            for h in range(H):
                act.wait_ge(cross_k_ready, H * g + h + 1)
                copy(keys_cross[:, 0, h, g * KB:(g + 1) * KB], scores[:, h, 0:KB]).then_inc(cross_k_hi, 1)
                if g >= 2:
                    for m in value_chunks(H * (g - 2) + h):
                        act.wait_ge(v_scale_step, 4)
                        act.activation(vals_cross[:, m, :, 0, :], v_f32[:, m, :].rearrange("p (h d) -> p h d", h=H), ACT.Copy,
                                       scale=v_scale[:, 0:1]).then_inc(cross_v_hi, 1)
        copy(barrier[:, 0:1], ident[:, 0:1]).then_inc(prologue_done, 1)
        act.wait_ge(prologue_done, 3)

        def weights_hi(n):
            e = n % E
            act.wait_ge(w_loaded[n % 2], 16 * (n // 2 + 1))
            if n < E:
                copy(w1s[:, 0, :, e * DF:(e + 1) * DF], w_stage[:, n % 2, :].rearrange("p (c n) -> p c n", c=C)).then_inc(
                    w_hi, 1)
            else:
                act.wait_ge(cross_p_used, 16 * T)
                copy(w2s[:, 0, :, e * D:(e + 1) * D], w_stage[:, n % 2, :].rearrange("p (c n) -> p c n", c=FC)).then_inc(
                    w_hi, 1)

        def cross_hi(j, k, h, g):
            use = ("x", h, g)
            t = j - stage_of(use)
            act.wait_ge(cross_flipped, 16 * t + 4 * h + g + 1)
            if h + g + k > 3 + 0:
                pass
            w = len(XG[g]) * P
            rows = P if g < NG - 1 else MLAST
            if not (k == 1 and h == 0):
                act.wait_ge(cross_p_used, 16 * t + 4 * h + g - 3)
            copy(ps_cross[0:rows, g, 0, 0:w], flip[0:rows, bank(use), 0:w]).then_inc(cross_p_hi, 1)

        def self_hi(j, k, g):
            act.wait_ge(self_flipped, 4 * j + g + 1)
            if k >= 1:
                act.wait_ge(self_p_used, 4 * j + g - 3)
            copy(ps_self[:, g, 0, :], flip[:, bank(("s", g)), :]).then_inc(self_p_hi, 1)

        def body(j, k):
            a, b, c = k < T, 1 <= k <= T, k >= 2
            if k == T + 1:
                act.activation(barrier[:, 1:2], ident[:, 0:1], ACT.Gelu).then_inc(gelu_table, 1)
            if c:
                cross_hi(j, k, 2, 2)
            if b:
                act.wait_ge(xn_flipped, j)
                copy(xt[:, 0, :, :], flip[:, bank(("xn",)), 0:D].rearrange("p (c s) -> p c s", c=C)).then_inc(xt_hi, 1)
            if c:
                cross_hi(j, k, 2, 3)
            if k == T:
                weights_hi(0)
            if b:
                act.wait_ge(q_ready, j)
                if k >= 2:
                    act.wait_ge(q_flipped, j - 1)
                copy(qs[:, :, 0, :], flip[:, bank(("xq",)), 0:D].rearrange("p (h d) -> p h d", h=H)).then_inc(qs_hi, 1)
            if c:
                cross_hi(j, k, 3, 0)
            if b:
                act.wait_ge(q_flipped, j)
                if k >= 2:
                    act.wait_ge(cross_scores_ready, 8 * (j - 1))
                act.activation(qt[:, :, :], flip[:, bank(("qs",)), :].rearrange("p (h s) -> p h s", h=H), ACT.Copy,
                               scale=HD ** -0.5).then_inc(qt_ready, 1)
            if a:
                self_exps(j, k, 0)
            if c:
                cross_hi(j, k, 3, 1)
                cross_hi(j, k, 3, 2)
            if a:
                self_exps(j, k, 1)
                self_hi(j, k, 0)
            if c:
                cross_hi(j, k, 3, 3)
            if k == T:
                weights_hi(1)
            if k == T + 1:
                weights_hi(4)
            if a:
                self_hi(j, k, 1)
                self_hi(j, k, 2)
            if b:
                cross_exp(j, k, 0, 0)
            if a:
                self_hi(j, k, 3)
            if c:
                act.wait_ge(o_flipped, j - 1)
                copy(ot[:, 0, :, :], flip[:, bank(("o",)), 0:D].rearrange("p (c s) -> p c s", c=C)).then_inc(ot_hi, 1)
            if k == T + 1:
                weights_hi(5)
            if b:
                cross_hi(j, k, 0, 0)
                cross_exp(j, k, 0, 1)
                cross_exp(j, k, 1, 0)
                cross_hi(j, k, 0, 1)
                cross_hi(j, k, 0, 2)
                cross_hi(j, k, 0, 3)
            if k == T:
                weights_hi(2)
            if b:
                cross_exp(j, k, 1, 1)
                cross_hi(j, k, 1, 0)
                cross_hi(j, k, 1, 1)
            if c:
                act.wait_ge(x3_flipped, j - 1)
                if k > 2:
                    act.wait_ge(gate_ready, j - 2)
                copy(x3t[:, :, :], flip[:, bank(("x3",)), 0:D].rearrange("p (c s) -> p c s", c=C)).then_inc(
                    x3t_ready, 1)
            if b:
                cross_hi(j, k, 1, 2)
                cross_exp(j, k, 2, 0)
                cross_hi(j, k, 1, 3)
            if k == T:
                weights_hi(3)
            if b:
                cross_hi(j, k, 2, 0)
                cross_exp(j, k, 2, 1)
                cross_hi(j, k, 2, 1)
                cross_exp(j, k, 3, 0)
                cross_exp(j, k, 3, 1)

        def self_exps(j, k, half):
            if half == 0:
                act.wait_ge(self_max, j + 1)
                if k >= 1:
                    act.wait_ge(self_p_used, 4 * j)
                    act.wait_ge(x1_ready, j)
            banks = slice(half * NB // 2, (half + 1) * NB // 2)
            act.activation(exp_self[:, half * N // 2:(half + 1) * N // 2].rearrange("p (n s) -> p n s", n=NB // 2),
                           scores[:, banks, :], ACT.Exp, bias=sneg[:, 0:1],
                           accum_out=sden[:, half:half + 1]).then_inc(self_exp, 1)

        def cross_exp(j, k, h, half):
            if half == 0:
                act.wait_ge(cross_max_ready, 4 * (j - 1) + h + 1)
                if h == 0 and k >= 2:
                    act.wait_ge(o_step, 3 * (j - 1))
            cols = slice(XHALF, MP) if half else slice(0, XHALF)
            act.activation(exp_cross[:, h % 2, cols], exp_cross[:, h % 2, cols], ACT.Exp, bias=xneg[:, h % 2, 1:2],
                           scale=-1.0, accum_out=xden[:, half, h:h + 1]).then_inc(cross_exp_ready, 1)

        run_pipeline(act, body)
        copy(barrier[:, 0:1], ident[:, 0:1]).then_inc(attention_done, 1)
        for n in (E + 2, E + 3):
            weights_hi(n)
        act.wait_ge(attention_done, 3)

        def blocks(b, k):
            def x_hi_f(b):
                act.wait_ge(f_x_flipped, b + 1)
                copy(xt_f[:, 0, :, :], self_out[:, 0:D].rearrange("p (c s) -> p c s", c=C)).then_inc(f_xt_hi, 1)

            def gelu(b, n):
                act.wait_ge(f_bias, 2 * b + n + 1)
                cols = slice(n * 512, (n + 1) * 512)
                act.activation(hidden[:, cols], hidden[:, cols], ACT.Gelu).then_inc(f_gelu, 1)

            if k == 0:
                x_hi_f(0)
            if k >= 1:
                for n in range(2):
                    act.wait_ge(f_h_flipped, 2 * (b - 1) + n + 1)
                    if k >= 2:
                        act.wait_ge(f_y, b - 1)
                    copy(ht[:, 0, 4 * n:4 * n + 4, :], flip[:, n, :].rearrange("p (c s) -> p c s", c=4)).then_inc(
                        f_ht_hi, 1)
            if k < BLOCKS:
                gelu(b, 0)
            if k < BLOCKS - 1:
                x_hi_f(b + 1)
            if k < BLOCKS:
                gelu(b, 1)
        run_blocks(act, blocks)

    @block.vector
    def _(dve):
        def low(out, full, hi):
            return dve.tensor_tensor(out, full, hi, ALU.subtract)

        def statistics_pro(g):
            tiles = range(4 * g, 4 * g + 4)
            dve.wait_ge(x_rows_loaded[g], 16)
            for t in tiles:
                dve.bn_stats(stats_pro[:, t, :], x_all[:, t, :]).then_inc(pro_stats, 1)
            dve.wait_ge(pro_stats, 8 * g + 4)
            for t in tiles:
                dve.bn_aggr(mv_pro[:, t, :], stats_pro[:, t, :]).then_inc(pro_stats, 1)
            dve.wait_ge(pro_stats, 8 * g + 8)
            dve.tensor_scalar(var_eps[:, 4 * g:4 * g + 4], mv_pro[:, 4 * g:4 * g + 4, 1], EPS, None, ALU.add).then_inc(
                pro_var_ready, 1)

        def scale_rows(g):
            cols = slice(4 * g, 4 * g + 4)
            dve.wait_ge(pro_powers, 2 * g + 2)
            dve.scalar_tensor_tensor(out=norms[:, cols], in0=rstd_pro[:, cols], scalar=float(D) ** 0.5, in1=std_pro[:, cols],
                                     op0=ALU.mult, op1=ALU.mult).then_inc(norm_step, 1)
            dve.wait_ge(norm_step, 4 * g + 1)
            dve.tensor_scalar(norm_eps[:, cols], norms[:, cols], 1e-9, None, ALU.add).then_inc(norm_step, 1)
            dve.wait_ge(norm_step, 4 * g + 2)
            dve.reciprocal(norm_inv[:, cols], norm_eps[:, cols]).then_inc(norm_step, 1)
            dve.wait_ge(norm_step, 4 * g + 3)
            dve.tensor_tensor(row_scale[:, cols], norm_inv[:, cols], rstd_pro[:, cols], ALU.mult).then_inc(norm_step, 1)
            dve.wait_ge(norm_step, 4 * g + 4)
            for t in range(4 * g, 4 * g + 4):
                dve.tensor_scalar(x_all[:, t, :], x_all[:, t, :], mv_pro[:, t, 0:1], row_scale[:, t:t + 1],
                                  ALU.subtract, ALU.mult).then_inc(rows_scaled, 1)

        def xt_lo_pro(g):
            for c in range(C):
                dve.wait_ge(pro_xt_hi, C * g + c + 1)
                low(xt_pro[:, g % 2, 1, c, :], flip[:, c, :], xt_pro[:, g % 2, 0, c, :].bitcast(F32)).then_inc(
                    pro_xt_lo, 1)

        def u_lo(g):
            for o in range(C):
                dve.wait_ge(u_hi_ready, C * g + o + 1)
                out = self_out if o == 0 else cross_out
                dve.scalar_tensor_tensor(out=u_out[:, :, C + o, :], in0=out[:, :].rearrange("p (t s) -> p t s", t=4),
                                         scalar=1.0 / 16.0, in1=u_out[:, :, o, :].bitcast(F32), op0=ALU.mult,
                                         op1=ALU.subtract).then_inc(u_lo_ready, 1)

        dve.memset(ctx_t[:, :, :, M:MP].bitcast(F32), 0.0).then_inc(v_scale_step, 1)
        statistics_pro(0)
        for n in range(3):
            if n == 1:
                scale_rows(0)
            dve.wait_ge(self_w_hi, n + 1)
            low(w_self[:, n, 1, :, :], w_raw[:, n, :, :], w_self[:, n, 0, :, :].bitcast(F32)).then_inc(self_w_lo, 1)
            if n == 1:
                xt_lo_pro(0)
                statistics_pro(1)
        scale_rows(1)
        dve.wait_ge(biases_loaded, 64)
        for g in range(GROUPS):
            for o in range(C):
                dve.wait_ge(pro_q_hi, C * g + o + 1)
                cols = slice(g * 512, (g + 1) * 512)
                dve.scalar_tensor_tensor(out=keys_self[:, 1, o, cols], in0=scores[:, o, :], scalar=bq_col[:, o:o + 1],
                                         in1=keys_self[:, 0, o, cols].bitcast(F32), op0=ALU.add,
                                         op1=ALU.subtract).then_inc(pro_q_lo, 1)
            if g < GROUPS - 1:
                xt_lo_pro(g + 1)
            if g < GROUPS - 2:
                statistics_pro(g + 2)
            for n in range(4):
                dve.wait_ge(pro_v_ready, 4 * g + n - n % 2 + 2)
                if 4 * g + n >= 2:
                    dve.wait_ge(pro_v_hi, 4 * g + n - 1)
                    dve.wait_ge(pro_v_lo, 4 * g + n - 1)
                dve.tensor_tensor(v_tmp[:, n % 2, :], scores[:, 2 + n // 2, (n % 2) * D:(n % 2 + 1) * D], bv_row[:, :],
                                  ALU.add).then_inc(pro_v_biased, 1)
                if n % 2:
                    for m in (n - 1, n):
                        dve.wait_ge(pro_v_hi, 4 * g + m + 1)
                        dve.wait_ge(pro_v_biased, 4 * g + m + 1)
                        low(vals_self[:, 4 * g + m, 1, :], v_tmp[:, m % 2, :],
                            vals_self[:, 4 * g + m, 0, :].bitcast(F32)).then_inc(pro_v_lo, 1)
            if g < GROUPS - 2:
                scale_rows(g + 2)
            u_lo(g)
            if g == 0:
                for dup in range(2):
                    dve.wait_ge(cross_w_hi, dup + 1)
                    for c in range(C):
                        op = low(wk_dup[:, 1, c, :, dup, :], w2_raw[:, 0, c, :].rearrange("p (h d) -> p h d", h=H),
                                 wk_dup[:, 0, c, :, dup, :].bitcast(F32))
                    if dup:
                        op.then_inc(cross_w_lo, 1)
            if g == 1:
                for n, w in ((1, wv_cross), (2, wq_cross), (3, wo_cross)):
                    dve.wait_ge(cross_w_hi, 2 + n)
                    low(w[:, 1, :, :], w2_raw[:, n, :, :], w[:, 0, :, :].bitcast(F32)).then_inc(cross_w_lo, 1)
            dve.wait_ge(ctx_hi, g + 1)
            cols = slice(g * KB, min((g + 1) * KB, M))
            low(ctx_t[:, 1, :, cols], ctx_raw[:, :, 0:min(KB, M - g * KB)], ctx_t[:, 0, :, cols].bitcast(F32)).then_inc(
                ctx_lo, 1)

        dve.wait_ge(u_stored, 16 * GROUPS)
        for g in range(4):
            for h in range(H):
                if g == 0:
                    dve.wait_ge(cross_v_copied, MC)
                    dve.tensor_reduce(v_max[:, 0, h:h + 1], v_f32[:, MC * h // H:MC * (h + 1) // H, :], AX.XY, ALU.max,
                                      apply_absolute_value=True).then_inc(v_max_part, 1)
                dve.wait_ge(cross_k_hi, H * g + h + 1)
                cols = slice(g * KB, (g + 1) * KB)
                low(keys_cross[:, 1, h, cols], scores[:, h, 0:KB], keys_cross[:, 0, h, cols].bitcast(F32)).then_inc(
                    cross_k_lo, 1)
                if g == 1 and h == H - 1:
                    dve.wait_ge(v_pool_step, 2)
                    dve.tensor_reduce(v_top[:, 0:1], v_max[:, 1, :], AX.X, ALU.max).then_inc(v_top_ready, 1)
                    dve.wait_ge(v_top_ready, 1)
                    dve.tensor_scalar(v_top[:, 1:2], v_top[:, 0:1], 1e-30, 1.0 / V_TOP, ALU.max, ALU.mult).then_inc(
                        v_scale_step, 1)
                    dve.wait_ge(v_scale_step, 2)
                    dve.tensor_copy(v_scale[:, 1:2], v_top[:, 1:2]).then_inc(v_scale_step, 1)
                    dve.reciprocal(v_scale[:, 0:1], v_top[:, 1:2]).then_inc(v_scale_step, 1)
                if g >= 2:
                    for m in value_chunks(H * (g - 2) + h):
                        dve.wait_ge(cross_v_hi, m + 1)
                        dve.wait_ge(v_scale_step, 4)
                        dve.scalar_tensor_tensor(out=vals_cross[:, m, :, 1, :], in0=v_f32[:, m, :].rearrange("p (h d) -> p h d", h=H),
                                                 scalar=v_scale[:, 0:1], in1=vals_cross[:, m, :, 0, :], op0=ALU.mult,
                                                 op1=ALU.subtract).then_inc(cross_v_lo, 1)
        dve.wait_ge(cross_v_lo, MC)
        dve.wait_ge(cross_k_lo, 4 * H)
        dve.tensor_copy(barrier[:, 1:2], ident[:, 0:1]).then_inc(prologue_done, 2)
        dve.wait_ge(prologue_done, 3)

        def weights_lo(n, part=None):
            e = n % E
            dve.wait_ge(w_hi, n + 1)
            if n < E:
                w, cols, ch = w1s, slice(e * DF, (e + 1) * DF), C
            else:
                w, cols, ch = w2s, slice(e * D, (e + 1) * D), FC
            at = slice(0, ch) if part is None else slice(part * ch // 2, (part + 1) * ch // 2)
            op = low(w[:, 1, at, cols], w_stage[:, n % 2, :].rearrange("p (c n) -> p c n", c=ch)[:, at, :],
                     w[:, 0, at, cols].bitcast(F32))
            if part != 0:
                op.then_inc(w_lo, 1)

        def cross_lo(j, k, h, g):
            use = ("x", h, g)
            t = j - stage_of(use)
            w = len(XG[g]) * P
            rows = P if g < NG - 1 else MLAST
            dve.wait_ge(cross_p_hi, 16 * t + 4 * h + g + 1)
            low(ps_cross[0:rows, g, 1, 0:w], flip[0:rows, bank(use), 0:w], ps_cross[0:rows, g, 0, 0:w]).then_inc(
                cross_p_lo, 1)

        def self_lo(j, k, g):
            dve.wait_ge(self_p_hi, 4 * j + g + 1)
            low(ps_self[:, g, 1, :], flip[:, bank(("s", g)), :], ps_self[:, g, 0, :].bitcast(F32)).then_inc(
                self_p_lo, 1)

        def part_max(j, k, n):
            dve.wait_ge(scores_ready, 4 * j + n + 1)
            dve.tensor_reduce(smax[:, n:n + 1], scores[:, n, :], AX.X, ALU.max).then_inc(max_part, 1)

        def cross_max(j, k, h, half):
            dve.wait_ge(cross_scores_ready, 8 * (j - 1) + 2 * h + half + 1)
            if half == 0:
                if h == 0:
                    dve.wait_ge(bias_ready, j)
                if h >= 2 or k >= 2:
                    dve.wait_ge(cross_flipped, 16 * (j - 1) + 4 * (h - 1))
            else:
                dve.wait_ge(cross_max_half, 4 * (j - 1) + h + 1)
            cols = slice(2 * half * KB, 2 * (half + 1) * KB)
            dve.tensor_tensor_reduce(exp_cross[:, h % 2, cols].rearrange("p (n s) -> p n s", n=2),
                                     scores[:, 2 * half:2 * half + 2, 0:KB],
                                     mask_bias[:, cols].rearrange("p (n s) -> p n s", n=2), -1.0,
                                     xneg[:, h % 2, 0:1] if half else MAX_CAP, ALU.add, ALU.min,
                                     xneg[:, h % 2, half:half + 1]).wait_op(
                                         constants_set, CONSTANTS, "sem-ge").then_inc(cross_max_ready if half else cross_max_half, 1)

        def body(j, k):
            a, b, c = k < T, 1 <= k <= T, k >= 2
            if k == T + 1:
                pad_rows()
            if a:
                part_max(j, k, 0)
            if c:
                cross_lo(j, k, 2, 2)
            if b:
                dve.wait_ge(xt_hi, j)
                low(xt[:, 1, :, :], flip[:, bank(("xn",)), 0:D].rearrange("p (c s) -> p c s", c=C),
                    xt[:, 0, :, :].bitcast(F32)).then_inc(xt_lo, 1)
            if a:
                part_max(j, k, 1)
                part_max(j, k, 2)
            if c:
                cross_lo(j, k, 2, 3)
            if k == T:
                weights_lo(0)
            if b:
                dve.wait_ge(qs_hi, j)
                low(qs[:, :, 1, :], flip[:, bank(("xq",)), 0:D].rearrange("p (h d) -> p h d", h=H),
                    qs[:, :, 0, :].bitcast(F32)).then_inc(qs_lo, 1)
            if a:
                part_max(j, k, 3)
                dve.wait_ge(max_part, 4 * j + 4)
                dve.tensor_reduce(sneg[:, 0:1], smax[:, :], AX.X, ALU.max, negate=True).then_inc(self_max, 1)
            if c:
                dve.wait_ge(cross_exp_ready, 8 * (j - 1))
                dve.tensor_tensor(xcoef[:, 2, :], xden[:, 0, :], xden[:, 1, :], ALU.add).then_inc(o_step, 1)
                dve.wait_ge(o_step, 3 * (j - 1) - 2)
                dve.reciprocal(xcoef[:, 0, :], xcoef[:, 2, :]).then_inc(o_step, 1)
                dve.wait_ge(o_step, 3 * (j - 1) - 1)
                dve.tensor_scalar(xcoef[:, 1, :], xcoef[:, 0, :], v_scale[:, 1:2], None, ALU.mult).then_inc(o_step, 1)
                cross_lo(j, k, 3, 0)
                cross_lo(j, k, 3, 1)
                cross_lo(j, k, 3, 2)
            if b:
                cross_max(j, k, 0, 0)
            if a:
                self_lo(j, k, 0)
            if c:
                cross_lo(j, k, 3, 3)
            if k == T:
                weights_lo(1)
            if a:
                self_lo(j, k, 1)
            if b:
                cross_max(j, k, 0, 1)
            if a:
                self_lo(j, k, 2)
            if c:
                dve.wait_ge(cross_p_used, 16 * (j - 1))
                dve.tensor_reduce(o_tile[:, :, :], cross_out[:, :].rearrange("p (h two d) -> p h d two", h=H, two=2),
                                  AX.X, ALU.add).then_inc(o_summed, 1)
                dve.wait_ge(o_step, 3 * (j - 1))
                dve.wait_ge(o_summed, j - 1)
                dve.tensor_tensor(o_tile[:, :, :], o_tile[:, :, :],
                                  xcoef[:, 1, :].unsqueeze(2).broadcast_to([P, H, HD]), ALU.mult).then_inc(o_ready, 1)
            if b:
                cross_max(j, k, 1, 0)
            if a:
                self_lo(j, k, 3)
            if c:
                dve.wait_ge(ot_hi, j - 1)
                low(ot[:, 1, :, :], flip[:, bank(("o",)), 0:D].rearrange("p (c s) -> p c s", c=C),
                    ot[:, 0, :, :].bitcast(F32)).then_inc(ot_lo, 1)
            if k == T + 1:
                weights_lo(4, 0)
            if a:
                dve.wait_ge(self_exp, 2 * j + 2)
                dve.tensor_tensor(ssum[:, :], sden[:, 0:1], sden[:, 1:2], ALU.add).then_inc(sum_ready, 1)
                dve.wait_ge(sum_ready, j + 1)
                dve.reciprocal(scoef[:, 0:1], ssum[:, :]).then_inc(coef_step, 1)
                dve.wait_ge(coef_step, 2 * j + 1)
                dve.wait_ge(norm_ready, j + 1)
                dve.tensor_tensor(scoef[:, 1:2], scoef[:, 0:1], norm_col[:, :], ALU.mult).then_inc(coef_step, 1)
            if b:
                cross_max(j, k, 1, 1)
            if c:
                dve.wait_ge(wo_ready, j - 1)
                dve.wait_ge(record_filled, j - 1)
                dve.tensor_tensor(record[:, 0:D], flip[:, bank(("wo",)), 0:D], record[:, 0:D], ALU.add).then_inc(
                    x2_ready, 1)
                dve.wait_ge(x2_ready, j - 1)
                dve.bn_stats(bs3[:, :], record[:, 0:D]).then_inc(stats3, 1)
                dve.wait_ge(stats3, 2 * (j - 1) - 1)
                dve.bn_aggr(mv3[:, :], bs3[:, :]).wait_op(constants_set, CONSTANTS, "sem-ge").then_inc(mean3, 1)
                dve.wait_ge(mean3, j - 1)
                dve.tensor_scalar(rs3[:, 0:1], mv3[:, 1:2], EPS, None, ALU.add).then_inc(stats3, 1)
            if k == T + 1:
                weights_lo(4, 1)
            if b:
                cross_lo(j, k, 0, 0)
            if a:
                dve.wait_ge(coef_step, 2 * j + 2)
                dve.wait_ge(self_p_used, 4 * j + 4)
                dve.wait_ge(x_loaded, 16 * (j + 1))
                if k >= 1:
                    dve.wait_ge(x1_copied, j)
                dve.scalar_tensor_tensor(out=x1[:, :], in0=self_out[:, 0:D], scalar=scoef[:, 1:2], in1=x_tile[:, :],
                                         op0=ALU.mult, op1=ALU.add).then_inc(x1_ready, 1)
            if c:
                dve.wait_ge(rstd3, j - 1)
                dve.tensor_scalar(xn3[:, :], record[:, 0:D], mv3[:, 0:1], rs3[:, 1:2], ALU.subtract,
                                  ALU.mult).then_inc(xn3_ready, 1)
            if k == T + 1:
                weights_lo(5, 0)
                weights_lo(5, 1)
            if a:
                dve.wait_ge(x1_ready, j + 1)
                dve.bn_stats(bs1[:, :], x1[:, :]).then_inc(stats1, 1)
            if b:
                cross_lo(j, k, 0, 1)
                cross_lo(j, k, 0, 2)
                cross_lo(j, k, 0, 3)
            if k == T:
                weights_lo(2)
            if b:
                cross_max(j, k, 2, 0)
                cross_lo(j, k, 1, 0)
                cross_max(j, k, 2, 1)
                cross_lo(j, k, 1, 1)
            if c:
                gates(j, k, 0)
            if b:
                cross_lo(j, k, 1, 2)
            if c:
                gates(j, k, 1)
            if b:
                cross_max(j, k, 3, 0)
                cross_lo(j, k, 1, 3)
            if k == T:
                weights_lo(3)
            if c:
                gates(j, k, 2)
            if b:
                cross_max(j, k, 3, 1)
            if c:
                ranks(j, k)
            if a:
                dve.wait_ge(stats1, 2 * j + 1)
                dve.bn_aggr(mv1[:, :], bs1[:, :]).wait_op(constants_set, CONSTANTS, "sem-ge").then_inc(mean1, 1)
            if b:
                cross_lo(j, k, 2, 0)
            if a:
                dve.wait_ge(mean1, j + 1)
                dve.tensor_scalar(rs1[:, 0:1], mv1[:, 1:2], EPS, None, ALU.add).then_inc(stats1, 1)
            if b:
                cross_lo(j, k, 2, 1)
            if a:
                dve.wait_ge(rstd1, j + 1)
                dve.tensor_scalar(xn[:, :], x1[:, :], mv1[:, 0:1], rs1[:, 1:2], ALU.subtract, ALU.mult).then_inc(
                    xn_ready, 1)
            if c:
                destination(j, k)

        def pad_rows():
            dve.wait_ge(rank_used, T - 1)
            for n in range(2):
                dve.tensor_scalar(pad_f[:, n, :], seen[:, :], lane[:, 0:1], float(n * P), ALU.add, ALU.add).then_inc(
                    pad_dest, 1)
            dve.wait_ge(pad_dest, 2)
            dve.tensor_copy(pad_i[:, :, :], pad_f[:, :, :]).then_inc(pad_dest_i, 1)

        def gates(j, k, part):
            def after(n):
                dve.wait_ge(gate_step, 6 * (j - 2) + n)

            if part == 0:
                dve.wait_ge(gate_ready, j - 1)
                dve.tensor_tensor(logits[:, :], flip[:, bank(("gate",)), 0:E], bg_row[:, :], ALU.add).then_inc(
                    logits_ready, 1)
                dve.wait_ge(logits_ready, j - 1)
                dve.tensor_reduce(gsc[:, 0, 0:1], logits[:, :], AX.X, ALU.max).then_inc(gate_step, 1)
            elif part == 1:
                after(1)
                dve.scalar_tensor_tensor(out=gsc[:, 1, :], in0=logits[:, :], scalar=gsc[:, 0, 0:1], in1=expert_w[:, :],
                                         op0=ALU.is_equal, op1=ALU.mult).then_inc(gate_step, 1)
                after(2)
                dve.tensor_reduce(gsc[:, 2, 0:1], gsc[:, 1, :], AX.X, ALU.max).then_inc(gate_step, 1)
            else:
                after(3)
                dve.tensor_scalar(gsc[:, 3, 0:1], gsc[:, 2, 0:1], 0.0, float(E), ALU.is_equal, ALU.mult).then_inc(
                    gate_step, 1)
                after(4)
                dve.tensor_tensor(gsc[:, 4, 0:1], gsc[:, 3, 0:1], gsc[:, 2, 0:1], ALU.add).then_inc(gate_step, 1)
                after(5)
                dve.tensor_scalar(onehot[:, :], expert_w[:, :], gsc[:, 4, 0:1], None, ALU.is_equal).then_inc(
                    gate_step, 1)
                after(6)
                if k > 2:
                    dve.wait_ge(rank_ready, j - 2)
                dve.tensor_copy(onehot16[:, :], onehot[:, :]).then_inc(onehot_ready, 1)

        def ranks(j, k):
            dve.wait_ge(rank_ready, j - 1)
            dve.tensor_tensor(rank_e[:, :], flip[:, bank(("rank",)), 0:E], seen[:, :], ALU.add).then_inc(rank_added, 1)
            dve.wait_ge(rank_added, j - 1)
            dve.tensor_tensor(seen[:, :], flip[:, bank(("rank",)), E:2 * E], seen[:, :], ALU.add).then_inc(rank_used, 1)

        def destination(j, k):
            dve.tensor_tensor_reduce(gsc[:, 5, :], rank_e[:, :], onehot[:, :], 1.0, 0.0, ALU.mult, ALU.add,
                                     dest[:, 0:1]).then_inc(dest_step, 1)
            dve.wait_ge(dest_step, j - 1)
            if k > 2:
                dve.wait_ge(routed, 16 * (j - 2))
            dve.tensor_copy(dest_i[:, :], dest[:, :]).then_inc(dest_ready, 1)

        run_pipeline(dve, body)

        dve.tensor_copy(barrier[:, 2:3], ident[:, 0:1]).then_inc(attention_done, 2)
        steps = [0]

        def step(op):
            steps[0] += 1
            op.then_inc(table_step, 1)
            dve.wait_ge(table_step, steps[0])

        step(dve.tensor_tensor(count[:, :], seen[:, :], region_base[:, :], ALU.subtract))
        step(dve.tensor_tensor(over[:, :, :], count[:, :].unsqueeze(2).broadcast_to([P, E, T]), sixteenth[:, :].unsqueeze(1).broadcast_to([P, E, T]), ALU.is_gt))
        step(dve.tensor_reduce(need[:, :], over[:, :, :], AX.X, ALU.add))
        step(dve.tensor_copy(ends[:, 0:1], need[:, 0:1]))
        for e in range(1, E):
            step(dve.tensor_tensor(ends[:, e:e + 1], ends[:, e - 1:e], need[:, e:e + 1], ALU.add))
        step(dve.tensor_tensor(past[:, :, :], block_no[:, 0, :].unsqueeze(2).broadcast_to([P, BLOCKS, E]),
                               ends[:, :].unsqueeze(1).broadcast_to([P, BLOCKS, E]), ALU.is_ge))
        step(dve.tensor_reduce(tab[:, 0, :], past[:, :, :], AX.X, ALU.add))
        step(dve.tensor_tensor(past[:, :, :], past[:, :, :], need[:, :].unsqueeze(1).broadcast_to([P, BLOCKS, E]), ALU.mult))
        step(dve.tensor_reduce(tab[:, 1, :], past[:, :, :], AX.X, ALU.add))
        step(dve.scalar_tensor_tensor(out=tab[:, 2, :], in0=tab[:, 0, :], scalar=float(REGION), in1=block_no[:, 1, :],
                                      op0=ALU.mult, op1=ALU.add))
        step(dve.scalar_tensor_tensor(out=tab[:, 3, :], in0=tab[:, 1, :], scalar=-float(P), in1=tab[:, 2, :],
                                      op0=ALU.mult, op1=ALU.add))
        dve.tensor_copy(table[:, 0, :], tab[:, 3, :]).then_inc(table_ready, 1)
        step(dve.tensor_scalar(tab[:, 4, :], tab[:, 0, :], float(E - 1), float(DF), ALU.min, ALU.mult))
        dve.tensor_copy(table[:, 1, :], tab[:, 4, :]).then_inc(table_ready, 1)
        dve.wait_ge(table_ready, 2)
        step(dve.tensor_scalar(tab[:, 4, :], tab[:, 0, :], float(E - 1), float(D), ALU.min, ALU.mult))
        dve.tensor_copy(table[:, 2, :], tab[:, 4, :]).then_inc(table_ready, 1)
        dve.wait_ge(table_ready, 3)

        dve.wait_ge(attention_done, 3)
        dve.wait_ge(b_loaded, 32)

        def statistics(b, k):
            dve.wait_ge(rows_loaded, 16 * (b + 1))
            if k >= 1:
                dve.wait_ge(f_mean, b)
            dve.bn_stats(bs_f[:, :], rows[:, k % RING, 0:D]).then_inc(f_stats, 1)
            dve.wait_ge(f_stats, b + 1)
            if k >= 1:
                dve.wait_ge(f_xn, b)
            dve.bn_aggr(mv_f[:, :], bs_f[:, :]).wait_op(constants_set, CONSTANTS, "sem-ge").then_inc(f_mean, 1)
            dve.wait_ge(f_mean, b + 1)
            if k >= 1:
                dve.wait_ge(f_rstd, b)
            dve.tensor_scalar(rs_f[:, 0:1], mv_f[:, 1:2], EPS, None, ALU.add).then_inc(f_eps, 1)

        def normalise(b, k):
            dve.wait_ge(f_rstd, b + 1)
            if k >= 1:
                dve.wait_ge(f_x_flipped, b)
            dve.tensor_scalar(xn_f[:, :], rows[:, k % RING, 0:D], mv_f[:, 0:1], rs_f[:, 1:2], ALU.subtract,
                              ALU.mult).then_inc(f_xn, 1)

        def blocks(b, k):
            def x_lo_f(b):
                dve.wait_ge(f_xt_hi, b + 1)
                low(xt_f[:, 1, :, :], self_out[:, 0:D].rearrange("p (c s) -> p c s", c=C),
                    xt_f[:, 0, :, :].bitcast(F32)).then_inc(f_xt_lo, 1)

            if k == 0:
                statistics(0, 0)
                normalise(0, 0)
                x_lo_f(0)
                for n in range(E + 2, 2 * E):
                    weights_lo(n)
                statistics(b + 1, 1)
                normalise(b + 1, 1)
            if k >= 1:
                for n in range(2):
                    dve.wait_ge(f_ht_hi, 2 * (b - 1) + n + 1)
                    low(ht[:, 1, 4 * n:4 * n + 4, :], flip[:, n, :].rearrange("p (c s) -> p c s", c=4),
                        ht[:, 0, 4 * n:4 * n + 4, :].bitcast(F32)).then_inc(f_ht_lo, 1)
            if k < BLOCKS:
                off = dve.value_load(table[0:1, 1, bass.ds(b, 1)], min_val=0, max_val=(E - 1) * DF)
                for n in range(2):
                    if k >= 1:
                        dve.wait_ge(f_h_flipped, 2 * (b - 1) + n + 1)
                    dve.wait_ge(f_h, 2 * b + n + 1)
                    dve.tensor_tensor(hidden[:, n * 512:(n + 1) * 512], scores[:, n, :],
                                      b1_row[:, bass.ds(off + n * 512, 512)], ALU.add).then_inc(f_bias, 1)
            if k < BLOCKS - 2:
                statistics(b + 2, k + 2)
            if k < BLOCKS - 1:
                x_lo_f(b + 1)
            if k < BLOCKS - 2:
                normalise(b + 2, k + 2)
            if k >= 1:
                off2 = dve.value_load(table[0:1, 2, bass.ds(b - 1, 1)], min_val=0, max_val=(E - 1) * D)
                if k >= 2:
                    dve.wait_ge(f_out, b - 1)
                dve.tensor_tensor(base_f[:, :], rows[:, (k - 1) % RING, 0:D], b2_row[:, bass.ds(off2, D)],
                                  ALU.add).then_inc(f_base, 1)
                dve.wait_ge(f_base, b)
                dve.wait_ge(f_y, b)
                if k >= 2:
                    dve.wait_ge(f_stored, 16 * (b - 1))
                dve.tensor_tensor(out_f[:, (k - 1) % 2, :], cross_out[:, 0:D], base_f[:, :], ALU.add).then_inc(f_out, 1)
        run_blocks(dve, blocks)


def kernel(**inputs):
    import numpy as _np
    import concourse.bacc as _bacc
    from concourse import mybir as _mybir
    from concourse.bass_utils import run_bass_kernel_spmd as _run

    def array(name):
        return _np.asarray(inputs[name])

    laid_out = {
        "x": array("x")[0],
        "ctxT": array("ctx_1024")[0].T,
        "mask": array("mask_BxSxS2_bf1")[0].view(_np.uint8),
        "WqT": array("L0_attn_Wq").T,
        "AT": array("L0_attn_anomaly_matrix").T,
        "WvT": array("L0_attn_Wv").T,
        "bq": array("L0_attn_bq"),
        "bv": array("L0_attn_bv"),
        "xWq": array("L0_xattn_Wq"),
        "Wkv": array("L0_xattn_Wkv"),
        "Wo": array("L0_xattn_Wo"),
        "Wg": array("L0_ffn_Wg"),
        "bg": array("L0_ffn_bg"),
        "W1": array("L0_ffn_W1"),
        "b1": array("L0_ffn_b1"),
        "W2": array("L0_ffn_W2"),
        "b2": array("L0_ffn_b2"),
    }
    nc = _bacc.Bacc("TRN2", target_bir_lowering=False, num_devices=1)
    arrays, io = {}, {}
    for name, a in laid_out.items():
        arrays[name] = _np.ascontiguousarray(a)
        io[name] = nc.dram_tensor(name, arrays[name].shape, _mybir.dt.from_np(arrays[name].dtype), kind="ExternalInput").ap()
    io["out"] = nc.dram_tensor("out", (N, D), F32, kind="ExternalOutput").ap()
    build(nc, io)
    r = _run(nc, [arrays], core_ids=[0])
    return r.results[0]["out"].reshape(1, N, D)
```
